# Optimizing a Trainium2 kernel written in Bass

```python
import numpy as np
import jax
import jax.numpy as jnp

def _softmax(x, axis=-1):
    return jax.nn.softmax(x, axis=axis)

def _gelu(x):
    return jax.nn.gelu(x, approximate=True)

def _silu(x):
    return jax.nn.silu(x)

def _sigmoid(x):
    return jax.nn.sigmoid(x)

def _layernorm(x, axis=-1, eps=1e-05):
    m = jnp.mean(x, axis=axis, keepdims=True)
    v = jnp.var(x, axis=axis, keepdims=True)
    return (x - m) / jnp.sqrt(v + eps)

def _scatter_add(tgt, idx, src, axis=0):
    return tgt.at[idx].add(src)

def _segment_sum(src, seg, n):
    return jax.ops.segment_sum(src, seg, n)
kernel_name = 'mk_gps_d1_gnn_r8_37f712'

def setup_inputs(seed: int=0):
    np.random.seed(seed)
    _w = jnp.asarray

    def _rec_inputs():
        import jax
        import jax.numpy as jnp
        _gk = jax.random.key(seed)
        x = -0.0003713 + 1 * jax.random.normal(jax.random.fold_in(_gk, 1), (6250, 256), jnp.float32)
        _s = jax.random.randint(jax.random.fold_in(_gk, 2), (50000,), 0, 6250, jnp.int32)
        _d = jax.random.randint(jax.random.fold_in(_gk, 3), (50000,), 0, 6250, jnp.int32)
        _loop = jnp.arange(6250, dtype=jnp.int32)
        src = jnp.concatenate([_s, _d, _loop])
        dst = jnp.concatenate([_d, _s, _loop])
        _o = jnp.argsort(dst, stable=True)
        src = src[_o]
        dst = dst[_o]
        return (x, src, dst)
    x, src, dst = _rec_inputs()

    def _L0_gnn_setup():
        import jax, jax.numpy as jnp
        import numpy as np
        N = 6250
        E = 100000
        D_IN = 256
        D_H = 512
        D_OUT = 256
        key = jax.random.key(seed)
        ks = jax.random.split(key, 12)
        s = lambda d: 1.0 / np.sqrt(d)
        x = jax.random.normal(ks[0], (N, D_IN), dtype=jnp.float32)
        edge_index = jax.random.randint(ks[1], (2, E), 0, N, dtype=jnp.int64)
        W_rel = jax.random.uniform(ks[2], (D_IN, D_H), jnp.float32, -s(D_IN), s(D_IN))
        b_rel = jax.random.uniform(ks[3], (D_H,), jnp.float32, -s(D_IN), s(D_IN))
        W_root = jax.random.uniform(ks[4], (D_IN, D_H), jnp.float32, -s(D_IN), s(D_IN))
        W_ih = jax.random.uniform(ks[5], (4 * D_H, D_H), jnp.float32, -s(D_H), s(D_H))
        W_hh = jax.random.uniform(ks[6], (4 * D_H, D_H), jnp.float32, -s(D_H), s(D_H))
        b_ih = jax.random.uniform(ks[7], (4 * D_H,), jnp.float32, -s(D_H), s(D_H))
        b_hh = jax.random.uniform(ks[8], (4 * D_H,), jnp.float32, -s(D_H), s(D_H))
        W_fc = jax.random.uniform(ks[9], (D_H, D_OUT), jnp.float32, -s(D_H), s(D_H))
        b_fc = jax.random.uniform(ks[10], (D_OUT,), jnp.float32, -s(D_H), s(D_H))
        return {'x': x, 'edge_index': edge_index, 'W_rel': W_rel, 'b_rel': b_rel, 'W_root': W_root, 'W_ih': W_ih, 'W_hh': W_hh, 'b_ih': b_ih, 'b_hh': b_hh, 'W_fc': W_fc, 'b_fc': b_fc}
    _L0_gnn_all = _L0_gnn_setup()
    _L0_gnn_in = {k: v for k, v in _L0_gnn_all.items() if k in ('W_rel', 'b_rel', 'W_root', 'W_ih', 'W_hh', 'b_ih', 'b_hh', 'W_fc', 'b_fc')}
    del _L0_gnn_all

    def _L0_mix_setup():
        import jax, jax.numpy as jnp
        import numpy as np
        D_MODEL = 256
        NHEAD = 8
        D_HEAD = D_MODEL // NHEAD
        DIM_FF = 1024
        B, L = (4, 2048)
        LN_EPS = 1e-05

        def _layernorm(x, g, b):
            mu = jnp.mean(x, axis=-1, keepdims=True)
            var = jnp.mean((x - mu) ** 2, axis=-1, keepdims=True)
            return (x - mu) * jax.lax.rsqrt(var + LN_EPS) * g + b

        def _phi(x):
            return jnp.where(x > 0, x + 1.0, jnp.exp(x))
        key = jax.random.key(seed)
        ks = jax.random.split(key, 16)
        s_in = 1.0 / np.sqrt(D_MODEL)
        s_ff = 1.0 / np.sqrt(DIM_FF)
        inp = {'x': jax.random.normal(ks[0], (B, L, D_MODEL), dtype=jnp.float32), 'Wq': jax.random.normal(ks[1], (D_MODEL, D_MODEL), dtype=jnp.float32) * s_in, 'bq': jnp.zeros((D_MODEL,), jnp.float32), 'Wk': jax.random.normal(ks[2], (D_MODEL, D_MODEL), dtype=jnp.float32) * s_in, 'bk': jnp.zeros((D_MODEL,), jnp.float32), 'Wv': jax.random.normal(ks[3], (D_MODEL, D_MODEL), dtype=jnp.float32) * s_in, 'bv': jnp.zeros((D_MODEL,), jnp.float32), 'Wo': jax.random.normal(ks[4], (D_MODEL, D_MODEL), dtype=jnp.float32) * s_in, 'bo': jnp.zeros((D_MODEL,), jnp.float32), 'W1': jax.random.normal(ks[5], (D_MODEL, DIM_FF), dtype=jnp.float32) * s_in, 'b1': jnp.zeros((DIM_FF,), jnp.float32), 'W2': jax.random.normal(ks[6], (DIM_FF, D_MODEL), dtype=jnp.float32) * s_ff, 'b2': jnp.zeros((D_MODEL,), jnp.float32), 'ln1_g': jnp.ones((D_MODEL,), jnp.float32), 'ln1_b': jnp.zeros((D_MODEL,), jnp.float32), 'ln2_g': jnp.ones((D_MODEL,), jnp.float32), 'ln2_b': jnp.zeros((D_MODEL,), jnp.float32)}
        return inp
    _L0_mix_all = _L0_mix_setup()
    _L0_mix_in = {k: v for k, v in _L0_mix_all.items() if k in ('Wq', 'bq', 'Wk', 'bk', 'Wv', 'bv', 'Wo', 'bo', 'W1', 'b1', 'W2', 'b2', 'ln1_g', 'ln1_b', 'ln2_g', 'ln2_b')}
    del _L0_mix_all

    def _L0_ffn_setup():
        import math
        import jax, jax.numpy as jnp
        import numpy as np
        CAPACITY_FACTOR = 1.25
        TOP_K = 2
        LN_EPS = 1e-05

        def _layer_norm(x, gamma, beta):
            mu = jnp.mean(x, axis=-1, keepdims=True)
            var = jnp.var(x, axis=-1, keepdims=True)
            return (x - mu) * jax.lax.rsqrt(var + LN_EPS) * gamma + beta
        key = jax.random.key(seed)
        ks = jax.random.split(key, 4)
        B, S, D, F, E = (8, 512, 256, 512, 8)
        x = jax.random.normal(ks[0], (B, S, D), dtype=jnp.float32)
        Wr = jax.random.normal(ks[1], (D, E), dtype=jnp.float32) / np.sqrt(D)
        br = jnp.zeros((E,), jnp.float32)
        W1 = jax.random.normal(ks[2], (E, D, F), dtype=jnp.float32) / np.sqrt(D)
        b1 = jnp.zeros((E, F), jnp.float32)
        W2 = jax.random.normal(ks[3], (E, F, D), dtype=jnp.float32) / np.sqrt(F)
        b2 = jnp.zeros((E, D), jnp.float32)
        gamma = jnp.ones((D,), jnp.float32)
        beta = jnp.zeros((D,), jnp.float32)
        return {'x': x, 'Wr': Wr, 'br': br, 'W1': W1, 'b1': b1, 'W2': W2, 'b2': b2, 'gamma': gamma, 'beta': beta}
    _L0_ffn_all = _L0_ffn_setup()
    _L0_ffn_in = {k: v for k, v in _L0_ffn_all.items() if k in ('Wr', 'br', 'W1', 'b1', 'W2', 'b2', 'gamma', 'beta')}
    del _L0_ffn_all
    return {'x': x, 'src': src, 'dst': dst, 'L0_gnn_W_rel': _L0_gnn_in['W_rel'], 'L0_gnn_b_rel': _L0_gnn_in['b_rel'], 'L0_gnn_W_root': _L0_gnn_in['W_root'], 'L0_gnn_W_ih': _L0_gnn_in['W_ih'], 'L0_gnn_W_hh': _L0_gnn_in['W_hh'], 'L0_gnn_b_ih': _L0_gnn_in['b_ih'], 'L0_gnn_b_hh': _L0_gnn_in['b_hh'], 'L0_gnn_W_fc': _L0_gnn_in['W_fc'], 'L0_gnn_b_fc': _L0_gnn_in['b_fc'], 'L0_mix_Wq': _L0_mix_in['Wq'], 'L0_mix_bq': _L0_mix_in['bq'], 'L0_mix_Wk': _L0_mix_in['Wk'], 'L0_mix_bk': _L0_mix_in['bk'], 'L0_mix_Wv': _L0_mix_in['Wv'], 'L0_mix_bv': _L0_mix_in['bv'], 'L0_mix_Wo': _L0_mix_in['Wo'], 'L0_mix_bo': _L0_mix_in['bo'], 'L0_mix_W1': _L0_mix_in['W1'], 'L0_mix_b1': _L0_mix_in['b1'], 'L0_mix_W2': _L0_mix_in['W2'], 'L0_mix_b2': _L0_mix_in['b2'], 'L0_mix_ln1_g': _L0_mix_in['ln1_g'], 'L0_mix_ln1_b': _L0_mix_in['ln1_b'], 'L0_mix_ln2_g': _L0_mix_in['ln2_g'], 'L0_mix_ln2_b': _L0_mix_in['ln2_b'], 'L0_ffn_Wr': _L0_ffn_in['Wr'], 'L0_ffn_br': _L0_ffn_in['br'], 'L0_ffn_W1': _L0_ffn_in['W1'], 'L0_ffn_b1': _L0_ffn_in['b1'], 'L0_ffn_W2': _L0_ffn_in['W2'], 'L0_ffn_b2': _L0_ffn_in['b2'], 'L0_ffn_gamma': _L0_ffn_in['gamma'], 'L0_ffn_beta': _L0_ffn_in['beta']}

def reference(x, src, dst, L0_gnn_W_rel, L0_gnn_b_rel, L0_gnn_W_root, L0_gnn_W_ih, L0_gnn_W_hh, L0_gnn_b_ih, L0_gnn_b_hh, L0_gnn_W_fc, L0_gnn_b_fc, L0_mix_Wq, L0_mix_bq, L0_mix_Wk, L0_mix_bk, L0_mix_Wv, L0_mix_bv, L0_mix_Wo, L0_mix_bo, L0_mix_W1, L0_mix_b1, L0_mix_W2, L0_mix_b2, L0_mix_ln1_g, L0_mix_ln1_b, L0_mix_ln2_g, L0_mix_ln2_b, L0_ffn_Wr, L0_ffn_br, L0_ffn_W1, L0_ffn_b1, L0_ffn_W2, L0_ffn_b2, L0_ffn_gamma, L0_ffn_beta):
    import jax
    import jax.numpy as jnp

    def _L0_gnn_ref(x, edge_index, W_rel, b_rel, W_root, W_ih, W_hh, b_ih, b_hh, W_fc, b_fc):
        import jax, jax.numpy as jnp
        import numpy as np
        N = 6250
        E = 100000
        D_IN = 256
        D_H = 512
        D_OUT = 256
        src, dst = (edge_index[0], edge_index[1])
        agg = jax.ops.segment_sum(x[src], dst, num_segments=N)
        h = jax.nn.relu(agg @ W_rel + b_rel + x @ W_root)
        gates = h @ W_ih.T + b_ih + b_hh
        i, f, g, o = jnp.split(gates, 4, axis=-1)
        c = jax.nn.sigmoid(i) * jnp.tanh(g)
        h_lstm = jax.nn.sigmoid(o) * jnp.tanh(c)
        return h_lstm @ W_fc + b_fc

    def _L0_mix_ref(x, Wq, bq, Wk, bk, Wv, bv, Wo, bo, W1, b1, W2, b2, ln1_g, ln1_b, ln2_g, ln2_b):
        import jax, jax.numpy as jnp
        import numpy as np
        D_MODEL = 256
        NHEAD = 8
        D_HEAD = D_MODEL // NHEAD
        DIM_FF = 1024
        B, L = (4, 2048)
        LN_EPS = 1e-05

        def _layernorm(x, g, b):
            mu = jnp.mean(x, axis=-1, keepdims=True)
            var = jnp.mean((x - mu) ** 2, axis=-1, keepdims=True)
            return (x - mu) * jax.lax.rsqrt(var + LN_EPS) * g + b

        def _phi(x):
            return jnp.where(x > 0, x + 1.0, jnp.exp(x))
        Bq, Lq, _ = x.shape
        q = (x @ Wq + bq).reshape(Bq, Lq, NHEAD, D_HEAD)
        k = (x @ Wk + bk).reshape(Bq, Lq, NHEAD, D_HEAD)
        v = (x @ Wv + bv).reshape(Bq, Lq, NHEAD, D_HEAD)
        q_phi = _phi(q)
        k_phi = _phi(k)
        kv = jnp.einsum('blhd,blhe->bhde', k_phi, v)
        k_sum = k_phi.sum(axis=1)
        z = 1.0 / (jnp.einsum('blhd,bhd->blh', q_phi, k_sum) + 1e-06)
        out = jnp.einsum('blhd,bhde,blh->blhe', q_phi, kv, z)
        out = out.reshape(Bq, Lq, D_MODEL) @ Wo + bo
        x = _layernorm(x + out, ln1_g, ln1_b)
        ff = jax.nn.relu(x @ W1 + b1) @ W2 + b2
        x = _layernorm(x + ff, ln2_g, ln2_b)
        return x

    def _L0_ffn_ref(x, Wr, br, W1, b1, W2, b2, gamma, beta):
        import math
        import jax, jax.numpy as jnp
        import numpy as np
        CAPACITY_FACTOR = 1.25
        TOP_K = 2
        LN_EPS = 1e-05

        def _layer_norm(x, gamma, beta):
            mu = jnp.mean(x, axis=-1, keepdims=True)
            var = jnp.var(x, axis=-1, keepdims=True)
            return (x - mu) * jax.lax.rsqrt(var + LN_EPS) * gamma + beta
        B, S, D = x.shape
        E = Wr.shape[1]
        N = B * S
        K = TOP_K
        logits = jnp.mean(x, axis=1) @ Wr + br
        routing_weights = jax.nn.softmax(logits, axis=-1)
        capacity = float(math.ceil(N * CAPACITY_FACTOR / E))
        expected_loads = routing_weights.sum(axis=0) * (N / B)
        scale = jnp.where(expected_loads > capacity, capacity / expected_loads, 1.0)
        routing_weights = jax.nn.softmax(routing_weights * scale, axis=-1)
        rw_tok = jnp.broadcast_to(routing_weights[:, None, :], (B, S, E)).reshape(N, E)
        top_w, top_i = jax.lax.top_k(rw_tok, K)
        top_w = jax.nn.softmax(top_w, axis=-1)
        xf = x.reshape(N, D)
        h = jax.nn.gelu(jnp.einsum('nd,edf->enf', xf, W1) + b1[:, None, :], approximate=False)
        y = jnp.einsum('enf,efd->end', h, W2) + b2[:, None, :]
        w_dense = jnp.zeros((N, E), x.dtype).at[jnp.arange(N)[:, None], top_i].add(top_w)
        out = jnp.einsum('ne,end->nd', w_dense, y).reshape(B, S, D)
        out = _layer_norm(out + x, gamma, beta)
        return out
    edge_index = jnp.stack([src, dst])
    xn = _layernorm(x, axis=-1)
    x = x + _L0_gnn_ref(xn, edge_index, L0_gnn_W_rel, L0_gnn_b_rel, L0_gnn_W_root, L0_gnn_W_ih, L0_gnn_W_hh, L0_gnn_b_ih, L0_gnn_b_hh, L0_gnn_W_fc, L0_gnn_b_fc) + _L0_mix_ref(xn[None], L0_mix_Wq, L0_mix_bq, L0_mix_Wk, L0_mix_bk, L0_mix_Wv, L0_mix_bv, L0_mix_Wo, L0_mix_bo, L0_mix_W1, L0_mix_b1, L0_mix_W2, L0_mix_b2, L0_mix_ln1_g, L0_mix_ln1_b, L0_mix_ln2_g, L0_mix_ln2_b)[0]
    x = x + _L0_ffn_ref(_layernorm(x, axis=-1)[None], L0_ffn_Wr, L0_ffn_br, L0_ffn_W1, L0_ffn_b1, L0_ffn_W2, L0_ffn_b2, L0_ffn_gamma, L0_ffn_beta)[0]
    return x

_drawn_inputs = setup_inputs


def setup_inputs(seed=0):
    import zlib

    import numpy as np

    out = dict(_drawn_inputs(seed))
    spreads = {'L0_mix_bq': (0.0, 2.0),
     'L0_mix_bk': (0.0, 2.0),
     'L0_mix_bv': (0.0, 0.1),
     'L0_mix_bo': (0.0, 0.1),
     'L0_mix_b1': (0.0, 0.1),
     'L0_mix_b2': (0.0, 0.1),
     'L0_mix_ln1_g': (1.0, 0.2),
     'L0_mix_ln1_b': (0.0, 0.1),
     'L0_mix_ln2_g': (1.0, 0.2),
     'L0_mix_ln2_b': (0.0, 0.1),
     'L0_ffn_br': (0.0, 0.1),
     'L0_ffn_b1': (0.0, 0.514),
     'L0_ffn_b2': (0.0, 0.338),
     'L0_ffn_gamma': (1.0, 0.2),
     'L0_ffn_beta': (0.0, 0.1)}
    factors = {'L0_gnn_b_rel': 64.0,
     'L0_gnn_W_root': 4.083,
     'L0_gnn_b_ih': 40.037,
     'L0_gnn_b_hh': 39.121,
     'L0_gnn_b_fc': 4.116,
     'L0_mix_Wq': 8.0,
     'L0_mix_Wk': 8.0,
     'L0_mix_Wv': 7.703}
    for name, (base, spread) in spreads.items():
        noise = np.random.default_rng([zlib.crc32(name.encode()), seed]).standard_normal(out[name].shape)
        drawn = base * np.exp(spread * noise) if base else spread * noise
        out[name] = jnp.asarray(drawn.astype(out[name].dtype))
    for name, factor in factors.items():
        out[name] = (out[name] * factor).astype(out[name].dtype)
    return out
```

```python
from contextlib import ExitStack

import numpy as np

import concourse.bass as bass
from concourse import mybir

F32 = mybir.dt.float32
I32 = mybir.dt.int32
U32 = mybir.dt.uint32
ALU = mybir.AluOpType
ACT = mybir.ActivationFunctionType
AX = mybir.AxisListType
RMAX = bass.bass_isa.ReduceOp.max

P = 128
N = 6250
D = 256
K2 = D // P
DH = 512
FF = 1024
NE = 8
EDGES = 106250
SUB = 125
GS = 4
GN = GS * SUB
GROUPS = N // GN
TAIL = (N - GROUPS * GN) // SUB
NSUB = N // SUB
W = 64
CPS = 4
SGE = CPS * P
NSG = -(-EDGES // SGE)
NCH = NSG * CPS
SGI = NSG // (GROUPS + 1)
RING = 4
HALF = 8
OH = 4
NORM_U = 10
BIG = float(2 ** 14)
PAD_DST = 2 ** 20
EPS = 1e-5
PRE = 16

assert NSG == SGI * (GROUPS + 1) and SGI % RING == 0 and NSUB % NORM_U == 0 and N < BIG


class Chain:

    def __init__(self, eng, sem, base, per):
        self.eng, self.sem, self.base, self.per, self.k = eng, sem, base, per, 0

    def __call__(self, ins):
        self.k += 1
        ins.then_inc(self.sem, 1)
        self.eng.wait_ge(self.sem, self.base + self.k)

    def start(self, ins):
        self.k += 1
        ins.then_inc(self.sem, 1)

    def wait(self):
        self.eng.wait_ge(self.sem, self.base + self.k)

    def end(self):
        assert self.per in (None, self.k), self.k


def rsqrt_steps(nc, step, v, y, t):
    step(nc.vector.tensor_scalar(t.bitcast(I32), v.bitcast(I32), 1, None, ALU.logical_shift_right))
    step(nc.vector.tensor_scalar(y.bitcast(I32), t.bitcast(I32), -1.0, float(0x5F3759DF), ALU.mult, ALU.add))
    for _ in range(3):
        step(nc.vector.tensor_tensor(t, y, y, ALU.mult))
        step(nc.vector.tensor_tensor(t, t, v, ALU.mult))
        step(nc.vector.tensor_scalar(t, t, -0.5, 1.5, ALU.mult, ALU.add))
        step(nc.vector.tensor_tensor(y, y, t, ALU.mult))


RSQRT_STEPS = 14


def gps_layer(nc, io):
    with ExitStack() as whole:
        def sb(ctx, name, shape, dt=F32):
            return ctx.enter_context(nc.sbuf_tensor(name, shape, dt))

        def psum(ctx, name, shape):
            return ctx.enter_context(nc.psum_tensor(name, shape, F32))

        def sem(ctx, name):
            return ctx.enter_context(nc.semaphore(name))

        xn_dram, s1_dram, x2_dram = io["xn_dram"], io["s1_dram"], io["x2_dram"]

        xnT = sb(whole, "xnT", [P, K2, N])
        ident = sb(whole, "ident", [P, P])
        flag_i = sb(whole, "flag_i", [P, 1], I32)
        zsum = sb(whole, "zsum", [P, K2, NSUB // 2])
        z_mv = sb(whole, "z_mv", [SUB, NSUB, 2])
        gnnw = whole.enter_context(ExitStack())
        mixw = whole.enter_context(ExitStack())
        accT = sb(gnnw, "accT", [P, K2, N + W])
        src_t = sb(mixw, "src_t", [P, NCH], I32)
        dst_rel = sb(mixw, "dst_rel", [P, NCH])
        base_i = sb(mixw, "base_i", [P, NSG], I32)
        iota_w = sb(mixw, "iota_w", [P, W])
        qdiv = sb(mixw, "qdiv", [P, K2, P])
        kvwo = sb(mixw, "kvwo", [P, K2, D])
        wq = sb(mixw, "wq", [P, K2, D])
        w1 = sb(mixw, "w1", [P, K2, FF])
        w2 = sb(mixw, "w2", [P, FF // P, D])
        colb = sb(mixw, "colb", [P, 14])
        rows = sb(mixw, "rows", [P, 7, D])

        set_up(nc, io, sb, psum, sem, ident, src_t, dst_rel, base_i, flag_i, iota_w, accT,
               wq, w1, w2, colb, rows)
        norm_phase(nc, io, sb, psum, sem, xnT, ident, xn_dram, qdiv, kvwo)
        mix_phase(nc, io, sb, psum, sem, xnT, accT, ident, src_t, dst_rel, base_i, iota_w,
                  qdiv, kvwo, wq, w1, w2, colb, rows, xn_dram, s1_dram)
        rest_phase(nc, io, sb, psum, sem, accT, ident, src_t, iota_w, flag_i, xn_dram)
        mixw.close()
        gnn_phase(nc, io, sb, psum, sem, xnT, accT, ident, zsum, z_mv, s1_dram, x2_dram)
        gnnw.close()
        e1 = sb(whole, "e1", [P, 2, K2, DH])
        e2 = sb(whole, "e2", [P, 2 * DH // P, D])
        e1b = sb(whole, "e1b", [P, 2, DH // P])
        zb2 = sb(whole, "zb2", [P, D])
        route_phase(nc, io, sb, psum, sem, zsum, e1, e2, e1b, zb2)
        moe_phase(nc, io, sb, psum, sem, xnT, z_mv, e1, e2, e1b, zb2, x2_dram)


def set_up(nc, io, sb, psum, sem, ident, src_t, dst_rel, base_i, flag_i, iota_w, accT,
           wq, w1, w2, colb, rows):
    with ExitStack() as ctx:
        dst_t = sb(ctx, "dst_t", [P, NCH], I32)
        dst_rest = sb(ctx, "dst_rest", [P, NCH])
        rest_ready = sem(ctx, "rest_ready")
        rest_out = sem(ctx, "rest_out")
        dst_f = sb(ctx, "dst_f", [P, NCH])
        low = sb(ctx, "low", [P, NSG])
        nbase = sb(ctx, "nbase", [P, NSG])
        outside = sb(ctx, "outside", [P, NCH])
        anyout = sb(ctx, "anyout", [P, 1])
        anyall = sb(ctx, "anyall", [P, 1])
        edges_in = sem(ctx, "edges_in")
        weights_in = sem(ctx, "weights_in")
        cleared = sem(ctx, "cleared")
        made = sem(ctx, "made")
        low_ready = sem(ctx, "low_ready")
        base_ready = sem(ctx, "base_ready")
        step_done = sem(ctx, "setup_step")
        out_ready = sem(ctx, "out_ready")
        any_ready = sem(ctx, "any_ready")
        block = ctx.enter_context(nc.Block())

        @block.sync
        def _(sp):
            sp.dma_start(dst_t[:], io["dst"]).then_inc(edges_in, 16)
            sp.dma_start(src_t[:], io["src"]).then_inc(weights_in, 16)
            sp.dma_start(wq[:], io["mix_wq"]).then_inc(weights_in, 16)
            sp.dma_start(w1[:], io["mix_w1"]).then_inc(weights_in, 16)
            sp.dma_start(w2[:], io["mix_w2"]).then_inc(weights_in, 16)
            sp.dma_start(colb[:], io["mix_cols"]).then_inc(weights_in, 16)
            sp.dma_start(rows[:], io["mix_rows"]).then_inc(weights_in, 16)
            sp.wait_ge(weights_in, 96)
            sp.wait_ge(rest_ready, 1)
            sp.dma_start(io["rest_dram"], dst_rest[:]).then_inc(rest_out, 16)
            sp.wait_ge(rest_out, 16)

        @block.gpsimd
        def _(pool):
            pool.memset(ident[:], 0.0).then_inc(cleared, 1)
            pool.iota(iota_w[:], [[1, W]], base=0, channel_multiplier=0,
                      allow_small_or_imprecise_dtypes=True).then_inc(made, 1)
            pool.wait_ge(cleared, 1)
            pool.affine_select(out=ident[:], in_=ident[:], compare_op=ALU.not_equal, fill=1.0,
                               base=0, pattern=[[-1, P]], channel_multiplier=1).then_inc(made, 1)
            pool.wait_ge(low_ready, 1)
            pool.partition_all_reduce(nbase[:], low[:], P, RMAX).then_inc(base_ready, 1)
            pool.wait_ge(out_ready, 1)
            pool.partition_all_reduce(anyall[:], anyout[:], P, RMAX).then_inc(any_ready, 1)

        @block.vector
        def _(dve):
            step = Chain(dve, step_done, 0, None)
            nc.vector.memset(accT[:], 0.0).then_inc(made, 1)
            dve.wait_ge(edges_in, 16)
            step(nc.vector.tensor_copy(dst_f[:], dst_t[:]))
            step(nc.vector.tensor_reduce(low[:], dst_f[:].rearrange("p (s c) -> p s c", c=CPS), AX.X, ALU.min))
            nc.vector.tensor_scalar(low[:], low[:], -1.0, None, ALU.mult).then_inc(low_ready, 1)
            dve.wait_ge(base_ready, 1)
            step(nc.vector.tensor_scalar(base_i[:], nbase[:], -1.0, None, ALU.mult))
            step(nc.vector.tensor_tensor(dst_rel[:].rearrange("p (s c) -> p s c", c=CPS),
                                         dst_f[:].rearrange("p (s c) -> p s c", c=CPS),
                                         nbase[:].rearrange("p (s o) -> p s o", o=1).to_broadcast([P, NSG, CPS]), ALU.add))
            step(nc.vector.tensor_scalar(outside[:], dst_f[:], float(N), None, ALU.is_lt))
            step(nc.vector.scalar_tensor_tensor(out=outside[:], in0=dst_rel[:], scalar=float(W), in1=outside[:],
                                                op0=ALU.is_ge, op1=ALU.mult))
            nc.vector.tensor_reduce(anyout[:], outside[:], AX.X, ALU.max).then_inc(out_ready, 1)
            step(nc.vector.scalar_tensor_tensor(out=dst_rest[:], in0=dst_f[:], scalar=BIG, in1=outside[:],
                                                op0=ALU.add, op1=ALU.mult))
            nc.vector.tensor_scalar(dst_rest[:], dst_rest[:], -BIG, None, ALU.add).then_inc(rest_ready, 1)
            dve.wait_ge(any_ready, 1)
            step(nc.vector.tensor_copy(flag_i[:], anyall[:]))


def norm_phase(nc, io, sb, psum, sem, xnT, ident, xn_dram, qdiv, kvwo):
    U = NORM_U
    VE = P + 1
    with ExitStack() as ctx:
        wkv = sb(ctx, "wkv", [P, K2, 2 * D])
        wo = sb(ctx, "wo", [P, K2, D])
        bkv = sb(ctx, "bkv", [P, 2 * D])
        headm = sb(ctx, "headm", [P, P])
        xin = sb(ctx, "xin", [SUB, U, D])
        xnb = sb(ctx, "xnb", [SUB, U, D])
        st = sb(ctx, "st", [SUB, U, 6])
        mv = sb(ctx, "mv", [SUB, U, 2])
        var = sb(ctx, "var", [SUB, U])
        rstd = sb(ctx, "rstd", [SUB, U])
        tmp = sb(ctx, "tmp", [SUB, U])
        xT = sb(ctx, "xT", [P, 2, K2, SUB])
        kb = sb(ctx, "kb", [SUB, 2, D])
        vx = sb(ctx, "vx", [SUB, 2, K2, VE])
        ek = sb(ctx, "ek", [SUB, 2, D])
        rk = sb(ctx, "rk", [SUB, 2, D])
        kphi = sb(ctx, "kphi", [SUB, 2, D])
        zero = sb(ctx, "zero", [SUB, VE])
        kvm = sb(ctx, "kvm", [P, K2, P])
        kvmT = sb(ctx, "kvmT", [P, K2, P])
        ksum = sb(ctx, "ksum", [P, K2])
        psT = psum(ctx, "psT", [P, 2, K2 * 256])
        psKV = psum(ctx, "psKV", [P, 2, 2 * D])
        psA = psum(ctx, "psA", [P, K2, 512])
        w_in = sem(ctx, "norm_w_in")
        x_in = [sem(ctx, f"x_in{j}") for j in range(U)]
        xn_out = [sem(ctx, f"xn_out{j}") for j in range(U)]
        zeroed = sem(ctx, "zeroed")
        nstep = sem(ctx, "nstep")
        stats_taken = sem(ctx, "nstep_stats_taken")
        xn_ready = sem(ctx, "xn_ready")
        t_ready = sem(ctx, "t_ready")
        xT_ready = sem(ctx, "xT_ready")
        xT_saved = sem(ctx, "xT_saved")
        kv_ready = sem(ctx, "kv_ready")
        kb_ready = sem(ctx, "kb_ready")
        vx_ready = sem(ctx, "vx_ready")
        ek_ready = sem(ctx, "ek_ready")
        rk_ready = sem(ctx, "rk_ready")
        kphi_ready = sem(ctx, "kphi_ready")
        acc_done = sem(ctx, "acc_done")
        sums_done = sem(ctx, "sums_done")
        kvm_ready = sem(ctx, "kvm_ready")
        kvmT_ps = sem(ctx, "kvmT_ps")
        kvmT_sb = sem(ctx, "kvmT_sb")
        kvwo_ps = sem(ctx, "kvwo_ps")
        fin = sem(ctx, "norm_fin")
        block = ctx.enter_context(nc.Block())
        ITERS = NSUB // U

        @block.sync
        def _(sp):
            sp.dma_start(wkv[:], io["mix_wkv"]).then_inc(w_in, 16)
            sp.dma_start(bkv[:], io["mix_bkv"]).then_inc(w_in, 16)
            sp.dma_start(wo[:], io["mix_wo"]).then_inc(w_in, 16)
            sp.dma_start(headm[:], io["headm"]).then_inc(w_in, 16)
            with sp.Fori(0, ITERS) as i:
                for j in range(U):
                    sp.wait_ge(xn_ready, PRE + i * U - U + j + 1)
                    sp.dma_start(xin[:, j, :], io["x"][bass.ds(i * (U * SUB) + j * SUB, SUB), :]).then_inc(x_in[j], 16)

        @block.gpsimd
        def _(pool):
            def save(i, j):
                pool.wait_ge(xT_ready, PRE + i * U + j + 1)
                pool.tensor_copy(xnT[:, :, bass.ds(i * (U * SUB) + j * SUB, SUB)], xT[:, j % 2, :, :]).then_inc(xT_saved, 1)

            with pool.Fori(0, ITERS) as i:
                for j in range(U):
                    pool.wait_ge(xn_ready, PRE + i * U + j + 1)
                    pool.dma_start(xn_dram[bass.ds(i * (U * SUB) + j * SUB, SUB), :], xnb[:, j, :]).then_inc(xn_out[j], 16)
                    if j:
                        save(i, j - 1)
                save(i, U - 1)
            for j in range(U):
                pool.wait_ge(xn_out[j], 16 * ITERS)

        @block.vector
        def _(dve):
            dve.sem_inc(xn_ready, PRE)
            dve.sem_inc(kb_ready, PRE)
            dve.sem_inc(vx_ready, PRE)
            dve.sem_inc(kphi_ready, PRE)
            nc.vector.memset(zero[:], 0.0).then_inc(zeroed, 1)
            nc.vector.memset(vx[:], 1.0).then_inc(zeroed, 1)
            dve.wait_ge(zeroed, 2)
            dve.wait_ge(w_in, 64)
            with dve.Fori(0, ITERS) as i:
                step = Chain(dve, nstep, i * (2 * U + 1 + RSQRT_STEPS), 2 * U + 1 + RSQRT_STEPS)
                for j in range(U):
                    dve.wait_ge(x_in[j], i * 16 + 16)
                    step.start(nc.vector.bn_stats(st[:, j, :], xin[:, j, :]))
                step.wait()
                dve.sem_inc(stats_taken, 1)
                for j in range(U):
                    step.start(nc.vector.bn_aggr(mv[:, j, :], st[:, j, :]))
                step.wait()
                step(nc.vector.tensor_scalar(var[:], mv[:, :, 1], EPS, None, ALU.add))
                rsqrt_steps(nc, step, var[:], rstd[:], tmp[:])
                step.end()
                for j in range(U + 2):
                    if j < U:
                        dve.wait_ge(xn_out[j], i * 16)
                        dve.wait_ge(t_ready, PRE + i * U + j + 1 - U)
                        nc.vector.tensor_scalar(xnb[:, j, :], xin[:, j, :], mv[:, j, 0:1], rstd[:, j:j + 1],
                                                ALU.subtract, ALU.mult).then_inc(xn_ready, 1)
                    if 1 <= j <= U:
                        a = j - 1
                        dve.wait_ge(kv_ready, PRE + i * U + a + 1)
                        dve.wait_ge(ek_ready, PRE + i * U + a + 1 - 2)
                        dve.wait_ge(rk_ready, PRE + i * U + a + 1 - 2)
                        nc.vector.tensor_tensor(kb[:, a % 2, :], psKV[0:SUB, a % 2, 0:D], bkv[0:SUB, 0:D],
                                                ALU.add).then_inc(kb_ready, 1)
                        dve.wait_ge(acc_done, PRE + i * U + a + 1 - 2)
                        nc.vector.tensor_tensor(vx[:, a % 2, :, 0:P],
                                                psKV[0:SUB, a % 2, D:2 * D].rearrange("p (h e) -> p h e", h=K2),
                                                bkv[0:SUB, D:2 * D].rearrange("p (h e) -> p h e", h=K2),
                                                ALU.add).then_inc(vx_ready, 1)
                    if j >= 2:
                        a = j - 2
                        dve.wait_ge(rk_ready, PRE + i * U + a + 1)
                        dve.wait_ge(acc_done, PRE + i * U + a + 1 - 2)
                        nc.vector.scalar_tensor_tensor(out=kphi[:, a % 2, :], in0=ek[:, a % 2, :], scalar=1.0,
                                                       in1=rk[:, a % 2, :], op0=ALU.min, op1=ALU.add
                                                       ).then_inc(kphi_ready, 1)
            dve.wait_ge(sums_done, 1)
            for h in range(K2):
                nc.vector.tensor_tensor(kvm[:, h, :], psA[:, h, 0:P], headm[:], ALU.mult).then_inc(kvm_ready, 1)
                nc.vector.tensor_copy(ksum[:, h:h + 1], psA[:, h, P:P + 1]).then_inc(kvm_ready, 1)
            dve.wait_ge(kvm_ready, 4)
            for h in range(K2):
                nc.vector.tensor_scalar(qdiv[:, h, :], headm[:], ksum[:, h:h + 1], None, ALU.mult).then_inc(fin, 1)
            dve.wait_ge(kvmT_ps, 1)
            nc.vector.tensor_copy(kvmT[:], psT[:, 0, 0:K2 * P].rearrange("p (h e) -> p h e", h=K2)).then_inc(kvmT_sb, 1)
            dve.wait_ge(kvwo_ps, 1)
            nc.vector.tensor_copy(kvwo[:], psKV[:, 0, :].rearrange("p (h e) -> p h e", h=K2)).then_inc(fin, 1)

        @block.scalar
        def _(act):
            act.sem_inc(xT_ready, PRE)
            act.sem_inc(xT_saved, PRE)
            act.sem_inc(ek_ready, PRE)
            act.sem_inc(rk_ready, PRE)
            with act.Fori(0, ITERS) as i:
                for j in range(U + 1):
                    if j < U:
                        act.wait_ge(t_ready, PRE + i * U + j + 1)
                        act.wait_ge(xT_saved, PRE + i * U + j + 1 - 2)
                        act.wait_ge(kv_ready, PRE + i * U + j + 1 - 2)
                        nc.scalar.copy(xT[:, j % 2, :, :],
                                       psT[:, j % 2, 0:K2 * SUB].rearrange("p (k n) -> p k n", k=K2)).then_inc(xT_ready, 1)
                    if j >= 1:
                        a = j - 1
                        act.wait_ge(kb_ready, PRE + i * U + a + 1)
                        act.wait_ge(kphi_ready, PRE + i * U + a + 1 - 2)
                        nc.scalar.activation(ek[:, a % 2, :], kb[:, a % 2, :], ACT.Exp).then_inc(ek_ready, 1)
                        nc.scalar.activation(rk[:, a % 2, :], kb[:, a % 2, :], ACT.Relu).then_inc(rk_ready, 1)

        @block.tensor
        def _(pe):
            pe.sem_inc(t_ready, PRE)
            pe.sem_inc(kv_ready, PRE)
            pe.sem_inc(acc_done, PRE)
            pe.wait_ge(zeroed, 2)
            pe.wait_ge(w_in, 64)
            for h in range(K2):
                nc.tensor.matmul(psA[:, h, 0:VE], zero[:, 0:P], zero[:], start=True, stop=False)
            with pe.Fori(0, ITERS) as i:
                for j in range(U + 3):
                    if j < U:
                        pe.wait_ge(xn_ready, PRE + i * U + j + 1)
                        pe.wait_ge(xT_ready, PRE + i * U + j + 1 - 2)
                        for k in range(K2):
                            last = nc.tensor.transpose(psT[:, j % 2, k * SUB:(k + 1) * SUB],
                                                       xnb[:, j, k * P:(k + 1) * P], ident[0:SUB, 0:SUB])
                        last.then_inc(t_ready, 1)
                    if 1 <= j <= U:
                        a = j - 1
                        pe.wait_ge(xT_ready, PRE + i * U + a + 1)
                        pe.wait_ge(kb_ready, PRE + i * U + a + 1 - 2)
                        pe.wait_ge(vx_ready, PRE + i * U + a + 1 - 2)
                        for k in range(K2):
                            last = nc.tensor.matmul(psKV[0:SUB, a % 2, :], xT[:, a % 2, k, :], wkv[:, k, :],
                                                    start=(k == 0), stop=(k == K2 - 1))
                        last.then_inc(kv_ready, 1)
                    if j >= 3:
                        a = j - 3
                        pe.wait_ge(vx_ready, PRE + i * U + a + 1)
                        pe.wait_ge(kphi_ready, PRE + i * U + a + 1)
                        for h in range(K2):
                            last = nc.tensor.matmul(psA[:, h, 0:VE], kphi[:, a % 2, h * P:(h + 1) * P],
                                                    vx[:, a % 2, h, :], start=False, stop=False)
                        last.then_inc(acc_done, 1)
            for h in range(K2):
                last = nc.tensor.matmul(psA[:, h, 0:VE], zero[:, 0:P], zero[:], start=False, stop=True)
            last.then_inc(sums_done, 1)
            pe.wait_ge(kvm_ready, 4)
            for h in range(K2):
                last = nc.tensor.transpose(psT[:, 0, h * P:(h + 1) * P], kvm[:, h, :], ident[:])
            last.then_inc(kvmT_ps, 1)
            pe.wait_ge(kvmT_sb, 1)
            for h in range(K2):
                last = nc.tensor.matmul(psKV[:, 0, h * D:(h + 1) * D], kvmT[:, h, :], wo[:, h, :], start=True, stop=True)
            last.then_inc(kvwo_ps, 1)


BQ, G1, B1LN, B1 = 0, 2, 4, 6
R_BO, R_G1, R_G2, R_LN1B, R_B2, R_LN2B, R_BFC = range(7)

def mix_order(ns):
    pairs = ns // 2
    order = [("oh", s) for s in range(OH)]
    spread = iter(range(SGI))

    def edges(count):
        for s in (next(spread) for _ in range(count)):
            order.append(("ag", s))
            if s + OH < SGI:
                order.append(("oh", s + OH))
            if s:
                order.append(("at", s - 1))

    order.extend([("q", 0), ("q", 1)])
    edges(1)
    order.append(("den", 0))
    edges(1)
    order.append(("den", 1))
    edges(2)
    order.extend(("wo", p) for p in range(pairs))
    edges(1)
    order.append(("ln1", 0))
    edges(1)
    order.extend(("t", p) for p in range(pairs))
    for m in range(FF // P):
        order.append(("w1", m))
        if m % 2:
            edges(1)
    for p in range(pairs):
        order.append(("w2", p))
        edges(4 // pairs)
    order.append(("ln2", 0))
    edges(1)
    order.extend(("out", p) for p in range(pairs))
    edges(1)
    order.append(("at", SGI - 1))
    return order


def mix_phase(nc, io, sb, psum, sem, xnT, accT, ident, src_t, dst_rel, base_i, iota_w,
              qdiv, kvwo, wq, w1, w2, colb, rows, xn_dram, s1_dram):
    F = 3
    NP = GS // 2
    NPG = 2 * NP
    FPG = 2 * K2 + FF // P
    with ExitStack() as ctx:
        ring = sb(ctx, "ring", [P, RING, CPS, D])
        stage = sb(ctx, "stage", [P, 2, HALF * CPS], I32)
        oh = sb(ctx, "oh", [P, OH, CPS, W])
        aggs = sb(ctx, "aggs", [W, 2, D])
        ea = sb(ctx, "ea", [P, K2, GN])
        eb = sb(ctx, "eb", [P, K2, GN])
        qphi = sb(ctx, "qphi", [P, K2, GN])
        xng = sb(ctx, "xng", [SUB, GS, D])
        xg = sb(ctx, "xg", [SUB, GS, D])
        ya = sb(ctx, "ya", [SUB, GS, D])
        yb = sb(ctx, "yb", [SUB, GS, D])
        x1T = sb(ctx, "x1T", [P, K2, GN])
        ffh = sb(ctx, "ffh", [P, FF // P, GN])
        st = sb(ctx, "st2", [SUB, GS, 6])
        mv = sb(ctx, "mv2", [SUB, GS, 2])
        var = sb(ctx, "var2", [SUB, GS])
        rstd = sb(ctx, "rstd2", [SUB, GS])
        tmp = sb(ctx, "tmp2", [SUB, GS])
        psF = psum(ctx, "psF", [P, F, 512])
        psN = psum(ctx, "psN", [P, 2, 2, D])
        psX = psum(ctx, "psX", [P, K2, 2 * P])
        psG = psum(ctx, "psG", [P, 512])
        psH = psum(ctx, "psH", [P, 512])
        mstep = sem(ctx, "mstep")
        stats_taken = sem(ctx, "mstep_stats_taken")
        rows_ready = sem(ctx, "rows_ready")
        staged = sem(ctx, "staged")
        slot_taken = sem(ctx, "slot_taken")
        at_begun = sem(ctx, "at_begun")
        gathered = [sem(ctx, f"gathered{r}") for r in range(RING)]
        oh_ready = sem(ctx, "oh_ready")
        ag_ready = sem(ctx, "ag_ready")
        ag_saved = sem(ctx, "ag_saved")
        at_ready = sem(ctx, "at_ready")
        at_added = sem(ctx, "at_added")
        xn_in = sem(ctx, "xn_in")
        x_in = sem(ctx, "x_in")
        s1_out = sem(ctx, "s1_out")
        f_ready = sem(ctx, "f_ready")
        f_saved = sem(ctx, "f_saved")
        qphi_ready = sem(ctx, "qphi_ready")
        qscaled = sem(ctx, "qscaled")
        n_ready = sem(ctx, "n_ready")
        n_saved = sem(ctx, "n_saved")
        x1_ready = sem(ctx, "x1_ready")
        x_t = sem(ctx, "x_t")
        x1T_ready = sem(ctx, "x1T_ready")
        s1_ready = sem(ctx, "s1_ready")
        block = ctx.enter_context(nc.Block())

        @block.sync
        def _(sp):
            def body(g, ns):
                sp.wait_ge(n_saved, PRE + g * NPG - NP)
                sp.dma_start(xng[:, 0:ns, :], xn_dram[bass.ds(g * GN, ns * SUB), :].rearrange("(j p) d -> p j d", p=SUB)
                             ).then_inc(xn_in, 16)
                sp.wait_ge(s1_ready, PRE + g * NP)
                sp.dma_start(xg[:, 0:ns, :], io["x"][bass.ds(g * GN, ns * SUB), :].rearrange("(j p) d -> p j d", p=SUB)
                             ).then_inc(x_in, 16)
                sp.wait_ge(s1_ready, PRE + g * NP + ns // 2)
                sp.dma_start(s1_dram[bass.ds(g * GN, ns * SUB), :].rearrange("(j p) d -> p j d", p=SUB),
                             yb[:, 0:ns, :]).then_inc(s1_out, 16)

            with sp.Fori(0, GROUPS) as g:
                body(g, GS)
            body(GROUPS, TAIL)
            sp.wait_ge(s1_out, 16 * (GROUPS + 1))

        @block.gpsimd
        def _(pool):
            def body(g):
                for a in range(SGI // HALF):
                    pool.wait_ge(ag_ready, PRE + g * SGI + (a + 1) * HALF - SGI)
                    pool.tensor_copy(stage[:, a, :], src_t[:, bass.ds(g * (SGI * CPS) + a * (HALF * CPS), HALF * CPS)]
                                     ).then_inc(staged, 1)
                    pool.wait_ge(staged, g * (SGI // HALF) + a + 1)
                    for h in range(HALF):
                        s = a * HALF + h
                        r = s % RING
                        pool.wait_ge(ag_ready, PRE + g * SGI + s + 1 - RING)
                        pool.sem_inc(slot_taken, 1)
                        for c in range(CPS):
                            col = h * CPS + c
                            pool.indirect_dma_start(
                                out=ring[:, r, c, :], out_offset=None, in_=xn_dram[:, :],
                                in_offset=bass.IndirectOffsetOnAxis(ap=stage[:, a, col:col + 1], axis=0),
                            ).then_inc(gathered[r], 16)

            with pool.Fori(0, GROUPS) as g:
                body(g)
            body(GROUPS)

        @block.scalar
        def _(act):
            act.sem_inc(f_saved, PRE)
            act.sem_inc(ag_saved, PRE)
            act.sem_inc(x1T_ready, PRE)

            def body(g, ns):
                n = ns * SUB
                for what, s in mix_order(ns):
                    if what == "q":
                        act.wait_ge(f_ready, PRE + g * FPG + s + 1)
                        act.wait_ge(qscaled, PRE + g * K2 + s + 1 - K2)
                        nc.scalar.activation(ea[:, s, 0:n], psF[:, s % F, 0:n], ACT.Exp, bias=colb[:, BQ + s:BQ + s + 1])
                        nc.scalar.activation(eb[:, s, 0:n], psF[:, s % F, 0:n], ACT.Relu, bias=colb[:, BQ + s:BQ + s + 1]
                                             ).then_inc(f_saved, 1)
                    elif what == "den":
                        act.wait_ge(f_ready, PRE + g * FPG + K2 + s + 1)
                        act.wait_ge(qphi_ready, PRE + g * K2 + s + 1)
                        nc.scalar.activation(eb[:, s, 0:n], psF[:, (K2 + s) % F, 0:n], ACT.Copy, bias=1e-6).then_inc(f_saved, 1)
                    elif what == "t":
                        act.wait_ge(x_t, PRE + g * NP + s + 1)
                        act.wait_ge(f_ready, PRE + g * FPG)
                        for k in range(K2):
                            last = nc.scalar.activation(
                                x1T[:, k, s * (2 * SUB):(s + 1) * (2 * SUB)].rearrange("p (j n) -> p j n", j=2),
                                psX[:, k, :].rearrange("p (j n) -> p j n", j=2)[:, :, 0:SUB], ACT.Identity,
                                scale=colb[:, G1 + k:G1 + k + 1], bias=colb[:, B1LN + k:B1LN + k + 1])
                        last.then_inc(x1T_ready, 1)
                    elif what == "w1":
                        act.wait_ge(f_ready, PRE + g * FPG + 2 * K2 + s + 1)
                        if s == 0:
                            act.wait_ge(n_ready, PRE + g * NPG)
                        nc.scalar.activation(ffh[:, s, 0:n], psF[:, (2 * K2 + s) % F, 0:n], ACT.Relu,
                                             bias=colb[:, B1 + s:B1 + s + 1]).then_inc(f_saved, 1)
                    elif what == "ag":
                        act.wait_ge(ag_ready, PRE + g * SGI + s + 1)
                        act.wait_ge(at_ready, PRE + g * SGI + s + 1 - 2)
                        nc.scalar.copy(aggs[:, s % 2, :], psG[0:W, 0:D]).then_inc(ag_saved, 1)

            with act.Fori(0, GROUPS) as g:
                body(g, GS)
            body(GROUPS, TAIL)

        @block.vector
        def _(dve):
            dve.sem_inc(at_added, PRE)
            dve.sem_inc(oh_ready, PRE)
            dve.sem_inc(qphi_ready, PRE)
            dve.sem_inc(qscaled, PRE)
            dve.sem_inc(n_saved, PRE)
            dve.sem_inc(x1_ready, PRE)
            dve.sem_inc(s1_ready, PRE)
            nc.vector.tensor_tensor(rows[:, R_LN1B, :], rows[:, R_LN1B, :], rows[:, R_B2, :], ALU.add).then_inc(rows_ready, 1)
            nc.vector.tensor_tensor(rows[:, R_LN2B, :], rows[:, R_LN2B, :], rows[:, R_BFC, :], ALU.add).then_inc(rows_ready, 1)
            dve.wait_ge(rows_ready, 2)

            def pair(t, p):
                return t[:, 2 * p:2 * p + 2, :]

            def row(r):
                return rows[0:SUB, r:r + 1, :].to_broadcast([SUB, 2, D])

            def norm(step, ns):
                dve.sem_inc(stats_taken, 1)
                for j in range(ns):
                    step.start(nc.vector.bn_aggr(mv[:, j, :], st[:, j, :]))
                step.wait()
                step(nc.vector.tensor_scalar(var[:, 0:ns], mv[:, 0:ns, 1], EPS, None, ALU.add))
                rsqrt_steps(nc, step, var[:, 0:ns], rstd[:, 0:ns], tmp[:, 0:ns])

            def body(g, ns, per):
                n = ns * SUB
                step = Chain(dve, mstep, g * PER, per)
                _, bases = nc.values_load_multi_w_load_instructions(
                    base_i[0:1, bass.ds(g * SGI, SGI)], engines=[mybir.EngineType.DVE], min_val=0, max_val=N - 1)
                for what, s in mix_order(ns):
                    if what == "oh":
                        dve.wait_ge(ag_ready, PRE + g * SGI + s + 1 - OH)
                        nc.vector.tensor_tensor(
                            oh[:, s % OH, :, :],
                            dst_rel[:, bass.ds(g * (SGI * CPS) + s * CPS, CPS)].rearrange("p (c o) -> p c o", o=1).to_broadcast([P, CPS, W]),
                            iota_w[:].rearrange("p (o w) -> p o w", o=1).to_broadcast([P, CPS, W]),
                            ALU.is_equal).then_inc(oh_ready, 1)
                    elif what == "at":
                        dve.wait_ge(at_ready, PRE + g * SGI + s + 1)
                        dve.wait_ge(at_added, PRE + g * SGI + s)
                        win = accT[:, :, bass.ds(bases[s], W)]
                        nc.vector.tensor_tensor(win, win, psH[:, 0:K2 * W].rearrange("p (k w) -> p k w", k=K2),
                                                ALU.add).then_inc(at_added, 1)
                    elif what == "q":
                        dve.wait_ge(f_saved, PRE + g * FPG + s + 1)
                        dve.wait_ge(n_ready, PRE + g * NPG - NP)
                        nc.vector.scalar_tensor_tensor(out=qphi[:, s, 0:n], in0=ea[:, s, 0:n], scalar=1.0, in1=eb[:, s, 0:n],
                                                       op0=ALU.min, op1=ALU.add).then_inc(qphi_ready, 1)
                    elif what == "den":
                        dve.wait_ge(f_saved, PRE + g * FPG + K2 + s + 1)
                        step(nc.vector.reciprocal(ea[:, s, 0:n], eb[:, s, 0:n]))
                        nc.vector.tensor_tensor(qphi[:, s, 0:n], qphi[:, s, 0:n], ea[:, s, 0:n], ALU.mult).then_inc(qscaled, 1)
                    elif what == "wo":
                        dve.wait_ge(xn_in, g * 16 + 16)
                        dve.wait_ge(n_ready, PRE + g * NPG + s + 1)
                        dve.wait_ge(x_t, PRE + g * NP)
                        nc.vector.tensor_tensor(pair(ya, s), psN[0:SUB, s % 2, :, :], pair(xng, s), ALU.add).then_inc(n_saved, 1)
                        dve.wait_ge(n_saved, PRE + g * NPG + s + 1)
                        step(nc.vector.tensor_tensor(pair(ya, s), pair(ya, s), row(R_BO), ALU.add))
                        for j in (2 * s, 2 * s + 1):
                            step.start(nc.vector.bn_stats(st[:, j, :], ya[:, j, :]))
                    elif what == "ln1":
                        step.wait()
                        norm(step, ns)
                        for j in range(ns):
                            last = nc.vector.tensor_scalar(ya[:, j, :], ya[:, j, :], mv[:, j, 0:1], rstd[:, j:j + 1],
                                                           ALU.subtract, ALU.mult)
                            if j % 2:
                                last.then_inc(x1_ready, 1)
                    elif what == "w2":
                        dve.wait_ge(x1_ready, PRE + g * NP + s + 1)
                        dve.wait_ge(s1_out, g * 16)
                        step(nc.vector.tensor_tensor(pair(yb, s), pair(ya, s), row(R_G1), ALU.mult))
                        step(nc.vector.tensor_tensor(pair(yb, s), pair(yb, s), row(R_LN1B), ALU.add))
                        dve.wait_ge(n_ready, PRE + g * NPG + ns // 2 + s + 1)
                        nc.vector.tensor_tensor(pair(yb, s), pair(yb, s), psN[0:SUB, (ns // 2 + s) % 2, :, :], ALU.add
                                                ).then_inc(n_saved, 1)
                        dve.wait_ge(n_saved, PRE + g * NPG + ns // 2 + s + 1)
                        for j in (2 * s, 2 * s + 1):
                            step.start(nc.vector.bn_stats(st[:, j, :], yb[:, j, :]))
                    elif what == "ln2":
                        step.wait()
                        norm(step, ns)
                        dve.wait_ge(x_in, g * 16 + 16)
                    elif what == "out":
                        for j in (2 * s, 2 * s + 1):
                            step.start(nc.vector.tensor_scalar(yb[:, j, :], yb[:, j, :], mv[:, j, 0:1], rstd[:, j:j + 1],
                                                               ALU.subtract, ALU.mult))
                        step.wait()
                        step(nc.vector.tensor_tensor(pair(yb, s), pair(yb, s), row(R_G2), ALU.mult))
                        step(nc.vector.tensor_tensor(pair(yb, s), pair(yb, s), row(R_LN2B), ALU.add))
                        nc.vector.tensor_tensor(pair(yb, s), pair(yb, s), pair(xg, s), ALU.add).then_inc(s1_ready, 1)
                step.end()

            PER = K2 + (NP + GS) + 2 * (GS + 1 + RSQRT_STEPS) + (2 * NP + GS) + (2 * NP + GS)
            with dve.Fori(0, GROUPS) as g:
                body(g, GS, PER)
            body(GROUPS, TAIL, None)

        @block.tensor
        def _(pe):
            pe.sem_inc(f_ready, PRE)
            pe.sem_inc(n_ready, PRE)
            pe.sem_inc(x_t, PRE)
            pe.sem_inc(ag_ready, PRE)
            pe.sem_inc(at_ready, PRE)

            def body(g, ns):
                n = ns * SUB
                for what, s in mix_order(ns):
                    if what == "q":
                        pe.wait_ge(f_saved, PRE + g * FPG + s + 1 - F)
                        for k in range(K2):
                            last = nc.tensor.matmul(psF[:, s % F, 0:n], wq[:, k, s * P:(s + 1) * P],
                                                    xnT[:, k, bass.ds(g * GN, n)], start=(k == 0), stop=(k == K2 - 1))
                        last.then_inc(f_ready, 1)
                    elif what == "den":
                        pe.wait_ge(f_saved, PRE + g * FPG + K2 + s + 1 - F)
                        pe.wait_ge(qphi_ready, PRE + g * K2 + s + 1)
                        nc.tensor.matmul(psF[:, (K2 + s) % F, 0:n], qdiv[:, s, :], qphi[:, s, 0:n],
                                         start=True, stop=True).then_inc(f_ready, 1)
                    elif what == "wo":
                        pe.wait_ge(qscaled, PRE + g * K2 + K2)
                        pe.wait_ge(n_saved, PRE + g * NPG + s + 1 - 2)
                        for j in range(2):
                            for k in range(K2):
                                cut = (2 * s + j) * SUB
                                last = nc.tensor.matmul(psN[0:SUB, s % 2, j, :], qphi[:, k, cut:cut + SUB], kvwo[:, k, :],
                                                        start=(k == 0), stop=(k == K2 - 1))
                        last.then_inc(n_ready, 1)
                    elif what == "t":
                        pe.wait_ge(x1_ready, PRE + g * NP + s + 1)
                        pe.wait_ge(x1T_ready, PRE + g * NP + s)
                        for j in range(2):
                            for k in range(K2):
                                last = nc.tensor.transpose(psX[:, k, j * P:j * P + SUB], ya[:, 2 * s + j, k * P:(k + 1) * P],
                                                           ident[0:SUB, 0:SUB])
                        last.then_inc(x_t, 1)
                    elif what == "w1":
                        pe.wait_ge(x1T_ready, PRE + g * NP + ns // 2)
                        pe.wait_ge(f_saved, PRE + g * FPG + 2 * K2 + s + 1 - F)
                        for k in range(K2):
                            last = nc.tensor.matmul(psF[:, (2 * K2 + s) % F, 0:n], w1[:, k, s * P:(s + 1) * P], x1T[:, k, 0:n],
                                                    start=(k == 0), stop=(k == K2 - 1))
                        last.then_inc(f_ready, 1)
                    elif what == "w2":
                        pe.wait_ge(f_saved, PRE + g * FPG + FPG)
                        pe.wait_ge(n_saved, PRE + g * NPG + ns // 2 + s + 1 - 2)
                        for j in range(2):
                            for k in range(FF // P):
                                cut = (2 * s + j) * SUB
                                last = nc.tensor.matmul(psN[0:SUB, (ns // 2 + s) % 2, j, :], ffh[:, k, cut:cut + SUB], w2[:, k, :],
                                                        start=(k == 0), stop=(k == FF // P - 1))
                        last.then_inc(n_ready, 1)
                    elif what == "ag":
                        pe.wait_ge(oh_ready, PRE + g * SGI + s + 1)
                        pe.wait_ge(ag_saved, PRE + g * SGI + s)
                        pe.wait_ge(gathered[s % RING], (g * (SGI // RING) + s // RING + 1) * (16 * CPS))
                        for c in range(CPS):
                            last = nc.tensor.matmul(psG[0:W, 0:D], oh[:, s % OH, c, :], ring[:, s % RING, c, :],
                                                    start=(c == 0), stop=(c == CPS - 1))
                        last.then_inc(ag_ready, 1)
                    elif what == "at":
                        pe.wait_ge(ag_saved, PRE + g * SGI + s + 1)
                        pe.wait_ge(at_added, PRE + g * SGI + s)
                        pe.sem_inc(at_begun, 1)
                        for k in range(K2):
                            last = nc.tensor.transpose(psH[:, k * W:(k + 1) * W], aggs[:, s % 2, k * P:(k + 1) * P],
                                                       ident[0:W, 0:W])
                        last.then_inc(at_ready, 1)

            with pe.Fori(0, GROUPS) as g:
                body(g, GS)
            body(GROUPS, TAIL)


def rest_phase(nc, io, sb, psum, sem, accT, ident, src_t, iota_w, flag_i, xn_dram):
    WINS = -(-N // W)
    with ExitStack() as ctx:
        dst_rest = sb(ctx, "rest_dst", [P, NCH])
        rows4 = sb(ctx, "rest_rows", [P, CPS, D])
        dst_in = sem(ctx, "rest_dst_in")
        idx = sb(ctx, "rest_idx", [P, CPS], I32)
        rel = sb(ctx, "rest_rel", [P, CPS])
        hot = sb(ctx, "rest_hot", [P, CPS, W])
        psR = psum(ctx, "psR", [P, K2, W])
        idx_ready = sem(ctx, "r_idx_ready")
        rest_in = sem(ctx, "rest_in")
        rest_begun = sem(ctx, "rest_begun")
        rel_ready = sem(ctx, "rel_ready")
        hot_ready = sem(ctx, "hot_ready")
        r_summed = sem(ctx, "r_summed")
        r_added = sem(ctx, "r_added")
        block = ctx.enter_context(nc.Block())

        def some(eng):
            return eng.If(eng.value_load(flag_i[0:1, 0:1], min_val=0, max_val=1))

        @block.gpsimd
        def _(pool):
            with some(pool):
                with pool.Fori(0, NSG) as s:
                    pool.wait_ge(r_added, s * WINS)
                    pool.tensor_copy(idx[:], src_t[:, bass.ds(s * CPS, CPS)]).then_inc(idx_ready, 1)
                    pool.wait_ge(idx_ready, s + 1)
                    pool.sem_inc(rest_begun, 1)
                    for c in range(CPS):
                        pool.indirect_dma_start(out=rows4[:, c, :], out_offset=None, in_=xn_dram[:, :],
                                                in_offset=bass.IndirectOffsetOnAxis(ap=idx[:, c:c + 1], axis=0),
                                                ).then_inc(rest_in, 16)
                    pool.wait_ge(rest_in, (s + 1) * (16 * CPS))

        @block.sync
        def _(sp):
            sp.dma_start(dst_rest[:], io["rest_dram"]).then_inc(dst_in, 16)
            sp.wait_ge(dst_in, 16)

        @block.vector
        def _(dve):
            dve.wait_ge(dst_in, 16)
            with some(dve):
                with dve.Fori(0, NSG) as s:
                    nc.vector.tensor_copy(rel[:], dst_rest[:, bass.ds(s * CPS, CPS)]).then_inc(rel_ready, 1)
                    with dve.Fori(0, WINS) as w:
                        dve.wait_ge(rel_ready, s * (WINS + 1) + w + 1)
                        nc.vector.tensor_tensor(hot[:], rel[:].rearrange("p (c o) -> p c o", o=1).to_broadcast([P, CPS, W]),
                                                iota_w[:].rearrange("p (o w) -> p o w", o=1).to_broadcast([P, CPS, W]),
                                                ALU.is_equal).then_inc(hot_ready, 1)
                        dve.wait_ge(hot_ready, s * WINS + w + 1)
                        nc.vector.tensor_scalar(rel[:], rel[:], -float(W), None, ALU.add).then_inc(rel_ready, 1)
                        dve.wait_ge(r_summed, s * WINS + w + 1)
                        win = accT[:, :, bass.ds(w * W, W)]
                        nc.vector.tensor_tensor(win, win, psR[:], ALU.add).then_inc(r_added, 1)
                        dve.wait_ge(r_added, s * WINS + w + 1)

        @block.tensor
        def _(pe):
            with some(pe):
                with pe.Fori(0, NSG) as s:
                    with pe.Fori(0, WINS) as w:
                        pe.wait_ge(rest_in, (s + 1) * (16 * CPS))
                        pe.wait_ge(hot_ready, s * WINS + w + 1)
                        pe.wait_ge(r_added, s * WINS + w)
                        for k in range(K2):
                            for c in range(CPS):
                                last = nc.tensor.matmul(psR[:, k, :], rows4[:, c, k * P:(k + 1) * P], hot[:, c, :],
                                                        start=(c == 0), stop=(c == CPS - 1))
                        last.then_inc(r_summed, 1)


def gnn_phase(nc, io, sb, psum, sem, xnT, accT, ident, zsum, z_mv, s1_dram, x2_dram):
    F = 4
    NP = GS // 2
    HM = DH // P
    GATES = 3
    FPG = HM + GATES * HM
    with ExitStack() as ctx:
        w_rel = sb(ctx, "w_rel", [P, K2, DH])
        w_root = sb(ctx, "w_root", [P, K2, DH])
        w_ih = sb(ctx, "w_ih", [P, HM, GATES * DH])
        w_fc = sb(ctx, "w_fc", [P, HM, D])
        cols = sb(ctx, "gnn_cols", [P, HM + 2 * GATES * HM])
        hT = sb(ctx, "hT", [P, HM, GN])
        gi = sb(ctx, "gi", [P, 2, GN])
        gg = sb(ctx, "gg", [P, 2, GN])
        go = sb(ctx, "go", [P, 2, GN])
        cell = sb(ctx, "cell", [P, 2, GN])
        tc = sb(ctx, "tc", [P, 2, GN])
        hl = sb(ctx, "hl", [P, HM, GN])
        s1g = sb(ctx, "s1g", [SUB, GS, D])
        x2 = sb(ctx, "x2", [SUB, GS, D])
        zz = sb(ctx, "zz", [SUB, GS, D])
        st = sb(ctx, "st3", [SUB, GS, 6])
        mv = sb(ctx, "mv3", [SUB, GS, 2])
        var = sb(ctx, "var3", [SUB, GS])
        rstd = sb(ctx, "rstd3", [SUB, GS])
        tmp = sb(ctx, "tmp3", [SUB, GS])
        psF = psum(ctx, "psF3", [P, F, 512])
        psN = psum(ctx, "psN3", [P, 2, 2, D])
        psX = psum(ctx, "psX3", [P, 2, K2, 2 * P])
        gw_in = sem(ctx, "gnn_w_in")
        bias_ready = sem(ctx, "bias_ready")
        gstep = sem(ctx, "gstep")
        stats_taken = sem(ctx, "gstep_stats_taken")
        s1_in = sem(ctx, "s1_in")
        x2_out = sem(ctx, "x2_out")
        f_ready = sem(ctx, "gf_ready")
        f_saved = sem(ctx, "gf_saved")
        c_ready = sem(ctx, "c_ready")
        tc_ready = sem(ctx, "tc_ready")
        hl_ready = sem(ctx, "hl_ready")
        fc_ready = sem(ctx, "fc_ready")
        x2_ready = sem(ctx, "x2_ready")
        z_ready = sem(ctx, "z_ready")
        z_t = sem(ctx, "z_t")
        zT_saved = sem(ctx, "zT_saved")
        block = ctx.enter_context(nc.Block())

        def order(ns):
            out = [("h", m) for m in range(HM)]
            for m in range(HM + 1):
                if m < HM:
                    out += [("gate", (m, x)) for x in range(GATES)]
                if m < HM:
                    out.append(("cell", m))
                if m:
                    out.append(("tanh", m - 1))
            out += [("fc", p) for p in range(ns // 2)] + [("ln", 0)] + [("t", p) for p in range(ns // 2)]
            return out

        @block.sync
        def _(sp):
            for dst, src in ((w_rel, "w_rel"), (w_root, "w_root"), (w_ih, "w_ih"), (w_fc, "w_fc"), (cols, "gnn_cols")):
                sp.dma_start(dst[:], io[src]).then_inc(gw_in, 16)

            def body(g, ns):
                sp.wait_ge(x2_ready, PRE + g * NP)
                sp.dma_start(s1g[:, 0:ns, :], s1_dram[bass.ds(g * GN, ns * SUB), :].rearrange("(j p) d -> p j d", p=SUB)
                             ).then_inc(s1_in, 16)
                sp.wait_ge(x2_ready, PRE + g * NP + ns // 2)
                sp.dma_start(x2_dram[bass.ds(g * GN, ns * SUB), :].rearrange("(j p) d -> p j d", p=SUB), x2[:, 0:ns, :]
                             ).then_inc(x2_out, 16)

            with sp.Fori(0, GROUPS) as g:
                body(g, GS)
            body(GROUPS, TAIL)
            sp.wait_ge(x2_out, 16 * (GROUPS + 1))

        @block.scalar
        def _(act):
            act.sem_inc(f_saved, PRE)
            act.sem_inc(tc_ready, PRE)
            act.sem_inc(zT_saved, PRE)
            act.wait_ge(bias_ready, 1)

            def body(g, ns):
                n = ns * SUB
                for what, s in order(ns):
                    if what == "h":
                        act.wait_ge(f_ready, PRE + g * FPG + s + 1)
                        nc.scalar.activation(hT[:, s, 0:n], psF[:, s % F, 0:n], ACT.Relu, bias=cols[:, s:s + 1]
                                             ).then_inc(f_saved, 1)
                    elif what == "gate":
                        m, x = s
                        pos = HM + GATES * m + x
                        act.wait_ge(f_ready, PRE + g * FPG + pos + 1)
                        if x == 0:
                            act.wait_ge(c_ready, PRE + g * HM + m + 1 - 2)
                        if x == 2:
                            act.wait_ge(hl_ready, PRE + g * HM + m + 1 - 2)
                        dst = (gi, gg, go)[x]
                        nc.scalar.activation(dst[:, m % 2, 0:n], psF[:, pos % F, 0:n], (ACT.Sigmoid, ACT.Tanh, ACT.Sigmoid)[x],
                                             bias=cols[:, HM + x * HM + m:HM + x * HM + m + 1]).then_inc(f_saved, 1)
                    elif what == "tanh":
                        act.wait_ge(c_ready, PRE + g * HM + s + 1)
                        act.wait_ge(hl_ready, PRE + g * HM + s + 1 - 2)
                        nc.scalar.activation(tc[:, s % 2, 0:n], cell[:, s % 2, 0:n], ACT.Tanh).then_inc(tc_ready, 1)
                    elif what == "t":
                        act.wait_ge(z_t, PRE + g * NP + s + 1)
                        for k in range(K2):
                            last = nc.scalar.copy(
                                xnT[:, k, bass.ds(g * GN + s * (2 * SUB), 2 * SUB)].rearrange("p (j n) -> p j n", j=2),
                                psX[:, s % 2, k, :].rearrange("p (j n) -> p j n", j=2)[:, :, 0:SUB])
                        last.then_inc(zT_saved, 1)

            with act.Fori(0, GROUPS) as g:
                body(g, GS)
            body(GROUPS, TAIL)

        @block.vector
        def _(dve):
            dve.sem_inc(c_ready, PRE)
            dve.sem_inc(hl_ready, PRE)
            dve.sem_inc(x2_ready, PRE)
            dve.sem_inc(z_ready, PRE)
            PER = GS + GS + 1 + RSQRT_STEPS
            dve.wait_ge(gw_in, 80)
            nc.vector.tensor_tensor(cols[:, HM:HM + GATES * HM], cols[:, HM:HM + GATES * HM],
                                    cols[:, HM + GATES * HM:HM + 2 * GATES * HM], ALU.add).then_inc(bias_ready, 1)

            def body(g, ns, per):
                n = ns * SUB
                step = Chain(dve, gstep, g * PER, per)
                for what, s in order(ns):
                    if what == "cell":
                        dve.wait_ge(f_saved, PRE + g * FPG + HM + GATES * s + 2)
                        dve.wait_ge(tc_ready, PRE + g * HM + s + 1 - 2)
                        nc.vector.tensor_tensor(cell[:, s % 2, 0:n], gi[:, s % 2, 0:n], gg[:, s % 2, 0:n],
                                                ALU.mult).then_inc(c_ready, 1)
                    elif what == "tanh":
                        dve.wait_ge(f_saved, PRE + g * FPG + HM + GATES * s + 3)
                        dve.wait_ge(tc_ready, PRE + g * HM + s + 1)
                        dve.wait_ge(fc_ready, PRE + g * NP)
                        nc.vector.tensor_tensor(hl[:, s, 0:n], go[:, s % 2, 0:n], tc[:, s % 2, 0:n],
                                                ALU.mult).then_inc(hl_ready, 1)
                    elif what == "fc":
                        if s == 0:
                            dve.wait_ge(s1_in, g * 16 + 16)
                            dve.wait_ge(x2_out, g * 16)
                        dve.wait_ge(fc_ready, PRE + g * NP + s + 1)
                        nc.vector.tensor_tensor(x2[:, 2 * s:2 * s + 2, :], psN[0:SUB, s % 2, :, :], s1g[:, 2 * s:2 * s + 2, :],
                                                ALU.add).then_inc(x2_ready, 1)
                        dve.wait_ge(x2_ready, PRE + g * NP + s + 1)
                        for j in (2 * s, 2 * s + 1):
                            step.start(nc.vector.bn_stats(st[:, j, :], x2[:, j, :]))
                    elif what == "ln":
                        step.wait()
                        dve.sem_inc(stats_taken, 1)
                        for j in range(ns):
                            step.start(nc.vector.bn_aggr(mv[:, j, :], st[:, j, :]))
                        step.wait()
                        step(nc.vector.tensor_scalar(var[:, 0:ns], mv[:, 0:ns, 1], EPS, None, ALU.add))
                        rsqrt_steps(nc, step, var[:, 0:ns], rstd[:, 0:ns], tmp[:, 0:ns])
                        nc.vector.tensor_copy(z_mv[:, bass.ds(g * GS, ns), 0], mv[:, 0:ns, 0])
                        nc.vector.tensor_copy(z_mv[:, bass.ds(g * GS, ns), 1], rstd[:, 0:ns])
                        dve.wait_ge(z_t, PRE + g * NP)
                        for j in range(ns):
                            last = nc.vector.tensor_scalar(zz[:, j, :], x2[:, j, :], mv[:, j, 0:1], rstd[:, j:j + 1],
                                                           ALU.subtract, ALU.mult)
                            if j % 2:
                                last.then_inc(z_ready, 1)
                    elif what == "t":
                        dve.wait_ge(zT_saved, PRE + g * NP + s + 1)
                        nc.vector.tensor_reduce(zsum[:, :, bass.ds(g * NP + s, 1)].rearrange("p k o -> p (k o)"),
                                                xnT[:, :, bass.ds(g * GN + s * (2 * SUB), 2 * SUB)], AX.X, ALU.add)
                step.end()

            with dve.Fori(0, GROUPS) as g:
                body(g, GS, PER)
            body(GROUPS, TAIL, None)

        @block.tensor
        def _(pe):
            pe.sem_inc(f_ready, PRE)
            pe.sem_inc(fc_ready, PRE)
            pe.sem_inc(z_t, PRE)
            pe.wait_ge(gw_in, 80)

            def body(g, ns):
                n = ns * SUB
                for what, s in order(ns):
                    if what == "h":
                        pe.wait_ge(f_saved, PRE + g * FPG + s + 1 - F)
                        for k in range(K2):
                            nc.tensor.matmul(psF[:, s % F, 0:n], w_rel[:, k, s * P:(s + 1) * P],
                                             accT[:, k, bass.ds(g * GN, n)], start=(k == 0), stop=False)
                        for k in range(K2):
                            last = nc.tensor.matmul(psF[:, s % F, 0:n], w_root[:, k, s * P:(s + 1) * P],
                                                    xnT[:, k, bass.ds(g * GN, n)], start=False, stop=(k == K2 - 1))
                        last.then_inc(f_ready, 1)
                    elif what == "gate":
                        m, x = s
                        pos = HM + GATES * m + x
                        pe.wait_ge(f_saved, PRE + g * FPG + max(HM, pos + 1 - F))
                        for k in range(HM):
                            last = nc.tensor.matmul(psF[:, pos % F, 0:n], w_ih[:, k, x * DH + m * P:x * DH + (m + 1) * P],
                                                    hT[:, k, 0:n], start=(k == 0), stop=(k == HM - 1))
                        last.then_inc(f_ready, 1)
                    elif what == "fc":
                        pe.wait_ge(hl_ready, PRE + g * HM + HM)
                        pe.wait_ge(x2_ready, PRE + g * NP + s + 1 - 2)
                        for j in range(2):
                            for k in range(HM):
                                cut = (2 * s + j) * SUB
                                last = nc.tensor.matmul(psN[0:SUB, s % 2, j, :], hl[:, k, cut:cut + SUB], w_fc[:, k, :],
                                                        start=(k == 0), stop=(k == HM - 1))
                        last.then_inc(fc_ready, 1)
                    elif what == "t":
                        pe.wait_ge(z_ready, PRE + g * NP + s + 1)
                        pe.wait_ge(zT_saved, PRE + g * NP + s + 1 - 2)
                        for j in range(2):
                            for k in range(K2):
                                last = nc.tensor.transpose(psX[:, s % 2, k, j * P:j * P + SUB],
                                                           zz[:, 2 * s + j, k * P:(k + 1) * P], ident[0:SUB, 0:SUB])
                        last.then_inc(z_t, 1)

            with pe.Fori(0, GROUPS) as g:
                body(g, GS)
            body(GROUPS, TAIL)


def route_phase(nc, io, sb, psum, sem, zsum, e1, e2, e1b, zb2):
    CAP = float(-(-N * 5 // (4 * NE)))
    HM = DH // P
    with ExitStack() as ctx:
        wr = sb(ctx, "wr", [P, K2, NE])
        br = sb(ctx, "br", [1, NE])
        ones = sb(ctx, "ones", [1, P])
        zm = sb(ctx, "zm", [P, K2])
        a = sb(ctx, "a", [1, NE])
        ex = sb(ctx, "ex", [1, NE])
        rw = sb(ctx, "rw", [1, NE])
        ld = sb(ctx, "ld", [1, NE])
        mx = sb(ctx, "mx", [1, 1])
        sm = sb(ctx, "sm", [1, 1])
        rs = sb(ctx, "rs", [1, 1])
        tv = sb(ctx, "tv", [1, NE])
        ti = sb(ctx, "ti", [1, NE], U32)
        wt = sb(ctx, "wt", [1, 2])
        wb = sb(ctx, "wb", [P, 2])
        b2 = sb(ctx, "b2", [P, 2, D])
        psL = psum(ctx, "psL", [P, NE])
        psW = psum(ctx, "psW", [P, 2])
        r_in = sem(ctx, "route_in")
        rstep = sem(ctx, "rstep")
        zm_ready = sem(ctx, "zm_ready")
        lg_ready = sem(ctx, "lg_ready")
        arg_ready = sem(ctx, "arg_ready")
        exp_ready = sem(ctx, "exp_ready")
        top_ready = sem(ctx, "top_ready")
        wt_ready = sem(ctx, "wt_ready")
        wb_ready = sem(ctx, "wb_ready")
        e_in = sem(ctx, "e_in")
        block = ctx.enter_context(nc.Block())

        @block.sync
        def _(sp):
            sp.dma_start(wr[:], io["ffn_wr"]).then_inc(r_in, 16)
            sp.dma_start(br[:], io["ffn_br"]).then_inc(r_in, 16)
            sp.wait_ge(top_ready, 1)
            for s in range(2):
                e = sp.value_load(ti[0:1, s:s + 1], min_val=0, max_val=NE - 1)
                rows = bass.ds(e * P, P)
                sp.dma_start(e1[:, s, :, :], io["ffn_w1"][rows, :].rearrange("p (k f) -> p k f", k=K2)).then_inc(e_in, 16)
                sp.dma_start(e2[:, s * HM:(s + 1) * HM, :], io["ffn_w2"][rows, :].rearrange("p (k f) -> p k f", k=HM)
                             ).then_inc(e_in, 16)
                sp.dma_start(e1b[:, s, :], io["ffn_b1"][rows, :]).then_inc(e_in, 16)
                sp.dma_start(b2[:, s, :], io["ffn_b2"][rows, :]).then_inc(e_in, 16)
            sp.wait_ge(e_in, 128)

        @block.scalar
        def _(act):
            for n in range(3):
                act.wait_ge(arg_ready, n + 1)
                width = 2 if n == 2 else NE
                nc.scalar.activation(ex[0:1, 0:width], a[0:1, 0:width], ACT.Exp, accum_out=sm[:]).then_inc(exp_ready, 1)

        @block.vector
        def _(dve):
            step = Chain(dve, rstep, 0, None)
            step(nc.vector.memset(ones[:], 1.0))
            step(nc.vector.tensor_reduce(zm[:], zsum[:], AX.X, ALU.add))
            nc.vector.tensor_scalar(zm[:], zm[:], 1.0 / N, None, ALU.mult).then_inc(zm_ready, 1)
            dve.wait_ge(r_in, 32)
            dve.wait_ge(lg_ready, 1)
            step(nc.vector.tensor_tensor(rw[:], psL[0:1, :], br[:], ALU.add))

            def softmax(src, n, dst, width):
                step(nc.vector.tensor_reduce(mx[:], src, AX.X, ALU.max))
                nc.vector.tensor_scalar(a[0:1, 0:width], src, mx[:], None, ALU.subtract).then_inc(arg_ready, 1)
                dve.wait_ge(exp_ready, n)
                step(nc.vector.reciprocal(rs[:], sm[:]))
                return nc.vector.tensor_scalar(dst, ex[0:1, 0:width], rs[:], None, ALU.mult)

            step(softmax(rw[:], 1, rw[:], NE))
            step(nc.vector.tensor_scalar(ld[:], rw[:], float(N), None, ALU.mult))
            step(nc.vector.reciprocal(ld[:], ld[:]))
            step(nc.vector.tensor_scalar(ld[:], ld[:], CAP, 1.0, ALU.mult, ALU.min))
            step(nc.vector.tensor_tensor(rw[:], rw[:], ld[:], ALU.mult))
            step(softmax(rw[:], 2, rw[:], NE))
            step(nc.vector.max(tv[:], rw[:]))
            nc.vector.max_index(ti[:], tv[:], rw[:]).then_inc(top_ready, 1)
            softmax(tv[0:1, 0:2], 3, wt[:], 2).then_inc(wt_ready, 1)
            dve.wait_ge(wb_ready, 1)
            step(nc.vector.tensor_copy(wb[:], psW[:]))
            dve.wait_ge(e_in, 128)
            step(nc.vector.tensor_scalar(zb2[:], b2[:, 0, :], wb[:, 0:1], None, ALU.mult))
            step(nc.vector.scalar_tensor_tensor(out=zb2[:], in0=b2[:, 1, :], scalar=wb[:, 1:2], in1=zb2[:],
                                                op0=ALU.mult, op1=ALU.add))
            for s in range(2):
                step(nc.vector.tensor_scalar(e2[:, s * HM:(s + 1) * HM, :], e2[:, s * HM:(s + 1) * HM, :], wb[:, s:s + 1],
                                             None, ALU.mult))

        @block.tensor
        def _(pe):
            pe.wait_ge(r_in, 32)
            pe.wait_ge(zm_ready, 1)
            for k in range(K2):
                last = nc.tensor.matmul(psL[0:1, :], zm[:, k:k + 1], wr[:, k, :], start=(k == 0), stop=(k == K2 - 1))
            last.then_inc(lg_ready, 1)
            pe.wait_ge(wt_ready, 1)
            nc.tensor.matmul(psW[:], ones[:], wt[:], start=True, stop=True).then_inc(wb_ready, 1)


def moe_phase(nc, io, sb, psum, sem, xnT, z_mv, e1, e2, e1b, zb2, x2_dram):
    F = 4
    HM = DH // P
    TILES = 2 * HM
    with ExitStack() as ctx:
        gb = sb(ctx, "gb", [P, 2, D])
        hg = sb(ctx, "hg", [P, TILES, GN])
        x2 = sb(ctx, "x2m", [SUB, GS, D])
        y = sb(ctx, "ym", [SUB, GS, D])
        st = sb(ctx, "st4", [SUB, GS, 6])
        mv = sb(ctx, "mv4", [SUB, GS, 2])
        var = sb(ctx, "var4", [SUB, GS])
        rstd = sb(ctx, "rstd4", [SUB, GS])
        tmp = sb(ctx, "tmp4", [SUB, GS])
        psF = psum(ctx, "psF4", [P, F, 512])
        psN = psum(ctx, "psN4", [P, 4, 512])
        gb_in = sem(ctx, "gb_in")
        x2_in = sem(ctx, "x2_in")
        y_out = sem(ctx, "y_out")
        f_ready = sem(ctx, "mf_ready")
        f_saved = sem(ctx, "mf_saved")
        n_ready = sem(ctx, "mn_ready")
        n_saved = sem(ctx, "mn_saved")
        y_ready = sem(ctx, "y_ready")
        ystep = sem(ctx, "ystep")
        stats_taken = sem(ctx, "ystep_stats_taken")
        block = ctx.enter_context(nc.Block())

        @block.sync
        def _(sp):
            sp.dma_start(gb[:], io["ffn_gb"]).then_inc(gb_in, 16)

            def body(g, ns):
                sp.wait_ge(y_ready, PRE + g * GS)
                sp.dma_start(x2[:, 0:ns, :], x2_dram[bass.ds(g * GN, ns * SUB), :].rearrange("(j p) d -> p j d", p=SUB)
                             ).then_inc(x2_in, 16)
                sp.wait_ge(y_ready, PRE + g * GS + ns)
                sp.dma_start(io["out"][bass.ds(g * GN, ns * SUB), :].rearrange("(j p) d -> p j d", p=SUB), y[:, 0:ns, :]
                             ).then_inc(y_out, 16)

            with sp.Fori(0, GROUPS) as g:
                body(g, GS)
            body(GROUPS, TAIL)
            sp.wait_ge(y_out, 16 * (GROUPS + 1))

        @block.scalar
        def _(act):
            act.sem_inc(f_saved, PRE)

            def body(g, ns):
                n = ns * SUB
                for m in range(TILES):
                    act.wait_ge(f_ready, PRE + g * TILES + m + 1)
                    if m == 0:
                        act.wait_ge(n_ready, PRE + g * GS)
                    nc.scalar.activation(hg[:, m, 0:n], psF[:, m % F, 0:n], ACT.Gelu, bias=e1b[:, m // HM, m % HM:m % HM + 1]
                                         ).then_inc(f_saved, 1)

            with act.Fori(0, GROUPS) as g:
                body(g, GS)
            body(GROUPS, TAIL)

        @block.vector
        def _(dve):
            dve.sem_inc(n_saved, PRE)
            dve.sem_inc(y_ready, PRE)
            PER = 3 * GS + GS + 1 + RSQRT_STEPS + 3 * GS
            dve.wait_ge(gb_in, 16)

            def body(g, ns, per):
                step = Chain(dve, ystep, g * PER, per)
                dve.wait_ge(x2_in, g * 16 + 16)
                dve.wait_ge(y_out, g * 16)
                for j in range(ns):
                    step(nc.vector.tensor_scalar(y[:, j, :], x2[:, j, :], z_mv[:, bass.ds(g * GS + j, 1), 0],
                                                 z_mv[:, bass.ds(g * GS + j, 1), 1], ALU.subtract, ALU.mult))
                    step(nc.vector.tensor_tensor(y[:, j, :], y[:, j, :], zb2[0:SUB, :], ALU.add))
                for j in range(ns):
                    dve.wait_ge(n_ready, PRE + g * GS + j + 1)
                    nc.vector.tensor_tensor(y[:, j, :], y[:, j, :], psN[0:SUB, j, 0:D], ALU.add).then_inc(n_saved, 1)
                    dve.wait_ge(n_saved, PRE + g * GS + j + 1)
                    step(nc.vector.bn_stats(st[:, j, :], y[:, j, :]))
                dve.sem_inc(stats_taken, 1)
                for j in range(ns):
                    step.start(nc.vector.bn_aggr(mv[:, j, :], st[:, j, :]))
                step.wait()
                step(nc.vector.tensor_scalar(var[:, 0:ns], mv[:, 0:ns, 1], EPS, None, ALU.add))
                rsqrt_steps(nc, step, var[:, 0:ns], rstd[:, 0:ns], tmp[:, 0:ns])
                for j in range(ns):
                    step(nc.vector.tensor_scalar(y[:, j, :], y[:, j, :], mv[:, j, 0:1], rstd[:, j:j + 1],
                                                 ALU.subtract, ALU.mult))
                    step(nc.vector.tensor_tensor(y[:, j, :], y[:, j, :], gb[0:SUB, 0, :], ALU.mult))
                    step(nc.vector.tensor_tensor(y[:, j, :], y[:, j, :], gb[0:SUB, 1, :], ALU.add))
                    nc.vector.tensor_tensor(y[:, j, :], y[:, j, :], x2[:, j, :], ALU.add).then_inc(y_ready, 1)
                step.end()

            with dve.Fori(0, GROUPS) as g:
                body(g, GS, PER)
            body(GROUPS, TAIL, None)

        @block.tensor
        def _(pe):
            pe.sem_inc(f_ready, PRE)
            pe.sem_inc(n_ready, PRE)

            def body(g, ns):
                n = ns * SUB
                for m in range(TILES):
                    pe.wait_ge(f_saved, PRE + g * TILES + m + 1 - F)
                    for k in range(K2):
                        last = nc.tensor.matmul(psF[:, m % F, 0:n], e1[:, m // HM, k, (m % HM) * P:(m % HM + 1) * P],
                                                xnT[:, k, bass.ds(g * GN, n)], start=(k == 0), stop=(k == K2 - 1))
                    last.then_inc(f_ready, 1)
                for j in range(ns):
                    pe.wait_ge(f_saved, PRE + g * TILES + TILES)
                    pe.wait_ge(n_saved, PRE + g * GS + j + 1 - GS)
                    for m in range(TILES):
                        last = nc.tensor.matmul(psN[0:SUB, j, 0:D], hg[:, m, j * SUB:(j + 1) * SUB], e2[:, m, :],
                                                start=(m == 0), stop=(m == TILES - 1))
                    last.then_inc(n_ready, 1)

            with pe.Fori(0, GROUPS) as g:
                body(g, GS)
            body(GROUPS, TAIL)


def kernel(**inputs):
    import numpy as _np
    import concourse.bacc as _bacc
    from concourse.bass_utils import run_bass_kernel_spmd as _run

    a = {name: _np.ascontiguousarray(value) for name, value in inputs.items()}

    def kxn(w):
        return _np.ascontiguousarray(w.reshape(-1, P, w.shape[-1]).transpose(1, 0, 2))

    def columns(*vectors):
        return _np.concatenate([v.reshape(-1, P).T for v in vectors], axis=1)

    def broadcast_rows(*vectors):
        return _np.ascontiguousarray(_np.broadcast_to(_np.stack(vectors)[None], (P, len(vectors), vectors[0].shape[0])))

    def edges(v, pad):
        full = _np.full(NCH * P, pad, v.dtype)
        full[:EDGES] = v
        return _np.ascontiguousarray(full.reshape(NCH, P).T)

    head = _np.arange(P) // 32
    w_ih = a["L0_gnn_W_ih"].reshape(4, DH, DH)
    gates = [0, 2, 3]
    arrays = {
        "x": a["x"],
        "src": edges(a["src"], 0), "dst": edges(a["dst"], PAD_DST),
        "mix_wkv": kxn(_np.concatenate([a["L0_mix_Wk"], a["L0_mix_Wv"]], axis=1)),
        "mix_bkv": broadcast_rows(_np.concatenate([a["L0_mix_bk"], a["L0_mix_bv"]])).reshape(P, 2 * D),
        "mix_wq": kxn(a["L0_mix_Wq"]), "mix_wo": kxn(a["L0_mix_Wo"]),
        "mix_w1": kxn(a["L0_mix_W1"]), "mix_w2": kxn(a["L0_mix_W2"]),
        "mix_cols": columns(a["L0_mix_bq"], a["L0_mix_ln1_g"], a["L0_mix_ln1_b"], a["L0_mix_b1"]),
        "mix_rows": broadcast_rows(a["L0_mix_bo"], a["L0_mix_ln1_g"], a["L0_mix_ln2_g"], a["L0_mix_ln1_b"],
                                   a["L0_mix_b2"], a["L0_mix_ln2_b"], a["L0_gnn_b_fc"]),
        "headm": (head[:, None] == head[None, :]).astype(_np.float32),
        "w_rel": kxn(a["L0_gnn_W_rel"]), "w_root": kxn(a["L0_gnn_W_root"]),
        "w_ih": kxn(_np.ascontiguousarray(_np.concatenate([w_ih[g] for g in gates]).T)),
        "w_fc": kxn(a["L0_gnn_W_fc"]),
        "gnn_cols": columns(a["L0_gnn_b_rel"], *[a[b].reshape(4, DH)[g] for b in ("L0_gnn_b_ih", "L0_gnn_b_hh") for g in gates]),
        "ffn_wr": kxn(a["L0_ffn_Wr"]), "ffn_br": a["L0_ffn_br"].reshape(1, NE),
        "ffn_w1": _np.ascontiguousarray(a["L0_ffn_W1"].reshape(NE, K2, P, DH).transpose(0, 2, 1, 3)).reshape(NE * P, K2 * DH),
        "ffn_w2": _np.ascontiguousarray(a["L0_ffn_W2"].reshape(NE, DH // P, P, D).transpose(0, 2, 1, 3)).reshape(NE * P, -1),
        "ffn_b1": _np.ascontiguousarray(a["L0_ffn_b1"].reshape(NE, DH // P, P).transpose(0, 2, 1)).reshape(NE * P, -1),
        "ffn_b2": _np.ascontiguousarray(_np.broadcast_to(a["L0_ffn_b2"][:, None, :], (NE, P, D))).reshape(NE * P, D),
        "ffn_gb": broadcast_rows(a["L0_ffn_gamma"], a["L0_ffn_beta"]),
    }
    nc = _bacc.Bacc("TRN2", target_bir_lowering=False, num_devices=1)
    arrays = {f"in_{name}": _np.ascontiguousarray(v) for name, v in arrays.items()}
    io = {name[3:]: nc.dram_tensor(name, v.shape, mybir.dt.from_np(v.dtype), kind="ExternalInput").ap()
          for name, v in arrays.items()}
    for name in ("xn_dram", "s1_dram", "x2_dram"):
        io[name] = nc.dram_tensor(name, (N, D), F32, kind="Internal").ap()
    io["rest_dram"] = nc.dram_tensor("rest_dram", (P, NCH), F32, kind="Internal").ap()
    io["out"] = nc.dram_tensor("out", (N, D), F32, kind="ExternalOutput").ap()
    gps_layer(nc, io)
    r = _run(nc, [arrays], core_ids=[0])
    return r.results[0]["out"]
```

```python
from contextlib import ExitStack

import numpy as np

import concourse.bass as bass
from concourse import mybir

F32 = mybir.dt.float32
F32R = mybir.dt.float32r
F16 = mybir.dt.float16
I32 = mybir.dt.int32
U32 = mybir.dt.uint32
ALU = mybir.AluOpType
ACT = mybir.ActivationFunctionType
AX = mybir.AxisListType
RMAX = bass.bass_isa.ReduceOp.max

P = 128
N = 6250
D = 256
K2 = D // P
DH = 512
FF = 1024
NE = 8
EDGES = 106250
SUB = 125
GS = 4
GN = GS * SUB
GROUPS = N // GN
TAIL = (N - GROUPS * GN) // SUB
NPAD = (GROUPS + 1) * GN
NSUB = N // SUB
W = 64
CPS = 4
SGE = CPS * P
NSG = -(-EDGES // SGE)
NCH = NSG * CPS
ACC = max(N + W, NPAD)
SGI = NSG // (GROUPS + 1)
RING = 4
HALF = 8
OH = 4
LEAD = 2
LAG = 1
NORM_U = 10
BIG = float(2 ** 14)
PAD_DST = 2 ** 20
EPS = 1e-5
PRE = 16

assert NSG == SGI * (GROUPS + 1) and SGI % RING == 0 and NSUB % NORM_U == 0 and N < BIG


class Chain:

    def __init__(self, eng, sem, base, per):
        self.eng, self.sem, self.base, self.per, self.k = eng, sem, base, per, 0

    def __call__(self, ins):
        self.k += 1
        ins.then_inc(self.sem, 1)
        self.eng.wait_ge(self.sem, self.base + self.k)

    def start(self, ins):
        self.k += 1
        ins.then_inc(self.sem, 1)

    def wait(self):
        self.eng.wait_ge(self.sem, self.base + self.k)

    def end(self):
        assert self.per in (None, self.k), self.k


def rsqrt_guess(nc, step, v, y, t):
    step(nc.vector.tensor_scalar(t.bitcast(I32), v.bitcast(I32), 1, None, ALU.logical_shift_right))
    step(nc.vector.tensor_scalar(y.bitcast(I32), t.bitcast(I32), -1.0, float(0x5F3759DF), ALU.mult, ALU.add))


def rsqrt_newton(nc, step, v, y, t, rounds):
    for _ in range(rounds):
        step(nc.vector.tensor_tensor(t, y, y, ALU.mult))
        step(nc.vector.tensor_tensor(t, t, v, ALU.mult))
        step(nc.vector.tensor_scalar(t, t, -0.5, 1.5, ALU.mult, ALU.add))
        step(nc.vector.tensor_tensor(y, y, t, ALU.mult))


def rsqrt_steps(nc, step, v, y, t):
    rsqrt_guess(nc, step, v, y, t)
    rsqrt_newton(nc, step, v, y, t, 3)


RSQRT_STEPS = 14


def gps_layer(nc, io):
    with ExitStack() as whole:
        def sb(ctx, name, shape, dt=F32):
            return ctx.enter_context(nc.sbuf_tensor(name, shape, dt))

        def psum(ctx, name, shape):
            return ctx.enter_context(nc.psum_tensor(name, shape, F32))

        def sem(ctx, name):
            return ctx.enter_context(nc.semaphore(name))

        xn_dram, s1_dram, x2_dram = io["xn_dram"], io["s1_dram"], io["x2_dram"]

        accT = sb(whole, "accT", [P, K2, ACC])
        ident = sb(whole, "ident", [P, P])
        flag_i = sb(whole, "flag_i", [P, 1], I32)
        zsum = sb(whole, "zsum", [P, K2, NSUB // 2])
        z_mv = sb(whole, "z_mv", [SUB, NSUB, 2])
        with ExitStack() as mixw:
            xnT = sb(mixw, "xnT", [P, K2, NPAD])
            src_t = sb(mixw, "src_t", [P, NCH], I32)
            dst_rel = sb(mixw, "dst_rel", [P, NCH + LEAD * CPS])
            base_i = sb(mixw, "base_i", [P, LAG + NSG], I32)
            iota_w = sb(mixw, "iota_w", [P, W])
            qdiv = sb(mixw, "qdiv", [P, K2, P])
            kvwo = sb(mixw, "kvwo", [P, K2, D])
            wq = sb(mixw, "wq", [P, K2, D])
            w1 = sb(mixw, "w1", [P, K2, FF])
            w2 = sb(mixw, "w2", [P, FF // P, D])
            colb = sb(mixw, "colb", [P, 14])
            rows = sb(mixw, "rows", [P, 7, D])
            set_up(nc, io, sb, psum, sem, ident, src_t, dst_rel, base_i, flag_i, iota_w, accT,
                   wq, w1, w2, colb, rows)
            norm_phase(nc, io, sb, psum, sem, xnT, ident, xn_dram, qdiv, kvwo)
            mix_phase(nc, io, sb, psum, sem, xnT, accT, ident, src_t, dst_rel, base_i, iota_w,
                      qdiv, kvwo, wq, w1, w2, colb, rows, xn_dram, s1_dram)
            rest_phase(nc, io, sb, psum, sem, accT, ident, src_t, iota_w, flag_i, xn_dram)
        with ExitStack() as gnnw:
            w_rel = sb(gnnw, "w_rel", [P, 2, K2, DH], F32R)
            w_root = sb(gnnw, "w_root", [P, 2, K2, DH], F32R)
            w_ih = sb(gnnw, "w_ih", [P, 2, DH // P, 3 * DH], F32R)
            split_weights(nc, io, sb, psum, sem, w_rel, w_root, w_ih)
            gnn_phase(nc, io, sb, psum, sem, accT, ident, zsum, z_mv, w_rel, w_root, w_ih, s1_dram, x2_dram)
        e1 = sb(whole, "e1", [P, 2, K2, DH])
        e2 = sb(whole, "e2", [P, 2 * DH // P, D])
        e1b = sb(whole, "e1b", [P, 2, DH // P])
        zb2 = sb(whole, "zb2", [P, D])
        route_phase(nc, io, sb, psum, sem, zsum, e1, e2, e1b, zb2)
        moe_phase(nc, io, sb, psum, sem, accT, z_mv, e1, e2, e1b, zb2, x2_dram)


def set_up(nc, io, sb, psum, sem, ident, src_t, dst_rel, base_i, flag_i, iota_w, accT,
           wq, w1, w2, colb, rows):
    with ExitStack() as ctx:
        dst_t = sb(ctx, "dst_t", [P, NCH], I32)
        dst_rest = sb(ctx, "dst_rest", [P, NCH])
        rest_ready = sem(ctx, "rest_ready")
        rest_out = sem(ctx, "rest_out")
        dst_f = sb(ctx, "dst_f", [P, NCH])
        low = sb(ctx, "low", [P, NSG])
        nbase = sb(ctx, "nbase", [P, NSG])
        outside = sb(ctx, "outside", [P, NCH])
        anyout = sb(ctx, "anyout", [P, 1])
        anyall = sb(ctx, "anyall", [P, 1])
        edges_in = sem(ctx, "edges_in")
        weights_in = sem(ctx, "weights_in")
        cleared = sem(ctx, "cleared")
        made = sem(ctx, "made")
        low_ready = sem(ctx, "low_ready")
        base_ready = sem(ctx, "base_ready")
        step_done = sem(ctx, "setup_step")
        out_ready = sem(ctx, "out_ready")
        any_ready = sem(ctx, "any_ready")
        block = ctx.enter_context(nc.Block())

        @block.sync
        def _(sp):
            sp.dma_start(dst_t[:], io["dst"]).then_inc(edges_in, 16)
            sp.dma_start(src_t[:], io["src"]).then_inc(weights_in, 16)
            sp.dma_start(wq[:], io["mix_wq"]).then_inc(weights_in, 16)
            sp.dma_start(w1[:], io["mix_w1"]).then_inc(weights_in, 16)
            sp.dma_start(w2[:], io["mix_w2"]).then_inc(weights_in, 16)
            sp.dma_start(colb[:], io["mix_cols"]).then_inc(weights_in, 16)
            sp.dma_start(rows[:], io["mix_rows"]).then_inc(weights_in, 16)
            sp.wait_ge(weights_in, 96)
            sp.wait_ge(rest_ready, 1)
            sp.dma_start(io["rest_dram"], dst_rest[:]).then_inc(rest_out, 16)
            sp.wait_ge(rest_out, 16)

        @block.gpsimd
        def _(pool):
            pool.memset(ident[:], 0.0).then_inc(cleared, 1)
            pool.iota(iota_w[:], [[1, W]], base=0, channel_multiplier=0,
                      allow_small_or_imprecise_dtypes=True).then_inc(made, 1)
            pool.wait_ge(cleared, 1)
            pool.affine_select(out=ident[:], in_=ident[:], compare_op=ALU.not_equal, fill=1.0,
                               base=0, pattern=[[-1, P]], channel_multiplier=1).then_inc(made, 1)
            pool.wait_ge(low_ready, 1)
            pool.partition_all_reduce(nbase[:], low[:], P, RMAX).then_inc(base_ready, 1)
            pool.wait_ge(out_ready, 1)
            pool.partition_all_reduce(anyall[:], anyout[:], P, RMAX).then_inc(any_ready, 1)

        @block.vector
        def _(dve):
            step = Chain(dve, step_done, 0, None)
            nc.vector.memset(accT[:], 0.0).then_inc(made, 1)
            dve.wait_ge(edges_in, 16)
            step(nc.vector.tensor_copy(dst_f[:], dst_t[:]))
            step(nc.vector.tensor_reduce(low[:], dst_f[:].rearrange("p (s c) -> p s c", c=CPS), AX.X, ALU.min))
            nc.vector.tensor_scalar(low[:], low[:], -1.0, None, ALU.mult).then_inc(low_ready, 1)
            dve.wait_ge(base_ready, 1)
            step(nc.vector.memset(base_i[:, 0:LAG], 0))
            step(nc.vector.tensor_scalar(base_i[:, LAG:LAG + NSG], nbase[:], -1.0, None, ALU.mult))
            step(nc.vector.memset(dst_rel[:, NCH:NCH + LEAD * CPS], -1.0))
            step(nc.vector.tensor_tensor(dst_rel[:, 0:NCH].rearrange("p (s c) -> p s c", c=CPS),
                                         dst_f[:].rearrange("p (s c) -> p s c", c=CPS),
                                         nbase[:].rearrange("p (s o) -> p s o", o=1).to_broadcast([P, NSG, CPS]), ALU.add))
            step(nc.vector.tensor_scalar(outside[:], dst_f[:], float(N), None, ALU.is_lt))
            step(nc.vector.scalar_tensor_tensor(out=outside[:], in0=dst_rel[:, 0:NCH], scalar=float(W), in1=outside[:],
                                                op0=ALU.is_ge, op1=ALU.mult))
            nc.vector.tensor_reduce(anyout[:], outside[:], AX.X, ALU.max).then_inc(out_ready, 1)
            step(nc.vector.scalar_tensor_tensor(out=dst_rest[:], in0=dst_f[:], scalar=BIG, in1=outside[:],
                                                op0=ALU.add, op1=ALU.mult))
            nc.vector.tensor_scalar(dst_rest[:], dst_rest[:], -BIG, None, ALU.add).then_inc(rest_ready, 1)
            dve.wait_ge(any_ready, 1)
            step(nc.vector.tensor_copy(flag_i[:], anyall[:]))


def norm_phase(nc, io, sb, psum, sem, xnT, ident, xn_dram, qdiv, kvwo):
    U = NORM_U
    VE = P + 1
    with ExitStack() as ctx:
        wkv = sb(ctx, "wkv", [P, K2, 2 * D])
        wo = sb(ctx, "wo", [P, K2, D])
        bkv = sb(ctx, "bkv", [P, 2 * D])
        headm = sb(ctx, "headm", [P, P])
        xin = sb(ctx, "xin", [SUB, U, D])
        xnb = sb(ctx, "xnb", [SUB, U, D])
        xhl = sb(ctx, "xhl", [SUB, U, 2, D], F16)
        st = sb(ctx, "st", [SUB, U, 6])
        mv = sb(ctx, "mv", [SUB, U, 2])
        var = sb(ctx, "var", [SUB, U])
        rstd = sb(ctx, "rstd", [SUB, U])
        tmp = sb(ctx, "tmp", [SUB, U])
        xT = sb(ctx, "xT", [P, 2, K2, SUB])
        kb = sb(ctx, "kb", [SUB, 2, D])
        vx = sb(ctx, "vx", [SUB, 2, K2, VE])
        ek = sb(ctx, "ek", [SUB, 2, D])
        rk = sb(ctx, "rk", [SUB, 2, D])
        kphi = sb(ctx, "kphi", [SUB, 2, D])
        zero = sb(ctx, "zero", [SUB, VE])
        kvm = sb(ctx, "kvm", [P, K2, P])
        kvmT = sb(ctx, "kvmT", [P, K2, P])
        ksum = sb(ctx, "ksum", [P, K2])
        psT = psum(ctx, "psT", [P, 2, K2 * 256])
        psKV = psum(ctx, "psKV", [P, 2, 2 * D])
        psA = psum(ctx, "psA", [P, K2, 512])
        w_in = sem(ctx, "norm_w_in")
        x_in = [sem(ctx, f"x_in{j}") for j in range(U)]
        xn_out = [sem(ctx, f"xn_out{j}") for j in range(U)]
        zeroed = sem(ctx, "zeroed")
        nstep = sem(ctx, "nstep")
        stats_taken = sem(ctx, "nstep_stats_taken")
        xn_ready = sem(ctx, "xn_ready")
        high_ready = sem(ctx, "high_ready")
        low_ready = sem(ctx, "low_part_ready")
        xn_stored = sem(ctx, "xn_stored")
        t_ready = sem(ctx, "t_ready")
        xT_ready = sem(ctx, "xT_ready")
        xT_saved = sem(ctx, "xT_saved")
        kv_ready = sem(ctx, "kv_ready")
        kb_ready = sem(ctx, "kb_ready")
        vx_ready = sem(ctx, "vx_ready")
        ek_ready = sem(ctx, "ek_ready")
        rk_ready = sem(ctx, "rk_ready")
        kphi_ready = sem(ctx, "kphi_ready")
        acc_done = sem(ctx, "acc_done")
        sums_done = sem(ctx, "sums_done")
        kvm_ready = sem(ctx, "kvm_ready")
        kvmT_ps = sem(ctx, "kvmT_ps")
        kvmT_sb = sem(ctx, "kvmT_sb")
        kvwo_ps = sem(ctx, "kvwo_ps")
        fin = sem(ctx, "norm_fin")
        block = ctx.enter_context(nc.Block())
        ITERS = NSUB // U

        @block.sync
        def _(sp):
            sp.dma_start(wkv[:], io["mix_wkv"]).then_inc(w_in, 16)
            sp.dma_start(bkv[:], io["mix_bkv"]).then_inc(w_in, 16)
            sp.dma_start(wo[:], io["mix_wo"]).then_inc(w_in, 16)
            sp.dma_start(headm[:], io["headm"]).then_inc(w_in, 16)
            with sp.Fori(0, ITERS) as i:
                for j in range(U):
                    sp.wait_ge(xn_ready, PRE + i * U - U + j + 1)
                    sp.dma_start(xin[:, j, :], io["x"][bass.ds(i * (U * SUB) + j * SUB, SUB), :]).then_inc(x_in[j], 16)

        @block.gpsimd
        def _(pool):
            def save(i, j):
                pool.wait_ge(xT_ready, PRE + i * U + j + 1)
                pool.tensor_copy(xnT[:, :, bass.ds(i * (U * SUB) + j * SUB, SUB)], xT[:, j % 2, :, :]).then_inc(xT_saved, 1)

            with pool.Fori(0, ITERS) as i:
                for j in range(U):
                    pool.wait_ge(xn_ready, PRE + i * U + j + 1)
                    rows = bass.ds(i * (U * SUB) + j * SUB, SUB)
                    pool.dma_start(xn_dram[rows, :], xnb[:, j, :]).then_inc(xn_out[j], 16)
                    pool.wait_ge(high_ready, PRE + i * U + j + 1)
                    pool.tensor_tensor(xhl[:, j, 1, :], xnb[:, j, :], xhl[:, j, 0, :], ALU.subtract).then_inc(low_ready, 1)
                    pool.wait_ge(low_ready, i * U + j + 1)
                    pool.dma_start(io["table_dram"][rows, :], xhl[:, j, :, :].rearrange("p t d -> p (t d)")).then_inc(xn_out[j], 16)
                    if j:
                        save(i, j - 1)
                save(i, U - 1)
                for j in range(U):
                    pool.wait_ge(xn_out[j], i * 32 + 32)
                pool.sem_inc(xn_stored, 1)

        @block.vector
        def _(dve):
            dve.sem_inc(xn_ready, PRE)
            dve.sem_inc(xn_stored, PRE)
            dve.sem_inc(kb_ready, PRE)
            dve.sem_inc(vx_ready, PRE)
            dve.sem_inc(kphi_ready, PRE)
            nc.vector.memset(zero[:], 0.0).then_inc(zeroed, 1)
            nc.vector.memset(vx[:], 1.0).then_inc(zeroed, 1)
            nc.vector.memset(xnT[:, :, N:NPAD], 0.0).then_inc(zeroed, 1)
            dve.wait_ge(zeroed, 3)
            dve.wait_ge(w_in, 64)
            with dve.Fori(0, ITERS) as i:
                step = Chain(dve, nstep, i * (2 * U + 1 + RSQRT_STEPS), 2 * U + 1 + RSQRT_STEPS)
                for j in range(U):
                    dve.wait_ge(x_in[j], i * 16 + 16)
                    step.start(nc.vector.bn_stats(st[:, j, :], xin[:, j, :]))
                step.wait()
                dve.sem_inc(stats_taken, 1)
                for j in range(U):
                    step.start(nc.vector.bn_aggr(mv[:, j, :], st[:, j, :]))
                step.wait()
                step(nc.vector.tensor_scalar(var[:], mv[:, :, 1], EPS, None, ALU.add))
                rsqrt_steps(nc, step, var[:], rstd[:], tmp[:])
                step.end()
                for j in range(U + 2):
                    if j < U:
                        dve.wait_ge(xn_stored, PRE + i)
                        dve.wait_ge(t_ready, PRE + i * U + j + 1 - U)
                        nc.vector.tensor_scalar(xnb[:, j, :], xin[:, j, :], mv[:, j, 0:1], rstd[:, j:j + 1],
                                                ALU.subtract, ALU.mult).then_inc(xn_ready, 1)
                    if 1 <= j <= U:
                        a = j - 1
                        dve.wait_ge(kv_ready, PRE + i * U + a + 1)
                        dve.wait_ge(ek_ready, PRE + i * U + a + 1 - 2)
                        dve.wait_ge(rk_ready, PRE + i * U + a + 1 - 2)
                        nc.vector.tensor_tensor(kb[:, a % 2, :], psKV[0:SUB, a % 2, 0:D], bkv[0:SUB, 0:D],
                                                ALU.add).then_inc(kb_ready, 1)
                        dve.wait_ge(acc_done, PRE + i * U + a + 1 - 2)
                        nc.vector.tensor_tensor(vx[:, a % 2, :, 0:P],
                                                psKV[0:SUB, a % 2, D:2 * D].rearrange("p (h e) -> p h e", h=K2),
                                                bkv[0:SUB, D:2 * D].rearrange("p (h e) -> p h e", h=K2),
                                                ALU.add).then_inc(vx_ready, 1)
                    if j >= 2:
                        a = j - 2
                        dve.wait_ge(rk_ready, PRE + i * U + a + 1)
                        dve.wait_ge(acc_done, PRE + i * U + a + 1 - 2)
                        nc.vector.scalar_tensor_tensor(out=kphi[:, a % 2, :], in0=ek[:, a % 2, :], scalar=1.0,
                                                       in1=rk[:, a % 2, :], op0=ALU.min, op1=ALU.add
                                                       ).then_inc(kphi_ready, 1)
            dve.wait_ge(sums_done, 1)
            for h in range(K2):
                nc.vector.tensor_tensor(kvm[:, h, :], psA[:, h, 0:P], headm[:], ALU.mult).then_inc(kvm_ready, 1)
                nc.vector.tensor_copy(ksum[:, h:h + 1], psA[:, h, P:P + 1]).then_inc(kvm_ready, 1)
            dve.wait_ge(kvm_ready, 4)
            for h in range(K2):
                nc.vector.tensor_scalar(qdiv[:, h, :], headm[:], ksum[:, h:h + 1], None, ALU.mult).then_inc(fin, 1)
            dve.wait_ge(kvmT_ps, 1)
            nc.vector.tensor_copy(kvmT[:], psT[:, 0, 0:K2 * P].rearrange("p (h e) -> p h e", h=K2)).then_inc(kvmT_sb, 1)
            dve.wait_ge(kvwo_ps, 1)
            nc.vector.tensor_copy(kvwo[:], psKV[:, 0, :].rearrange("p (h e) -> p h e", h=K2)).then_inc(fin, 1)

        @block.scalar
        def _(act):
            act.sem_inc(xT_ready, PRE)
            act.sem_inc(high_ready, PRE)
            act.sem_inc(xT_saved, PRE)
            act.sem_inc(ek_ready, PRE)
            act.sem_inc(rk_ready, PRE)
            with act.Fori(0, ITERS) as i:
                for j in range(U + 1):
                    if j < U:
                        act.wait_ge(xn_ready, PRE + i * U + j + 1)
                        nc.scalar.copy(xhl[:, j, 0, :], xnb[:, j, :]).then_inc(high_ready, 1)
                        act.wait_ge(t_ready, PRE + i * U + j + 1)
                        act.wait_ge(xT_saved, PRE + i * U + j + 1 - 2)
                        act.wait_ge(kv_ready, PRE + i * U + j + 1 - 2)
                        nc.scalar.copy(xT[:, j % 2, :, :],
                                       psT[:, j % 2, 0:K2 * SUB].rearrange("p (k n) -> p k n", k=K2)).then_inc(xT_ready, 1)
                    if j >= 1:
                        a = j - 1
                        act.wait_ge(kb_ready, PRE + i * U + a + 1)
                        act.wait_ge(kphi_ready, PRE + i * U + a + 1 - 2)
                        nc.scalar.activation(ek[:, a % 2, :], kb[:, a % 2, :], ACT.Exp).then_inc(ek_ready, 1)
                        nc.scalar.activation(rk[:, a % 2, :], kb[:, a % 2, :], ACT.Relu).then_inc(rk_ready, 1)

        @block.tensor
        def _(pe):
            pe.sem_inc(t_ready, PRE)
            pe.sem_inc(kv_ready, PRE)
            pe.sem_inc(acc_done, PRE)
            pe.wait_ge(zeroed, 2)
            pe.wait_ge(w_in, 64)
            for h in range(K2):
                nc.tensor.matmul(psA[:, h, 0:VE], zero[:, 0:P], zero[:], start=True, stop=False)
            with pe.Fori(0, ITERS) as i:
                for j in range(U + 3):
                    if j < U:
                        pe.wait_ge(xn_ready, PRE + i * U + j + 1)
                        pe.wait_ge(xT_ready, PRE + i * U + j + 1 - 2)
                        for k in range(K2):
                            last = nc.tensor.transpose(psT[:, j % 2, k * SUB:(k + 1) * SUB],
                                                       xnb[:, j, k * P:(k + 1) * P], ident[0:SUB, 0:SUB])
                        last.then_inc(t_ready, 1)
                    if 1 <= j <= U:
                        a = j - 1
                        pe.wait_ge(xT_ready, PRE + i * U + a + 1)
                        pe.wait_ge(kb_ready, PRE + i * U + a + 1 - 2)
                        pe.wait_ge(vx_ready, PRE + i * U + a + 1 - 2)
                        for k in range(K2):
                            last = nc.tensor.matmul(psKV[0:SUB, a % 2, :], xT[:, a % 2, k, :], wkv[:, k, :],
                                                    start=(k == 0), stop=(k == K2 - 1))
                        last.then_inc(kv_ready, 1)
                    if j >= 3:
                        a = j - 3
                        pe.wait_ge(vx_ready, PRE + i * U + a + 1)
                        pe.wait_ge(kphi_ready, PRE + i * U + a + 1)
                        for h in range(K2):
                            last = nc.tensor.matmul(psA[:, h, 0:VE], kphi[:, a % 2, h * P:(h + 1) * P],
                                                    vx[:, a % 2, h, :], start=False, stop=False)
                        last.then_inc(acc_done, 1)
            for h in range(K2):
                last = nc.tensor.matmul(psA[:, h, 0:VE], zero[:, 0:P], zero[:], start=False, stop=True)
            last.then_inc(sums_done, 1)
            pe.wait_ge(kvm_ready, 4)
            for h in range(K2):
                last = nc.tensor.transpose(psT[:, 0, h * P:(h + 1) * P], kvm[:, h, :], ident[:])
            last.then_inc(kvmT_ps, 1)
            pe.wait_ge(kvmT_sb, 1)
            for h in range(K2):
                last = nc.tensor.matmul(psKV[:, 0, h * D:(h + 1) * D], kvmT[:, h, :], wo[:, h, :], start=True, stop=True)
            last.then_inc(kvwo_ps, 1)


BQ, G1, B1LN, B1 = 0, 2, 4, 6
R_BO, R_G1, R_G2, R_LN1B, R_B2, R_LN2B, R_BFC = range(7)

def mix_order(ns, first=False, last=False):
    pairs = ns // 2
    order = []
    spread = iter(range(SGI))

    def edges(count=1):
        for s in (next(spread) for _ in range(count)):
            order.extend([("ag", s), ("hot", s), ("add", s)])

    order.append(("wo", 0))
    edges()
    order.extend(("wo", p) for p in range(1, pairs))
    for p in range(pairs):
        order.append(("wo_sum", p))
    edges()
    order.append(("ln1", 0))
    edges()
    order.append(("ln1", 1))
    order.extend(("x1", p) for p in range(pairs))
    edges()
    order.extend(("t", p) for p in range(pairs))
    for m in range(FF // P):
        order.append(("w1", m))
        if m in (1, 2, 4, 6, 7):
            edges()
        if not first:
            order.extend({1: [("ln2", 0)], 2: [("ln2", 1)], 4: [("out", 0)], 6: [("out", 1)]}.get(m, []))
    order.append(("w2", 0))
    edges()
    if not last:
        order.append(("q", 0))
    order.append(("w2", 1))
    edges()
    order.append(("w2_sum", 0))
    if not last:
        order.extend([("qphi", 0), ("q", 1)])
    for j in range(2, ns):
        order.append(("w2", j))
        if not last:
            order.append(("den", 0) if j == 2 else ("den", 1))
            order.append(("qphi", 1) if j == 2 else ("divide", 0))
        edges()
    edges(GS - ns)
    order.extend(("w2_sum", p) for p in range(1, pairs))
    edges(1)
    if not last:
        order.append(("divide", 1))
    edges(1)
    edges(SGI - 15)
    return order


def mix_phase(nc, io, sb, psum, sem, xnT, accT, ident, src_t, dst_rel, base_i, iota_w,
              qdiv, kvwo, wq, w1, w2, colb, rows, xn_dram, s1_dram):
    F = 3
    NP = GS // 2
    NPG = 2 * NP
    FPG = 2 * K2 + FF // P
    with ExitStack() as ctx:
        ring = sb(ctx, "ring", [P, RING, CPS, 2 * D], F16)
        stage = sb(ctx, "stage", [P, 2, HALF * CPS], I32)
        oh = sb(ctx, "oh", [P, OH, CPS, W], F16)
        ea = sb(ctx, "ea", [P, K2, GN])
        eb = sb(ctx, "eb", [P, K2, GN])
        qphi = sb(ctx, "qphi", [P, K2, GN])
        xng = sb(ctx, "xng", [SUB, GS, D])
        xg = sb(ctx, "xg", [SUB, GS, D])
        ya = sb(ctx, "ya", [SUB, GS, D])
        yb = sb(ctx, "yb", [SUB, GS, D])
        x1T = sb(ctx, "x1T", [P, K2, GN])
        ffh = sb(ctx, "ffh", [P, FF // P, GN])
        st = sb(ctx, "st2", [SUB, 2, GS, 6])
        mv = sb(ctx, "mv2", [SUB, 2, GS, 2])
        var = sb(ctx, "var2", [SUB, 2, GS])
        rstd = sb(ctx, "rstd2", [SUB, 2, GS])
        tmp = sb(ctx, "tmp2", [SUB, 2, GS])
        psF = psum(ctx, "psF", [P, F, 512])
        psN = psum(ctx, "psN", [P, 2, 2, D])
        psX = psum(ctx, "psX", [P, K2, 2 * P])
        psG = psum(ctx, "psG", [P, 2, 512])
        mstep = sem(ctx, "mstep")
        late_step = sem(ctx, "late_step")
        stats_taken = sem(ctx, "mstep_stats_taken")
        rows_ready = sem(ctx, "rows_ready")
        bank_zeroed = sem(ctx, "bank_zeroed")
        staged = sem(ctx, "staged")
        slot_taken = sem(ctx, "slot_taken")
        gathered = [sem(ctx, f"gathered{r}") for r in range(RING)]
        oh_ready = sem(ctx, "oh_ready")
        ag_ready = sem(ctx, "ag_ready")
        ag_added = sem(ctx, "ag_added")
        xn_in = sem(ctx, "xn_in")
        x_in = sem(ctx, "x_in")
        xnT_out = sem(ctx, "xnT_out")
        s1_out = sem(ctx, "s1_out")
        s1_stored = sem(ctx, "s1_stored")
        f_ready = sem(ctx, "f_ready")
        f_saved = sem(ctx, "f_saved")
        qphi_ready = sem(ctx, "qphi_ready")
        divided = sem(ctx, "divided")
        qscaled = sem(ctx, "qscaled")
        n_ready = sem(ctx, "n_ready")
        n_saved = sem(ctx, "n_saved")
        x1_ready = sem(ctx, "x1_ready")
        x_t = sem(ctx, "x_t")
        x1T_ready = sem(ctx, "x1T_ready")
        s1_ready = sem(ctx, "s1_ready")
        block = ctx.enter_context(nc.Block())

        @block.sync
        def _(sp):
            def store(g, ns):
                sp.wait_ge(s1_ready, PRE + g * NP + ns // 2)
                sp.dma_start(s1_dram[bass.ds(g * GN, ns * SUB), :].rearrange("(j p) d -> p j d", p=SUB),
                             yb[:, 0:ns, :]).then_inc(s1_out, 16)
                sp.wait_ge(s1_out, g * 16 + 16)
                sp.sem_inc(s1_stored, 1)

            def body(g, ns, first=False):
                sp.wait_ge(n_saved, PRE + g * NPG - NP)
                sp.dma_start(xng[:, 0:ns, :], xn_dram[bass.ds(g * GN, ns * SUB), :].rearrange("(j p) d -> p j d", p=SUB)
                             ).then_inc(xn_in, 16)
                if not first:
                    store(g - 1, GS)
                sp.dma_start(xg[:, 0:ns, :], io["x"][bass.ds(g * GN, ns * SUB), :].rearrange("(j p) d -> p j d", p=SUB)
                             ).then_inc(x_in, 16)

            body(0, GS, first=True)
            sp.dma_start(io["xnT_dram"], xnT[:]).then_inc(xnT_out, 16)
            with sp.Fori(1, GROUPS) as g:
                body(g, GS)
            body(GROUPS, TAIL)
            store(GROUPS, TAIL)
            sp.wait_ge(xnT_out, 16)

        @block.gpsimd
        def _(pool):
            def body(g):
                for a in range(SGI // HALF):
                    pool.wait_ge(ag_ready, PRE + g * SGI + (a + 1) * HALF - SGI)
                    pool.tensor_copy(stage[:, a, :], src_t[:, bass.ds(g * (SGI * CPS) + a * (HALF * CPS), HALF * CPS)]
                                     ).then_inc(staged, 1)
                    pool.wait_ge(staged, g * (SGI // HALF) + a + 1)
                    for h in range(HALF):
                        s = a * HALF + h
                        r = s % RING
                        pool.wait_ge(ag_ready, PRE + g * SGI + s + 1 - RING)
                        pool.sem_inc(slot_taken, 1)
                        for c in range(CPS):
                            col = h * CPS + c
                            pool.indirect_dma_start(
                                out=ring[:, r, c, :], out_offset=None, in_=io["table_dram"][:, :],
                                in_offset=bass.IndirectOffsetOnAxis(ap=stage[:, a, col:col + 1], axis=0),
                            ).then_inc(gathered[r], 16)

            with pool.Fori(0, GROUPS) as g:
                body(g)
            body(GROUPS)

        @block.scalar
        def _(act):
            act.sem_inc(f_saved, PRE)
            act.sem_inc(x1T_ready, PRE)

            def queries(g, s):
                act.wait_ge(f_ready, PRE + g * FPG + s + 1)
                act.wait_ge(qscaled, PRE + g * K2 + s + 1 - K2)
                nc.scalar.activation(ea[:, s, :], psF[:, s % F, 0:GN], ACT.Exp, bias=colb[:, BQ + s:BQ + s + 1])
                nc.scalar.activation(eb[:, s, :], psF[:, s % F, 0:GN], ACT.Relu, bias=colb[:, BQ + s:BQ + s + 1]
                                     ).then_inc(f_saved, 1)

            def divisors(g, s):
                act.wait_ge(f_ready, PRE + g * FPG + K2 + s + 1)
                act.wait_ge(qphi_ready, PRE + g * K2 + s + 1)
                nc.scalar.activation(eb[:, s, :], psF[:, (K2 + s) % F, 0:GN], ACT.Copy, bias=1e-6).then_inc(f_saved, 1)

            for s in range(K2):
                queries(0, s)
            for s in range(K2):
                divisors(0, s)

            def body(g, ns, **place):
                n = ns * SUB
                for what, s in mix_order(ns, **place):
                    if what == "q":
                        queries(g + 1, s)
                    elif what == "den":
                        divisors(g + 1, s)
                    elif what == "t":
                        act.wait_ge(x_t, PRE + g * NP + s + 1)
                        act.wait_ge(f_ready, PRE + g * FPG)
                        for k in range(K2):
                            last = nc.scalar.activation(
                                x1T[:, k, s * (2 * SUB):(s + 1) * (2 * SUB)].rearrange("p (j n) -> p j n", j=2),
                                psX[:, k, :].rearrange("p (j n) -> p j n", j=2)[:, :, 0:SUB], ACT.Identity,
                                scale=colb[:, G1 + k:G1 + k + 1], bias=colb[:, B1LN + k:B1LN + k + 1])
                        last.then_inc(x1T_ready, 1)
                    elif what == "w1":
                        act.wait_ge(f_ready, PRE + g * FPG + 2 * K2 + s + 1)
                        if s == 0:
                            act.wait_ge(n_ready, PRE + g * NPG)
                        nc.scalar.activation(ffh[:, s, 0:n], psF[:, (2 * K2 + s) % F, 0:n], ACT.Relu,
                                             bias=colb[:, B1 + s:B1 + s + 1]).then_inc(f_saved, 1)

            body(0, GS, first=True)
            with act.Fori(1, GROUPS) as g:
                body(g, GS)
            body(GROUPS, TAIL, last=True)

        @block.vector
        def _(dve):
            dve.sem_inc(ag_added, PRE)
            dve.sem_inc(oh_ready, PRE)
            dve.sem_inc(qphi_ready, PRE)
            dve.sem_inc(qscaled, PRE)
            dve.sem_inc(n_saved, PRE)
            dve.sem_inc(x1_ready, PRE)
            dve.sem_inc(s1_stored, PRE)
            dve.sem_inc(s1_ready, PRE)
            nc.vector.tensor_tensor(rows[:, R_LN1B, :], rows[:, R_LN1B, :], rows[:, R_B2, :], ALU.add).then_inc(rows_ready, 1)
            nc.vector.tensor_tensor(rows[:, R_LN2B, :], rows[:, R_LN2B, :], rows[:, R_BFC, :], ALU.add).then_inc(rows_ready, 1)
            dve.wait_ge(rows_ready, 2)

            def pair(t, p):
                return t[:, 2 * p:2 * p + 2, :]

            def row(r):
                return rows[0:SUB, r:r + 1, :].to_broadcast([SUB, 2, D])

            def norm(step, which, ns, part):
                v, y, t = var[:, which, 0:ns], rstd[:, which, 0:ns], tmp[:, which, 0:ns]
                if part == 0:
                    dve.sem_inc(stats_taken, 1)
                    for j in range(ns):
                        step.start(nc.vector.bn_aggr(mv[:, which, j, :], st[:, which, j, :]))
                    step.wait()
                    step(nc.vector.tensor_scalar(v, mv[:, which, 0:ns, 1], EPS, None, ALU.add))
                    rsqrt_guess(nc, step, v, y, t)
                    rsqrt_newton(nc, step, v, y, t, 1)
                else:
                    rsqrt_newton(nc, step, v, y, t, 2)

            def out(step, g, s):
                for j in (2 * s, 2 * s + 1):
                    step.start(nc.vector.tensor_scalar(yb[:, j, :], yb[:, j, :], mv[:, 1, j, 0:1], rstd[:, 1, j:j + 1],
                                                       ALU.subtract, ALU.mult))
                step.wait()
                step(nc.vector.tensor_tensor(pair(yb, s), pair(yb, s), row(R_G2), ALU.mult))
                step(nc.vector.tensor_tensor(pair(yb, s), pair(yb, s), row(R_LN2B), ALU.add))
                dve.wait_ge(x_in, g * 16 + 16)
                nc.vector.tensor_tensor(pair(yb, s), pair(yb, s), pair(xg, s), ALU.add).then_inc(s1_ready, 1)

            def one_hot(sg, slot):
                dve.wait_ge(ag_ready, PRE + sg + 1 - OH)
                nc.vector.tensor_tensor(
                    oh[:, slot, :, :],
                    dst_rel[:, bass.ds(sg * CPS, CPS)].rearrange("p (c o) -> p c o", o=1).to_broadcast([P, CPS, W]),
                    iota_w[:].rearrange("p (o w) -> p o w", o=1).to_broadcast([P, CPS, W]),
                    ALU.is_equal).then_inc(oh_ready, 1)

            def add_window(turn, bank):
                base = dve.value_load(base_i[0:1, bass.ds(turn, 1)], min_val=0, max_val=N - 1)
                dve.wait_ge(ag_ready, PRE + turn + 1 - LAG)
                dve.wait_ge(ag_added, PRE + turn)
                win = accT[:, :, bass.ds(base, W)]
                nc.vector.tensor_tensor(win, win, psG[:, bank, 0:K2 * W].rearrange("p (k w) -> p k w", k=K2),
                                        ALU.add).then_inc(ag_added, 1)

            def divide(g, s):
                dve.wait_ge(f_saved, PRE + g * FPG + K2 + s + 1)
                nc.vector.reciprocal(ea[:, s, :], eb[:, s, :]).then_inc(divided, 1)
                dve.wait_ge(divided, g * K2 + s + 1)
                nc.vector.tensor_tensor(qphi[:, s, :], qphi[:, s, :], ea[:, s, :], ALU.mult).then_inc(qscaled, 1)

            def queries(g, s):
                dve.wait_ge(f_saved, PRE + g * FPG + s + 1)
                dve.wait_ge(n_ready, PRE + g * NPG - NP)
                nc.vector.scalar_tensor_tensor(out=qphi[:, s, :], in0=ea[:, s, :], scalar=1.0, in1=eb[:, s, :],
                                               op0=ALU.min, op1=ALU.add).then_inc(qphi_ready, 1)

            nc.vector.memset(psG[:, LAG, :], 0.0).then_inc(bank_zeroed, 1)
            dve.wait_ge(bank_zeroed, 1)
            for s in range(LEAD):
                one_hot(s, s)
            for s in range(K2):
                queries(0, s)
            for s in range(K2):
                divide(0, s)

            def body(g, ns, **place):
                step = Chain(dve, mstep, g * PER, None if "last" in place else PER)
                late = Chain(dve, late_step, (g - 1) * PER_LATE, PER_LATE)
                for what, s in mix_order(ns, **place):
                    if what == "hot":
                        one_hot(g * SGI + s + LEAD, (s + LEAD) % OH)
                    elif what == "add":
                        add_window(g * SGI + s, (s - LAG) % 2)
                    elif what == "qphi":
                        queries(g + 1, s)
                    elif what == "divide":
                        divide(g + 1, s)
                    elif what == "wo_sum":
                        dve.wait_ge(xn_in, g * 16 + 16)
                        dve.wait_ge(n_ready, PRE + g * NPG + s + 1)
                        dve.wait_ge(x_t, PRE + g * NP)
                        nc.vector.tensor_tensor(pair(ya, s), psN[0:SUB, s % 2, :, :], pair(xng, s), ALU.add).then_inc(n_saved, 1)
                        dve.wait_ge(n_saved, PRE + g * NPG + s + 1)
                        step(nc.vector.tensor_tensor(pair(ya, s), pair(ya, s), row(R_BO), ALU.add))
                        for j in (2 * s, 2 * s + 1):
                            step.start(nc.vector.bn_stats(st[:, 0, j, :], ya[:, j, :]))
                        step.wait()
                    elif what == "ln1":
                        norm(step, 0, ns, s)
                    elif what == "x1":
                        for j in (2 * s, 2 * s + 1):
                            last = nc.vector.tensor_scalar(ya[:, j, :], ya[:, j, :], mv[:, 0, j, 0:1], rstd[:, 0, j:j + 1],
                                                           ALU.subtract, ALU.mult)
                        last.then_inc(x1_ready, 1)
                    elif what == "w2_sum":
                        dve.wait_ge(x1_ready, PRE + g * NP + s + 1)
                        dve.wait_ge(s1_stored, PRE + g)
                        step(nc.vector.tensor_tensor(pair(yb, s), pair(ya, s), row(R_G1), ALU.mult))
                        step(nc.vector.tensor_tensor(pair(yb, s), pair(yb, s), row(R_LN1B), ALU.add))
                        dve.wait_ge(n_ready, PRE + g * NPG + ns // 2 + s + 1)
                        nc.vector.tensor_tensor(pair(yb, s), pair(yb, s), psN[0:SUB, (ns // 2 + s) % 2, :, :], ALU.add
                                                ).then_inc(n_saved, 1)
                        dve.wait_ge(n_saved, PRE + g * NPG + ns // 2 + s + 1)
                        for j in (2 * s, 2 * s + 1):
                            step.start(nc.vector.bn_stats(st[:, 1, j, :], yb[:, j, :]))
                        step.wait()
                    elif what == "ln2":
                        norm(late, 1, GS, s)
                    elif what == "out":
                        out(late, g - 1, s)
                step.end()
                if "first" not in place:
                    late.end()

            PER = (NP + GS) + (GS + 1 + RSQRT_STEPS) + (2 * NP + GS)
            PER_LATE = (GS + 1 + RSQRT_STEPS) + (2 * NP + GS)
            body(0, GS, first=True)
            with dve.Fori(1, GROUPS) as g:
                body(g, GS)
            body(GROUPS, TAIL, last=True)
            for turn in range(NSG, NSG + LAG):
                add_window(turn, (turn - LAG) % 2)
            late = Chain(dve, late_step, GROUPS * PER_LATE, None)
            for part in range(2):
                norm(late, 1, TAIL, part)
            for s in range(TAIL // 2):
                out(late, GROUPS, s)

        @block.tensor
        def _(pe):
            pe.sem_inc(f_ready, PRE)
            pe.sem_inc(n_ready, PRE)
            pe.sem_inc(x_t, PRE)
            pe.sem_inc(ag_ready, PRE)

            def queries(g, s):
                pe.wait_ge(f_saved, PRE + g * FPG + s + 1 - F)
                for k in range(K2):
                    last = nc.tensor.matmul(psF[:, s % F, 0:GN], wq[:, k, s * P:(s + 1) * P],
                                            xnT[:, k, bass.ds(g * GN, GN)], start=(k == 0), stop=(k == K2 - 1))
                last.then_inc(f_ready, 1)

            def divisors(g, s):
                pe.wait_ge(f_saved, PRE + g * FPG + K2 + s + 1 - F)
                pe.wait_ge(qphi_ready, PRE + g * K2 + s + 1)
                nc.tensor.matmul(psF[:, (K2 + s) % F, 0:GN], qdiv[:, s, :], qphi[:, s, :],
                                 start=True, stop=True).then_inc(f_ready, 1)

            for s in range(K2):
                queries(0, s)
            for s in range(K2):
                divisors(0, s)

            def body(g, ns, **place):
                n = ns * SUB
                for what, s in mix_order(ns, **place):
                    if what == "q":
                        queries(g + 1, s)
                    elif what == "den":
                        divisors(g + 1, s)
                    elif what == "wo":
                        pe.wait_ge(qscaled, PRE + g * K2 + K2)
                        pe.wait_ge(n_saved, PRE + g * NPG + s + 1 - 2)
                        for j in range(2):
                            for k in range(K2):
                                cut = (2 * s + j) * SUB
                                last = nc.tensor.matmul(psN[0:SUB, s % 2, j, :], qphi[:, k, cut:cut + SUB], kvwo[:, k, :],
                                                        start=(k == 0), stop=(k == K2 - 1))
                        last.then_inc(n_ready, 1)
                    elif what == "t":
                        pe.wait_ge(x1_ready, PRE + g * NP + s + 1)
                        pe.wait_ge(x1T_ready, PRE + g * NP + s)
                        for j in range(2):
                            for k in range(K2):
                                last = nc.tensor.transpose(psX[:, k, j * P:j * P + SUB], ya[:, 2 * s + j, k * P:(k + 1) * P],
                                                           ident[0:SUB, 0:SUB])
                        last.then_inc(x_t, 1)
                    elif what == "w1":
                        pe.wait_ge(x1T_ready, PRE + g * NP + ns // 2)
                        pe.wait_ge(f_saved, PRE + g * FPG + 2 * K2 + s + 1 - F)
                        for k in range(K2):
                            last = nc.tensor.matmul(psF[:, (2 * K2 + s) % F, 0:n], w1[:, k, s * P:(s + 1) * P], x1T[:, k, 0:n],
                                                    start=(k == 0), stop=(k == K2 - 1))
                        last.then_inc(f_ready, 1)
                    elif what == "w2":
                        p = s // 2
                        if s % 2 == 0:
                            pe.wait_ge(f_saved, PRE + g * FPG + FPG)
                            pe.wait_ge(n_saved, PRE + g * NPG + ns // 2 + p + 1 - 2)
                        for k in range(FF // P):
                            last = nc.tensor.matmul(psN[0:SUB, (ns // 2 + p) % 2, s % 2, :], ffh[:, k, s * SUB:(s + 1) * SUB],
                                                    w2[:, k, :], start=(k == 0), stop=(k == FF // P - 1))
                        if s % 2:
                            last.then_inc(n_ready, 1)
                    elif what == "ag":
                        pe.wait_ge(oh_ready, PRE + g * SGI + s + 1)
                        pe.wait_ge(ag_added, PRE + g * SGI + s + LAG - 1)
                        pe.wait_ge(gathered[s % RING], (g * (SGI // RING) + s // RING + 1) * (16 * CPS))
                        for k in range(K2):
                            for c in range(CPS):
                                for part in range(2):
                                    cut = part * D + k * P
                                    last = nc.tensor.matmul(psG[:, s % 2, k * W:(k + 1) * W], ring[:, s % RING, c, cut:cut + P],
                                                            oh[:, s % OH, c, :], start=(c + part == 0), stop=(c + part == CPS))
                        last.then_inc(ag_ready, 1)

            body(0, GS, first=True)
            with pe.Fori(1, GROUPS) as g:
                body(g, GS)
            body(GROUPS, TAIL, last=True)


def rest_phase(nc, io, sb, psum, sem, accT, ident, src_t, iota_w, flag_i, xn_dram):
    WINS = -(-N // W)
    with ExitStack() as ctx:
        dst_rest = sb(ctx, "rest_dst", [P, NCH])
        rows4 = sb(ctx, "rest_rows", [P, CPS, 2 * D], F16)
        dst_in = sem(ctx, "rest_dst_in")
        idx = sb(ctx, "rest_idx", [P, CPS], I32)
        rel = sb(ctx, "rest_rel", [P, CPS])
        hot = sb(ctx, "rest_hot", [P, CPS, W], F16)
        psR = psum(ctx, "psR", [P, K2, W])
        idx_ready = sem(ctx, "r_idx_ready")
        rest_in = sem(ctx, "rest_in")
        rest_begun = sem(ctx, "rest_begun")
        rel_ready = sem(ctx, "rel_ready")
        hot_ready = sem(ctx, "hot_ready")
        r_summed = sem(ctx, "r_summed")
        r_added = sem(ctx, "r_added")
        block = ctx.enter_context(nc.Block())

        def some(eng):
            return eng.If(eng.value_load(flag_i[0:1, 0:1], min_val=0, max_val=1))

        @block.gpsimd
        def _(pool):
            with some(pool):
                with pool.Fori(0, NSG) as s:
                    pool.wait_ge(r_added, PRE + s * WINS)
                    pool.tensor_copy(idx[:], src_t[:, bass.ds(s * CPS, CPS)]).then_inc(idx_ready, 1)
                    pool.wait_ge(idx_ready, s + 1)
                    pool.sem_inc(rest_begun, 1)
                    for c in range(CPS):
                        pool.indirect_dma_start(out=rows4[:, c, :], out_offset=None, in_=io["table_dram"][:, :],
                                                in_offset=bass.IndirectOffsetOnAxis(ap=idx[:, c:c + 1], axis=0),
                                                ).then_inc(rest_in, 16)
                    pool.wait_ge(rest_in, (s + 1) * (16 * CPS))

        @block.sync
        def _(sp):
            sp.dma_start(dst_rest[:], io["rest_dram"]).then_inc(dst_in, 16)
            sp.wait_ge(dst_in, 16)

        @block.vector
        def _(dve):
            dve.wait_ge(dst_in, 16)
            dve.sem_inc(r_added, PRE)
            with some(dve):
                with dve.Fori(0, NSG) as s:
                    nc.vector.tensor_copy(rel[:], dst_rest[:, bass.ds(s * CPS, CPS)]).then_inc(rel_ready, 1)
                    with dve.Fori(0, WINS) as w:
                        dve.wait_ge(rel_ready, s * (WINS + 1) + w + 1)
                        nc.vector.tensor_tensor(hot[:], rel[:].rearrange("p (c o) -> p c o", o=1).to_broadcast([P, CPS, W]),
                                                iota_w[:].rearrange("p (o w) -> p o w", o=1).to_broadcast([P, CPS, W]),
                                                ALU.is_equal).then_inc(hot_ready, 1)
                        dve.wait_ge(hot_ready, s * WINS + w + 1)
                        nc.vector.tensor_scalar(rel[:], rel[:], -float(W), None, ALU.add).then_inc(rel_ready, 1)
                        dve.wait_ge(r_summed, s * WINS + w + 1)
                        win = accT[:, :, bass.ds(w * W, W)]
                        nc.vector.tensor_tensor(win, win, psR[:], ALU.add).then_inc(r_added, 1)
                        dve.wait_ge(r_added, PRE + s * WINS + w + 1)

        @block.tensor
        def _(pe):
            with some(pe):
                with pe.Fori(0, NSG) as s:
                    with pe.Fori(0, WINS) as w:
                        pe.wait_ge(rest_in, (s + 1) * (16 * CPS))
                        pe.wait_ge(hot_ready, s * WINS + w + 1)
                        pe.wait_ge(r_added, PRE + s * WINS + w)
                        for k in range(K2):
                            for c in range(CPS):
                                for part in range(2):
                                    cut = part * D + k * P
                                    last = nc.tensor.matmul(psR[:, k, :], rows4[:, c, cut:cut + P], hot[:, c, :],
                                                            start=(c + part == 0), stop=(c + part == CPS))
                        last.then_inc(r_summed, 1)


def split_weights(nc, io, sb, psum, sem, w_rel, w_root, w_ih):
    with ExitStack() as ctx:
        pieces = [(f"raw_rel{k}", io["w_rel"][:, k, :], w_rel, k) for k in range(K2)]
        pieces += [(f"raw_root{k}", io["w_root"][:, k, :], w_root, k) for k in range(K2)]
        pieces += [(f"raw_ih{k}", io["w_ih"][:, k, :], w_ih, k) for k in range(DH // P)]
        raw = [sb(ctx, name, [P, src.shape[-1]]) for name, src, _, _ in pieces]
        raw_in = [sem(ctx, f"{name}_in") for name, _, _, _ in pieces]
        high_ready = sem(ctx, "w_high_ready")
        block = ctx.enter_context(nc.Block())

        @block.sync
        def _(sp):
            for n, (_, src, _, _) in enumerate(pieces):
                sp.dma_start(raw[n][:], src).then_inc(raw_in[n], 16)

        @block.scalar
        def _(act):
            for n, (_, _, dst, k) in enumerate(pieces):
                act.wait_ge(raw_in[n], 16)
                nc.scalar.copy(dst[:, 0, k, :], raw[n][:]).then_inc(high_ready, 1)

        @block.vector
        def _(dve):
            for n, (_, _, dst, k) in enumerate(pieces):
                dve.wait_ge(raw_in[n], 16)
                dve.wait_ge(high_ready, n + 1)
                nc.vector.tensor_tensor(dst[:, 1, k, :], raw[n][:], dst[:, 0, k, :].bitcast(F32), ALU.subtract)


PARTS = ((0, 0), (0, 1), (1, 0))


def gnn_phase(nc, io, sb, psum, sem, accT, ident, zsum, z_mv, w_rel, w_root, w_ih, s1_dram, x2_dram):
    F = 4
    NP = GS // 2
    HM = DH // P
    GATES = 3
    FPG = HM + GATES * HM
    with ExitStack() as ctx:
        w_fc = sb(ctx, "w_fc", [P, HM, D])
        cols = sb(ctx, "gnn_cols", [P, HM + 2 * GATES * HM])
        xnt = sb(ctx, "xn_tile", [P, K2, GN])
        acc_s = sb(ctx, "acc_split", [P, 2, K2, GN], F32R)
        xn_s = sb(ctx, "xn_split", [P, 2, K2, GN], F32R)
        hx = sb(ctx, "hx", [P, 2, GN])
        h_s = sb(ctx, "h_split", [P, 2, HM, GN], F32R)
        gi = sb(ctx, "gi", [P, 2, GN])
        gg = sb(ctx, "gg", [P, 2, GN])
        go = sb(ctx, "go", [P, 2, GN])
        hl = sb(ctx, "hl", [P, HM, GN])
        s1g = sb(ctx, "s1g", [SUB, GS, D])
        x2 = sb(ctx, "x2", [SUB, GS, D])
        zz = sb(ctx, "zz", [SUB, GS, D])
        st = sb(ctx, "st3", [SUB, GS, 6])
        mv = sb(ctx, "mv3", [SUB, GS, 2])
        var = sb(ctx, "var3", [SUB, GS])
        rstd = sb(ctx, "rstd3", [SUB, GS])
        tmp = sb(ctx, "tmp3", [SUB, GS])
        psF = psum(ctx, "psF3", [P, F, 512])
        psN = psum(ctx, "psN3", [P, 2, 2, D])
        psX = psum(ctx, "psX3", [P, 2, K2, 2 * P])
        gw_in = sem(ctx, "gnn_w_in")
        bias_ready = sem(ctx, "bias_ready")
        gstep = sem(ctx, "gstep")
        late_step = sem(ctx, "gnn_late_step")
        stats_taken = sem(ctx, "gstep_stats_taken")
        xn_in = sem(ctx, "xn_tile_in")
        s1_in = sem(ctx, "s1_in")
        x2_out = sem(ctx, "x2_out")
        x2_stored = sem(ctx, "x2_stored")
        high_ready = sem(ctx, "in_high_ready")
        split_ready = sem(ctx, "split_ready")
        f_ready = sem(ctx, "gf_ready")
        f_saved = sem(ctx, "gf_saved")
        h_high = sem(ctx, "h_high")
        h_ready = sem(ctx, "h_ready")
        c_ready = sem(ctx, "c_ready")
        tc_ready = sem(ctx, "tc_ready")
        hl_ready = sem(ctx, "hl_ready")
        fc_ready = sem(ctx, "fc_ready")
        x2_ready = sem(ctx, "x2_ready")
        z_ready = sem(ctx, "z_ready")
        z_t = sem(ctx, "z_t")
        zT_saved = sem(ctx, "zT_saved")
        block = ctx.enter_context(nc.Block())

        def order(ns, first=False, last=False):
            late = {} if first else {-1: [("ln", 0), ("ln", 1), ("z", 0), ("z", 1)], 0: [("t", 0)], 1: [("t", 1), ("zsum", 0)],
                                     2: [("zsum", 1)]}
            out = late.get(-1, [])
            for m in range(HM + 1):
                if m < HM:
                    out = out + [("gate", (m, x)) for x in range(GATES)] + [("cell", m)]
                if m:
                    out = out + [("tanh", m - 1)]
                out = out + late.get(m, [])
                if m == 1 and not last:
                    out = out + [("split", 0)]
            if not last:
                for m in range(HM):
                    out = out + [("h", m), ("h_split", m)]
            return out + [(what, p) for p in range(ns // 2) for what in ("fc", "x2")]

        @block.sync
        def _(sp):
            sp.dma_start(cols[:], io["gnn_cols"]).then_inc(gw_in, 16)
            sp.dma_start(w_fc[:], io["w_fc"]).then_inc(gw_in, 16)

            def load_xn(g):
                sp.dma_start(xnt[:], io["xnT_dram"][:, :, bass.ds(g * GN, GN)]).then_inc(xn_in, 16)

            def body(g, ns, last=False):
                if not last:
                    sp.wait_ge(split_ready, PRE + g + 1)
                    load_xn(g + 1)
                sp.wait_ge(x2_ready, PRE + g * NP)
                sp.dma_start(s1g[:, 0:ns, :], s1_dram[bass.ds(g * GN, ns * SUB), :].rearrange("(j p) d -> p j d", p=SUB)
                             ).then_inc(s1_in, 16)
                sp.wait_ge(x2_ready, PRE + g * NP + ns // 2)
                sp.dma_start(x2_dram[bass.ds(g * GN, ns * SUB), :].rearrange("(j p) d -> p j d", p=SUB), x2[:, 0:ns, :]
                             ).then_inc(x2_out, 16)
                sp.wait_ge(x2_out, g * 16 + 16)
                sp.sem_inc(x2_stored, 1)

            load_xn(0)
            with sp.Fori(0, GROUPS) as g:
                body(g, GS)
            body(GROUPS, TAIL, last=True)

        @block.scalar
        def _(act):
            act.sem_inc(f_saved, PRE)
            act.sem_inc(tc_ready, PRE)
            act.sem_inc(zT_saved, PRE)
            act.wait_ge(bias_ready, 1)

            def hidden(g, m):
                act.wait_ge(f_ready, PRE + g * FPG + m + 1)
                act.wait_ge(h_ready, PRE + g * HM + m + 1 - 2)
                nc.scalar.activation(hx[:, m % 2, :], psF[:, m % F, 0:GN], ACT.Relu, bias=cols[:, m:m + 1]
                                     ).then_inc(f_saved, 1)

            def save_z(g, s):
                act.wait_ge(z_t, PRE + g * NP + s + 1)
                for k in range(K2):
                    last = nc.scalar.copy(
                        accT[:, k, bass.ds(g * GN + s * (2 * SUB), 2 * SUB)].rearrange("p (j n) -> p j n", j=2),
                        psX[:, s % 2, k, :].rearrange("p (j n) -> p j n", j=2)[:, :, 0:SUB])
                last.then_inc(zT_saved, 1)

            def body(g, ns, **place):
                n = ns * SUB
                for what, s in order(ns, **place):
                    if what == "h":
                        hidden(g + 1, s)
                    elif what == "gate":
                        m, x = s
                        pos = HM + GATES * m + x
                        act.wait_ge(f_ready, PRE + g * FPG + pos + 1)
                        act.wait_ge(hl_ready, PRE + g * HM + m + 1 - 2)
                        dst = (gi, gg, go)[x]
                        nc.scalar.activation(dst[:, m % 2, 0:n], psF[:, pos % F, 0:n], (ACT.Sigmoid, ACT.Tanh, ACT.Sigmoid)[x],
                                             bias=cols[:, HM + x * HM + m:HM + x * HM + m + 1]).then_inc(f_saved, 1)
                    elif what == "tanh":
                        act.wait_ge(c_ready, PRE + g * HM + s + 1)
                        nc.scalar.activation(gi[:, s % 2, 0:n], gi[:, s % 2, 0:n], ACT.Tanh).then_inc(tc_ready, 1)
                    elif what == "t":
                        save_z(g - 1, s)

            for m in range(HM):
                hidden(0, m)
            body(0, GS, first=True)
            with act.Fori(1, GROUPS) as g:
                body(g, GS)
            body(GROUPS, TAIL, last=True)
            for s in range(TAIL // 2):
                save_z(GROUPS, s)

        @block.vector
        def _(dve):
            dve.sem_inc(c_ready, PRE)
            dve.sem_inc(hl_ready, PRE)
            dve.sem_inc(x2_ready, PRE)
            dve.sem_inc(x2_stored, PRE)
            dve.sem_inc(z_ready, PRE)
            dve.sem_inc(split_ready, PRE)
            dve.sem_inc(h_ready, PRE)
            PER = GS
            PER_LATE = GS + 1 + RSQRT_STEPS
            dve.wait_ge(gw_in, 32)
            nc.vector.tensor_tensor(cols[:, HM:HM + GATES * HM], cols[:, HM:HM + GATES * HM],
                                    cols[:, HM + GATES * HM:HM + 2 * GATES * HM], ALU.add).then_inc(bias_ready, 1)

            def split_inputs(g):
                sums = accT[:, :, bass.ds(g * GN, GN)]
                dve.wait_ge(xn_in, g * 16 + 16)
                dve.wait_ge(f_ready, PRE + (g - 1) * FPG + HM)
                nc.vector.tensor_copy(acc_s[:, 0, :, :], sums).then_inc(high_ready, 1)
                nc.vector.tensor_copy(xn_s[:, 0, :, :], xnt[:]).then_inc(high_ready, 1)
                dve.wait_ge(high_ready, g * 2 + 1)
                nc.vector.tensor_tensor(acc_s[:, 1, :, :], sums, acc_s[:, 0, :, :].bitcast(F32), ALU.subtract)
                dve.wait_ge(high_ready, g * 2 + 2)
                nc.vector.tensor_tensor(xn_s[:, 1, :, :], xnt[:], xn_s[:, 0, :, :].bitcast(F32), ALU.subtract
                                        ).then_inc(split_ready, 1)

            def split_hidden(g, m):
                dve.wait_ge(f_saved, PRE + g * FPG + m + 1)
                nc.vector.tensor_copy(h_s[:, 0, m, :], hx[:, m % 2, :]).then_inc(h_high, 1)
                dve.wait_ge(h_high, g * HM + m + 1)
                nc.vector.tensor_tensor(h_s[:, 1, m, :], hx[:, m % 2, :], h_s[:, 0, m, :].bitcast(F32), ALU.subtract
                                        ).then_inc(h_ready, 1)

            def norm(step, g, ns, part):
                v, y, t = var[:, 0:ns], rstd[:, 0:ns], tmp[:, 0:ns]
                if part == 0:
                    for j in range(ns):
                        step.start(nc.vector.bn_aggr(mv[:, j, :], st[:, j, :]))
                    step.wait()
                    step(nc.vector.tensor_scalar(v, mv[:, 0:ns, 1], EPS, None, ALU.add))
                    rsqrt_guess(nc, step, v, y, t)
                    rsqrt_newton(nc, step, v, y, t, 1)
                else:
                    rsqrt_newton(nc, step, v, y, t, 2)
                    nc.vector.tensor_copy(z_mv[:, bass.ds(g * GS, ns), 0], mv[:, 0:ns, 0])
                    nc.vector.tensor_copy(z_mv[:, bass.ds(g * GS, ns), 1], y)

            def make_z(g, s):
                dve.wait_ge(z_t, PRE + g * NP)
                for j in (2 * s, 2 * s + 1):
                    last = nc.vector.tensor_scalar(zz[:, j, :], x2[:, j, :], mv[:, j, 0:1], rstd[:, j:j + 1],
                                                   ALU.subtract, ALU.mult)
                last.then_inc(z_ready, 1)

            def sum_z(g, s):
                dve.wait_ge(zT_saved, PRE + g * NP + s + 1)
                nc.vector.tensor_reduce(zsum[:, :, bass.ds(g * NP + s, 1)].rearrange("p k o -> p (k o)"),
                                        accT[:, :, bass.ds(g * GN + s * (2 * SUB), 2 * SUB)], AX.X, ALU.add)

            def body(g, ns, **place):
                n = ns * SUB
                step = Chain(dve, gstep, g * PER, None if "last" in place else PER)
                late = Chain(dve, late_step, (g - 1) * PER_LATE, None if "first" in place else PER_LATE)
                for what, s in order(ns, **place):
                    if what == "split":
                        split_inputs(g + 1)
                    elif what == "h_split":
                        split_hidden(g + 1, s)
                    elif what == "cell":
                        dve.wait_ge(f_saved, PRE + g * FPG + HM + GATES * s + 2)
                        nc.vector.tensor_tensor(gi[:, s % 2, 0:n], gi[:, s % 2, 0:n], gg[:, s % 2, 0:n],
                                                ALU.mult).then_inc(c_ready, 1)
                    elif what == "tanh":
                        dve.wait_ge(f_saved, PRE + g * FPG + HM + GATES * s + 3)
                        dve.wait_ge(tc_ready, PRE + g * HM + s + 1)
                        dve.wait_ge(fc_ready, PRE + g * NP)
                        nc.vector.tensor_tensor(hl[:, s, 0:n], go[:, s % 2, 0:n], gi[:, s % 2, 0:n],
                                                ALU.mult).then_inc(hl_ready, 1)
                    elif what == "x2":
                        if s == 0:
                            dve.wait_ge(s1_in, g * 16 + 16)
                            dve.wait_ge(x2_stored, PRE + g)
                        dve.wait_ge(fc_ready, PRE + g * NP + s + 1)
                        nc.vector.tensor_tensor(x2[:, 2 * s:2 * s + 2, :], psN[0:SUB, s % 2, :, :], s1g[:, 2 * s:2 * s + 2, :],
                                                ALU.add).then_inc(x2_ready, 1)
                        dve.wait_ge(x2_ready, PRE + g * NP + s + 1)
                        for j in (2 * s, 2 * s + 1):
                            step.start(nc.vector.bn_stats(st[:, j, :], x2[:, j, :]))
                    elif what == "ln":
                        norm(late, g - 1, GS, s)
                    elif what == "z":
                        make_z(g - 1, s)
                    elif what == "zsum":
                        sum_z(g - 1, s)
                step.wait()
                dve.sem_inc(stats_taken, 1)
                step.end()
                if "first" not in place:
                    late.end()

            split_inputs(0)
            for m in range(HM):
                split_hidden(0, m)
            body(0, GS, first=True)
            with dve.Fori(1, GROUPS) as g:
                body(g, GS)
            body(GROUPS, TAIL, last=True)
            late = Chain(dve, late_step, GROUPS * PER_LATE, None)
            for part in range(2):
                norm(late, GROUPS, TAIL, part)
            for s in range(TAIL // 2):
                make_z(GROUPS, s)
                sum_z(GROUPS, s)

        @block.tensor
        def _(pe):
            pe.sem_inc(f_ready, PRE)
            pe.sem_inc(fc_ready, PRE)
            pe.sem_inc(z_t, PRE)
            pe.wait_ge(gw_in, 32)

            def hidden(g, m):
                pe.wait_ge(split_ready, PRE + g + 1)
                pe.wait_ge(f_saved, PRE + g * FPG + m + 1 - F)
                products = [(w, x, k) for w, x in ((w_rel, acc_s), (w_root, xn_s)) for k in range(K2)]
                for w, x, k in products:
                    for wp, xp in PARTS:
                        last = nc.tensor.matmul(psF[:, m % F, 0:GN], w[:, wp, k, m * P:(m + 1) * P], x[:, xp, k, :],
                                                start=(w is w_rel and k == 0 and (wp, xp) == PARTS[0]),
                                                stop=(w is w_root and k == K2 - 1 and (wp, xp) == PARTS[-1]))
                last.then_inc(f_ready, 1)

            def transposes(g, s):
                pe.wait_ge(z_ready, PRE + g * NP + s + 1)
                pe.wait_ge(zT_saved, PRE + g * NP + s + 1 - 2)
                for j in range(2):
                    for k in range(K2):
                        last = nc.tensor.transpose(psX[:, s % 2, k, j * P:j * P + SUB],
                                                   zz[:, 2 * s + j, k * P:(k + 1) * P], ident[0:SUB, 0:SUB])
                last.then_inc(z_t, 1)

            def body(g, ns, **place):
                n = ns * SUB
                for what, s in order(ns, **place):
                    if what == "h":
                        hidden(g + 1, s)
                    elif what == "gate":
                        m, x = s
                        pos = HM + GATES * m + x
                        pe.wait_ge(h_ready, PRE + g * HM + HM)
                        pe.wait_ge(f_saved, PRE + g * FPG + pos + 1 - F)
                        for k in range(HM):
                            for wp, xp in PARTS:
                                last = nc.tensor.matmul(psF[:, pos % F, 0:n], w_ih[:, wp, k, x * DH + m * P:x * DH + (m + 1) * P],
                                                        h_s[:, xp, k, 0:n], start=(k == 0 and (wp, xp) == PARTS[0]),
                                                        stop=(k == HM - 1 and (wp, xp) == PARTS[-1]))
                        last.then_inc(f_ready, 1)
                    elif what == "fc":
                        pe.wait_ge(hl_ready, PRE + g * HM + HM)
                        pe.wait_ge(x2_ready, PRE + g * NP + s + 1 - 2)
                        for j in range(2):
                            for k in range(HM):
                                cut = (2 * s + j) * SUB
                                last = nc.tensor.matmul(psN[0:SUB, s % 2, j, :], hl[:, k, cut:cut + SUB], w_fc[:, k, :],
                                                        start=(k == 0), stop=(k == HM - 1))
                        last.then_inc(fc_ready, 1)
                    elif what == "t":
                        transposes(g - 1, s)

            for m in range(HM):
                hidden(0, m)
            body(0, GS, first=True)
            with pe.Fori(1, GROUPS) as g:
                body(g, GS)
            body(GROUPS, TAIL, last=True)
            for s in range(TAIL // 2):
                transposes(GROUPS, s)


def route_phase(nc, io, sb, psum, sem, zsum, e1, e2, e1b, zb2):
    CAP = float(-(-N * 5 // (4 * NE)))
    HM = DH // P
    with ExitStack() as ctx:
        wr = sb(ctx, "wr", [P, K2, NE])
        br = sb(ctx, "br", [1, NE])
        ones = sb(ctx, "ones", [1, P])
        zm = sb(ctx, "zm", [P, K2])
        a = sb(ctx, "a", [1, NE])
        ex = sb(ctx, "ex", [1, NE])
        rw = sb(ctx, "rw", [1, NE])
        ld = sb(ctx, "ld", [1, NE])
        mx = sb(ctx, "mx", [1, 1])
        sm = sb(ctx, "sm", [1, 1])
        rs = sb(ctx, "rs", [1, 1])
        tv = sb(ctx, "tv", [1, NE])
        ti = sb(ctx, "ti", [1, NE], U32)
        wt = sb(ctx, "wt", [1, 2])
        wb = sb(ctx, "wb", [P, 2])
        b2 = sb(ctx, "b2", [P, 2, D])
        psL = psum(ctx, "psL", [P, NE])
        psW = psum(ctx, "psW", [P, 2])
        r_in = sem(ctx, "route_in")
        rstep = sem(ctx, "rstep")
        zm_ready = sem(ctx, "zm_ready")
        lg_ready = sem(ctx, "lg_ready")
        arg_ready = sem(ctx, "arg_ready")
        exp_ready = sem(ctx, "exp_ready")
        top_ready = sem(ctx, "top_ready")
        wt_ready = sem(ctx, "wt_ready")
        wb_ready = sem(ctx, "wb_ready")
        e_in = sem(ctx, "e_in")
        block = ctx.enter_context(nc.Block())

        @block.sync
        def _(sp):
            sp.dma_start(wr[:], io["ffn_wr"]).then_inc(r_in, 16)
            sp.dma_start(br[:], io["ffn_br"]).then_inc(r_in, 16)
            sp.wait_ge(top_ready, 1)
            for s in range(2):
                e = sp.value_load(ti[0:1, s:s + 1], min_val=0, max_val=NE - 1)
                rows = bass.ds(e * P, P)
                sp.dma_start(e1[:, s, :, :], io["ffn_w1"][rows, :].rearrange("p (k f) -> p k f", k=K2)).then_inc(e_in, 16)
                sp.dma_start(e2[:, s * HM:(s + 1) * HM, :], io["ffn_w2"][rows, :].rearrange("p (k f) -> p k f", k=HM)
                             ).then_inc(e_in, 16)
                sp.dma_start(e1b[:, s, :], io["ffn_b1"][rows, :]).then_inc(e_in, 16)
                sp.dma_start(b2[:, s, :], io["ffn_b2"][rows, :]).then_inc(e_in, 16)
            sp.wait_ge(e_in, 128)

        @block.scalar
        def _(act):
            for n in range(3):
                act.wait_ge(arg_ready, n + 1)
                width = 2 if n == 2 else NE
                nc.scalar.activation(ex[0:1, 0:width], a[0:1, 0:width], ACT.Exp, accum_out=sm[:]).then_inc(exp_ready, 1)

        @block.vector
        def _(dve):
            step = Chain(dve, rstep, 0, None)
            step(nc.vector.memset(ones[:], 1.0))
            step(nc.vector.tensor_reduce(zm[:], zsum[:], AX.X, ALU.add))
            nc.vector.tensor_scalar(zm[:], zm[:], 1.0 / N, None, ALU.mult).then_inc(zm_ready, 1)
            dve.wait_ge(r_in, 32)
            dve.wait_ge(lg_ready, 1)
            step(nc.vector.tensor_tensor(rw[:], psL[0:1, :], br[:], ALU.add))

            def softmax(src, n, dst, width):
                step(nc.vector.tensor_reduce(mx[:], src, AX.X, ALU.max))
                nc.vector.tensor_scalar(a[0:1, 0:width], src, mx[:], None, ALU.subtract).then_inc(arg_ready, 1)
                dve.wait_ge(exp_ready, n)
                step(nc.vector.reciprocal(rs[:], sm[:]))
                return nc.vector.tensor_scalar(dst, ex[0:1, 0:width], rs[:], None, ALU.mult)

            step(softmax(rw[:], 1, rw[:], NE))
            step(nc.vector.tensor_scalar(ld[:], rw[:], float(N), None, ALU.mult))
            step(nc.vector.reciprocal(ld[:], ld[:]))
            step(nc.vector.tensor_scalar(ld[:], ld[:], CAP, 1.0, ALU.mult, ALU.min))
            step(nc.vector.tensor_tensor(rw[:], rw[:], ld[:], ALU.mult))
            step(softmax(rw[:], 2, rw[:], NE))
            step(nc.vector.max(tv[:], rw[:]))
            nc.vector.max_index(ti[:], tv[:], rw[:]).then_inc(top_ready, 1)
            softmax(tv[0:1, 0:2], 3, wt[:], 2).then_inc(wt_ready, 1)
            dve.wait_ge(wb_ready, 1)
            step(nc.vector.tensor_copy(wb[:], psW[:]))
            dve.wait_ge(e_in, 128)
            step(nc.vector.tensor_scalar(zb2[:], b2[:, 0, :], wb[:, 0:1], None, ALU.mult))
            step(nc.vector.scalar_tensor_tensor(out=zb2[:], in0=b2[:, 1, :], scalar=wb[:, 1:2], in1=zb2[:],
                                                op0=ALU.mult, op1=ALU.add))
            for s in range(2):
                step(nc.vector.tensor_scalar(e2[:, s * HM:(s + 1) * HM, :], e2[:, s * HM:(s + 1) * HM, :], wb[:, s:s + 1],
                                             None, ALU.mult))

        @block.tensor
        def _(pe):
            pe.wait_ge(r_in, 32)
            pe.wait_ge(zm_ready, 1)
            for k in range(K2):
                last = nc.tensor.matmul(psL[0:1, :], zm[:, k:k + 1], wr[:, k, :], start=(k == 0), stop=(k == K2 - 1))
            last.then_inc(lg_ready, 1)
            pe.wait_ge(wt_ready, 1)
            nc.tensor.matmul(psW[:], ones[:], wt[:], start=True, stop=True).then_inc(wb_ready, 1)


def moe_phase(nc, io, sb, psum, sem, zT, z_mv, e1, e2, e1b, zb2, x2_dram):
    F = 4
    HM = DH // P
    TILES = 2 * HM
    with ExitStack() as ctx:
        gb = sb(ctx, "gb", [P, 2, D])
        hg = sb(ctx, "hg", [P, TILES, GN])
        x2 = sb(ctx, "x2m", [SUB, GS, D])
        y = sb(ctx, "ym", [SUB, GS, D])
        st = sb(ctx, "st4", [SUB, GS, 6])
        mv = sb(ctx, "mv4", [SUB, GS, 2])
        var = sb(ctx, "var4", [SUB, GS])
        rstd = sb(ctx, "rstd4", [SUB, GS])
        tmp = sb(ctx, "tmp4", [SUB, GS])
        psF = psum(ctx, "psF4", [P, F, 512])
        psN = psum(ctx, "psN4", [P, 4, 512])
        gb_in = sem(ctx, "gb_in")
        x2_in = sem(ctx, "x2_in")
        y_out = sem(ctx, "y_out")
        y_stored = sem(ctx, "y_stored")
        f_ready = sem(ctx, "mf_ready")
        f_saved = sem(ctx, "mf_saved")
        n_ready = sem(ctx, "mn_ready")
        n_saved = sem(ctx, "mn_saved")
        y_ready = sem(ctx, "y_ready")
        ystep = sem(ctx, "ystep")
        stats_taken = sem(ctx, "ystep_stats_taken")
        block = ctx.enter_context(nc.Block())

        @block.sync
        def _(sp):
            sp.dma_start(gb[:], io["ffn_gb"]).then_inc(gb_in, 16)

            def body(g, ns):
                sp.wait_ge(y_ready, PRE + g * GS)
                sp.dma_start(x2[:, 0:ns, :], x2_dram[bass.ds(g * GN, ns * SUB), :].rearrange("(j p) d -> p j d", p=SUB)
                             ).then_inc(x2_in, 16)
                sp.wait_ge(y_ready, PRE + g * GS + ns)
                sp.dma_start(io["out"][bass.ds(g * GN, ns * SUB), :].rearrange("(j p) d -> p j d", p=SUB), y[:, 0:ns, :]
                             ).then_inc(y_out, 16)
                sp.wait_ge(y_out, g * 16 + 16)
                sp.sem_inc(y_stored, 1)

            with sp.Fori(0, GROUPS) as g:
                body(g, GS)
            body(GROUPS, TAIL)

        @block.scalar
        def _(act):
            act.sem_inc(f_saved, PRE)

            def body(g, ns):
                n = ns * SUB
                for m in range(TILES):
                    act.wait_ge(f_ready, PRE + g * TILES + m + 1)
                    if m == 0:
                        act.wait_ge(n_ready, PRE + g * GS)
                    nc.scalar.activation(hg[:, m, 0:n], psF[:, m % F, 0:n], ACT.Gelu, bias=e1b[:, m // HM, m % HM:m % HM + 1]
                                         ).then_inc(f_saved, 1)

            with act.Fori(0, GROUPS) as g:
                body(g, GS)
            body(GROUPS, TAIL)

        @block.vector
        def _(dve):
            dve.sem_inc(n_saved, PRE)
            dve.sem_inc(y_ready, PRE)
            dve.sem_inc(y_stored, PRE)
            PER = 3 * GS + GS + 1 + RSQRT_STEPS + 3 * GS
            dve.wait_ge(gb_in, 16)

            def body(g, ns, per):
                step = Chain(dve, ystep, g * PER, per)
                dve.wait_ge(x2_in, g * 16 + 16)
                dve.wait_ge(y_stored, PRE + g)
                for j in range(ns):
                    step(nc.vector.tensor_scalar(y[:, j, :], x2[:, j, :], z_mv[:, bass.ds(g * GS + j, 1), 0],
                                                 z_mv[:, bass.ds(g * GS + j, 1), 1], ALU.subtract, ALU.mult))
                    step(nc.vector.tensor_tensor(y[:, j, :], y[:, j, :], zb2[0:SUB, :], ALU.add))
                for j in range(ns):
                    dve.wait_ge(n_ready, PRE + g * GS + j + 1)
                    nc.vector.tensor_tensor(y[:, j, :], y[:, j, :], psN[0:SUB, j, 0:D], ALU.add).then_inc(n_saved, 1)
                    dve.wait_ge(n_saved, PRE + g * GS + j + 1)
                    step(nc.vector.bn_stats(st[:, j, :], y[:, j, :]))
                dve.sem_inc(stats_taken, 1)
                for j in range(ns):
                    step.start(nc.vector.bn_aggr(mv[:, j, :], st[:, j, :]))
                step.wait()
                step(nc.vector.tensor_scalar(var[:, 0:ns], mv[:, 0:ns, 1], EPS, None, ALU.add))
                rsqrt_steps(nc, step, var[:, 0:ns], rstd[:, 0:ns], tmp[:, 0:ns])
                for j in range(ns):
                    step(nc.vector.tensor_scalar(y[:, j, :], y[:, j, :], mv[:, j, 0:1], rstd[:, j:j + 1],
                                                 ALU.subtract, ALU.mult))
                    step(nc.vector.tensor_tensor(y[:, j, :], y[:, j, :], gb[0:SUB, 0, :], ALU.mult))
                    step(nc.vector.tensor_tensor(y[:, j, :], y[:, j, :], gb[0:SUB, 1, :], ALU.add))
                    nc.vector.tensor_tensor(y[:, j, :], y[:, j, :], x2[:, j, :], ALU.add).then_inc(y_ready, 1)
                step.end()

            with dve.Fori(0, GROUPS) as g:
                body(g, GS, PER)
            body(GROUPS, TAIL, None)

        @block.tensor
        def _(pe):
            pe.sem_inc(f_ready, PRE)
            pe.sem_inc(n_ready, PRE)

            def body(g, ns):
                n = ns * SUB
                for m in range(TILES):
                    pe.wait_ge(f_saved, PRE + g * TILES + m + 1 - F)
                    for k in range(K2):
                        last = nc.tensor.matmul(psF[:, m % F, 0:n], e1[:, m // HM, k, (m % HM) * P:(m % HM + 1) * P],
                                                zT[:, k, bass.ds(g * GN, n)], start=(k == 0), stop=(k == K2 - 1))
                    last.then_inc(f_ready, 1)
                for j in range(ns):
                    pe.wait_ge(f_saved, PRE + g * TILES + TILES)
                    pe.wait_ge(n_saved, PRE + g * GS + j + 1 - GS)
                    for m in range(TILES):
                        last = nc.tensor.matmul(psN[0:SUB, j, 0:D], hg[:, m, j * SUB:(j + 1) * SUB], e2[:, m, :],
                                                start=(m == 0), stop=(m == TILES - 1))
                    last.then_inc(n_ready, 1)

            with pe.Fori(0, GROUPS) as g:
                body(g, GS)
            body(GROUPS, TAIL)


def kernel(**inputs):
    import numpy as _np
    import concourse.bacc as _bacc
    from concourse.bass_utils import run_bass_kernel_spmd as _run

    a = {name: _np.ascontiguousarray(value) for name, value in inputs.items()}

    def kxn(w):
        return _np.ascontiguousarray(w.reshape(-1, P, w.shape[-1]).transpose(1, 0, 2))

    def columns(*vectors):
        return _np.concatenate([v.reshape(-1, P).T for v in vectors], axis=1)

    def broadcast_rows(*vectors):
        return _np.ascontiguousarray(_np.broadcast_to(_np.stack(vectors)[None], (P, len(vectors), vectors[0].shape[0])))

    def edges(v, pad):
        full = _np.full(NCH * P, pad, v.dtype)
        full[:EDGES] = v
        return _np.ascontiguousarray(full.reshape(NCH, P).T)

    head = _np.arange(P) // 32
    w_ih = a["L0_gnn_W_ih"].reshape(4, DH, DH)
    gates = [0, 2, 3]
    arrays = {
        "x": a["x"],
        "src": edges(a["src"], 0), "dst": edges(a["dst"], PAD_DST),
        "mix_wkv": kxn(_np.concatenate([a["L0_mix_Wk"], a["L0_mix_Wv"]], axis=1)),
        "mix_bkv": broadcast_rows(_np.concatenate([a["L0_mix_bk"], a["L0_mix_bv"]])).reshape(P, 2 * D),
        "mix_wq": kxn(a["L0_mix_Wq"]), "mix_wo": kxn(a["L0_mix_Wo"]),
        "mix_w1": kxn(a["L0_mix_W1"]), "mix_w2": kxn(a["L0_mix_W2"]),
        "mix_cols": columns(a["L0_mix_bq"], a["L0_mix_ln1_g"], a["L0_mix_ln1_b"], a["L0_mix_b1"]),
        "mix_rows": broadcast_rows(a["L0_mix_bo"], a["L0_mix_ln1_g"], a["L0_mix_ln2_g"], a["L0_mix_ln1_b"],
                                   a["L0_mix_b2"], a["L0_mix_ln2_b"], a["L0_gnn_b_fc"]),
        "headm": (head[:, None] == head[None, :]).astype(_np.float32),
        "w_rel": kxn(a["L0_gnn_W_rel"]), "w_root": kxn(a["L0_gnn_W_root"]),
        "w_ih": kxn(_np.ascontiguousarray(_np.concatenate([w_ih[g] for g in gates]).T)),
        "w_fc": kxn(a["L0_gnn_W_fc"]),
        "gnn_cols": columns(a["L0_gnn_b_rel"], *[a[b].reshape(4, DH)[g] for b in ("L0_gnn_b_ih", "L0_gnn_b_hh") for g in gates]),
        "ffn_wr": kxn(a["L0_ffn_Wr"]), "ffn_br": a["L0_ffn_br"].reshape(1, NE),
        "ffn_w1": _np.ascontiguousarray(a["L0_ffn_W1"].reshape(NE, K2, P, DH).transpose(0, 2, 1, 3)).reshape(NE * P, K2 * DH),
        "ffn_w2": _np.ascontiguousarray(a["L0_ffn_W2"].reshape(NE, DH // P, P, D).transpose(0, 2, 1, 3)).reshape(NE * P, -1),
        "ffn_b1": _np.ascontiguousarray(a["L0_ffn_b1"].reshape(NE, DH // P, P).transpose(0, 2, 1)).reshape(NE * P, -1),
        "ffn_b2": _np.ascontiguousarray(_np.broadcast_to(a["L0_ffn_b2"][:, None, :], (NE, P, D))).reshape(NE * P, D),
        "ffn_gb": broadcast_rows(a["L0_ffn_gamma"], a["L0_ffn_beta"]),
    }
    nc = _bacc.Bacc("TRN2", target_bir_lowering=False, num_devices=1)
    arrays = {f"in_{name}": _np.ascontiguousarray(v) for name, v in arrays.items()}
    io = {name[3:]: nc.dram_tensor(name, v.shape, mybir.dt.from_np(v.dtype), kind="ExternalInput").ap()
          for name, v in arrays.items()}
    for name in ("xn_dram", "s1_dram", "x2_dram"):
        io[name] = nc.dram_tensor(name, (N, D), F32, kind="Internal").ap()
    io["table_dram"] = nc.dram_tensor("table_dram", (N, 2 * D), F16, kind="Internal").ap()
    io["xnT_dram"] = nc.dram_tensor("xnT_dram", (P, K2, NPAD), F32, kind="Internal").ap()
    io["rest_dram"] = nc.dram_tensor("rest_dram", (P, NCH), F32, kind="Internal").ap()
    io["out"] = nc.dram_tensor("out", (N, D), F32, kind="ExternalOutput").ap()
    gps_layer(nc, io)
    r = _run(nc, [arrays], core_ids=[0])
    return r.results[0]["out"]
```

```python
from contextlib import ExitStack

import numpy as np

import concourse.bass as bass
from concourse import mybir

F32 = mybir.dt.float32
F32R = mybir.dt.float32r
F16 = mybir.dt.float16
I32 = mybir.dt.int32
U32 = mybir.dt.uint32
ALU = mybir.AluOpType
ACT = mybir.ActivationFunctionType
AX = mybir.AxisListType
RMAX = bass.bass_isa.ReduceOp.max

P = 128
N = 6250
D = 256
K2 = D // P
DH = 512
FF = 1024
NE = 8
EDGES = 106250
SUB = 125
GS = 4
GN = GS * SUB
GROUPS = N // GN
TAIL = (N - GROUPS * GN) // SUB
NPAD = (GROUPS + 1) * GN
NSUB = N // SUB
W = 64
CPS = 4
SGE = CPS * P
NSG = -(-EDGES // SGE)
NCH = NSG * CPS
ACC = max(N + W, NPAD)
KV_SG = NSUB + 2
SGI = (NSG - KV_SG) // (GROUPS + 1)
RING = 4
HALF = SGI // 2
OH = 4
LEAD = 2
LAG = 1
NORM_U = 10
BIG = float(2 ** 14)
PAD_DST = 2 ** 20
EPS = 1e-5
PRE = 16

assert NSG == KV_SG + SGI * (GROUPS + 1) and SGI % RING == 0 and SGI % 2 == 0 and KV_SG - NSUB == LEAD and NSUB % NORM_U == 0 and N < BIG


class Chain:

    def __init__(self, eng, sem, base, per):
        self.eng, self.sem, self.base, self.per, self.k = eng, sem, base, per, 0

    def __call__(self, ins):
        self.k += 1
        ins.then_inc(self.sem, 1)
        self.eng.wait_ge(self.sem, self.base + self.k)

    def start(self, ins):
        self.k += 1
        ins.then_inc(self.sem, 1)

    def wait(self):
        self.eng.wait_ge(self.sem, self.base + self.k)

    def end(self):
        assert self.per in (None, self.k), self.k


def rsqrt_guess(nc, step, v, y, t):
    step(nc.vector.tensor_scalar(t.bitcast(I32), v.bitcast(I32), 1, None, ALU.logical_shift_right))
    step(nc.vector.tensor_scalar(y.bitcast(I32), t.bitcast(I32), -1.0, float(0x5F3759DF), ALU.mult, ALU.add))


def rsqrt_newton(nc, step, v, y, t, rounds):
    for _ in range(rounds):
        step(nc.vector.tensor_tensor(t, y, y, ALU.mult))
        step(nc.vector.tensor_tensor(t, t, v, ALU.mult))
        step(nc.vector.tensor_scalar(t, t, -0.5, 1.5, ALU.mult, ALU.add))
        step(nc.vector.tensor_tensor(y, y, t, ALU.mult))


def rsqrt_steps(nc, step, v, y, t):
    rsqrt_guess(nc, step, v, y, t)
    rsqrt_newton(nc, step, v, y, t, 3)


RSQRT_STEPS = 14


def gps_layer(nc, io):
    with ExitStack() as whole:
        def sb(ctx, name, shape, dt=F32):
            return ctx.enter_context(nc.sbuf_tensor(name, shape, dt))

        def psum(ctx, name, shape):
            return ctx.enter_context(nc.psum_tensor(name, shape, F32))

        def sem(ctx, name):
            return ctx.enter_context(nc.semaphore(name))

        xn_dram, s1_dram, x2_dram = io["xn_dram"], io["s1_dram"], io["x2_dram"]

        accT = sb(whole, "accT", [P, K2, ACC])
        ident = sb(whole, "ident", [P, P])
        flag_i = sb(whole, "flag_i", [P, 1], I32)
        zsum = sb(whole, "zsum", [P, K2, NSUB // 2])
        z_mv = sb(whole, "z_mv", [SUB, NSUB, 2])
        edgew = whole.enter_context(ExitStack())
        src_t = sb(edgew, "src_t", [P, NCH], I32)
        iota_w = sb(edgew, "iota_w", [P, W])
        with ExitStack() as mixw:
            xnT = sb(mixw, "xnT", [P, K2, NPAD])
            dst_rel = sb(mixw, "dst_rel", [P, NCH + LEAD * CPS])
            base_i = sb(mixw, "base_i", [P, LAG + NSG], I32)
            qdiv = sb(mixw, "qdiv", [P, K2, P])
            kvwo = sb(mixw, "kvwo", [P, K2, D])
            wq = sb(mixw, "wq", [P, K2, D])
            w1 = sb(mixw, "w1", [P, K2, FF])
            w2 = sb(mixw, "w2", [P, FF // P, D])
            colb = sb(mixw, "colb", [P, 14])
            rows = sb(mixw, "rows", [P, 7, D])
            set_up(nc, io, sb, psum, sem, ident, src_t, dst_rel, base_i, flag_i, iota_w, accT)
            with ExitStack() as kvw:
                wkv = sb(kvw, "wkv", [P, K2, 2 * D])
                bkv = sb(kvw, "bkv", [P, 2 * D])
                wo = sb(kvw, "wo", [P, K2, D])
                w_root = sb(kvw, "w_root", [P, K2, DH])
                headm = sb(kvw, "headm", [P, P])
                norm_phase(nc, io, sb, psum, sem, xnT, accT, ident, xn_dram, wkv, bkv, wo, w_root, headm)
                kv_phase(nc, io, sb, psum, sem, xnT, accT, ident, src_t, dst_rel, base_i, iota_w,
                         wkv, bkv, wo, w_root, headm, qdiv, kvwo, wq, w1, w2, colb, rows)
            mix_phase(nc, io, sb, psum, sem, xnT, accT, ident, src_t, dst_rel, base_i, iota_w,
                      qdiv, kvwo, wq, w1, w2, colb, rows, xn_dram, s1_dram)
        with ExitStack() as gnnw:
            w_rel = sb(gnnw, "w_rel", [P, 2, K2, DH], F32R)
            w_ih = sb(gnnw, "w_ih", [P, 2, DH // P, 3 * DH], F32R)
            w_fc = sb(gnnw, "w_fc", [P, DH // P, D])
            cols = sb(gnnw, "gnn_cols", [P, 7 * DH // P])
            rest_phase(nc, io, sb, psum, sem, accT, src_t, iota_w, flag_i, w_rel, w_ih, w_fc, cols)
            gnn_phase(nc, io, sb, psum, sem, accT, ident, zsum, z_mv, w_rel, w_ih, w_fc, cols, s1_dram, x2_dram)
        edgew.close()
        e1 = sb(whole, "e1", [P, 2, 2, K2, DH], F32R)
        e2 = sb(whole, "e2", [P, 2 * DH // P, D])
        e1b = sb(whole, "e1b", [P, 2, DH // P])
        zb2 = sb(whole, "zb2", [P, D])
        route_phase(nc, io, sb, psum, sem, zsum, e1, e2, e1b, zb2)
        moe_phase(nc, io, sb, psum, sem, accT, z_mv, e1, e2, e1b, zb2, x2_dram)


def set_up(nc, io, sb, psum, sem, ident, src_t, dst_rel, base_i, flag_i, iota_w, accT):
    with ExitStack() as ctx:
        dst_t = sb(ctx, "dst_t", [P, NCH], I32)
        dst_rest = sb(ctx, "dst_rest", [P, NCH])
        rest_ready = sem(ctx, "rest_ready")
        rest_out = sem(ctx, "rest_out")
        dst_f = sb(ctx, "dst_f", [P, NCH])
        low = sb(ctx, "low", [P, NSG])
        nbase = sb(ctx, "nbase", [P, NSG])
        outside = sb(ctx, "outside", [P, NCH])
        anyout = sb(ctx, "anyout", [P, 1])
        anyall = sb(ctx, "anyall", [P, 1])
        edges_in = sem(ctx, "edges_in")
        src_in = sem(ctx, "src_in")
        cleared = sem(ctx, "cleared")
        made = sem(ctx, "made")
        low_ready = sem(ctx, "low_ready")
        base_ready = sem(ctx, "base_ready")
        step_done = sem(ctx, "setup_step")
        out_ready = sem(ctx, "out_ready")
        any_ready = sem(ctx, "any_ready")
        block = ctx.enter_context(nc.Block())

        @block.sync
        def _(sp):
            sp.dma_start(dst_t[:], io["dst"]).then_inc(edges_in, 16)
            sp.dma_start(src_t[:], io["src"]).then_inc(src_in, 16)
            sp.wait_ge(src_in, 16)
            sp.wait_ge(rest_ready, 1)
            sp.dma_start(io["rest_dram"], dst_rest[:]).then_inc(rest_out, 16)
            sp.wait_ge(rest_out, 16)

        @block.gpsimd
        def _(pool):
            pool.memset(ident[:], 0.0).then_inc(cleared, 1)
            pool.iota(iota_w[:], [[1, W]], base=0, channel_multiplier=0,
                      allow_small_or_imprecise_dtypes=True).then_inc(made, 1)
            pool.wait_ge(cleared, 1)
            pool.affine_select(out=ident[:], in_=ident[:], compare_op=ALU.not_equal, fill=1.0,
                               base=0, pattern=[[-1, P]], channel_multiplier=1).then_inc(made, 1)
            pool.memset(accT[:, 0, :], 0.0)
            pool.wait_ge(low_ready, 1)
            pool.partition_all_reduce(nbase[:], low[:], P, RMAX).then_inc(base_ready, 1)
            pool.wait_ge(out_ready, 1)
            pool.partition_all_reduce(anyall[:], anyout[:], P, RMAX).then_inc(any_ready, 1)

        @block.vector
        def _(dve):
            step = Chain(dve, step_done, 0, None)
            dve.wait_ge(edges_in, 16)
            step(nc.vector.tensor_copy(dst_f[:], dst_t[:]))
            step(nc.vector.tensor_reduce(low[:], dst_f[:].rearrange("p (s c) -> p s c", c=CPS), AX.X, ALU.min))
            nc.vector.tensor_scalar(low[:], low[:], -1.0, None, ALU.mult).then_inc(low_ready, 1)
            dve.wait_ge(base_ready, 1)
            step(nc.vector.memset(base_i[:, 0:LAG], 0))
            step(nc.vector.tensor_scalar(base_i[:, LAG:LAG + NSG], nbase[:], -1.0, None, ALU.mult))
            step(nc.vector.memset(dst_rel[:, NCH:NCH + LEAD * CPS], -1.0))
            step(nc.vector.tensor_tensor(dst_rel[:, 0:NCH].rearrange("p (s c) -> p s c", c=CPS),
                                         dst_f[:].rearrange("p (s c) -> p s c", c=CPS),
                                         nbase[:].rearrange("p (s o) -> p s o", o=1).to_broadcast([P, NSG, CPS]), ALU.add))
            step(nc.vector.tensor_scalar(outside[:], dst_f[:], float(N), None, ALU.is_lt))
            step(nc.vector.scalar_tensor_tensor(out=outside[:], in0=dst_rel[:, 0:NCH], scalar=float(W), in1=outside[:],
                                                op0=ALU.is_ge, op1=ALU.mult))
            step(nc.vector.scalar_tensor_tensor(out=dst_rest[:], in0=dst_f[:], scalar=BIG, in1=outside[:],
                                                op0=ALU.add, op1=ALU.mult))
            nc.vector.tensor_scalar(dst_rest[:], dst_rest[:], -BIG, None, ALU.add).then_inc(rest_ready, 1)
            nc.vector.tensor_reduce(anyout[:], outside[:], AX.X, ALU.max).then_inc(out_ready, 1)
            dve.wait_ge(any_ready, 1)
            step(nc.vector.tensor_copy(flag_i[:], anyall[:]))


def norm_phase(nc, io, sb, psum, sem, xnT, accT, ident, xn_dram, wkv, bkv, wo, w_root, headm):
    U = NORM_U
    T = 5
    CH = 5
    with ExitStack() as ctx:
        xin = sb(ctx, "xin", [SUB, 2, U, D])
        xnb = sb(ctx, "xnb", [SUB, U, D])
        xhl = sb(ctx, "xhl", [SUB, U, 2, D], F16)
        st = sb(ctx, "st", [SUB, U, 6])
        mv = sb(ctx, "mv", [SUB, U, 2])
        var = sb(ctx, "var", [SUB, U])
        rstd = sb(ctx, "rstd", [SUB, U])
        tmp = sb(ctx, "tmp", [SUB, U])
        psT = psum(ctx, "psT", [P, T, 512])
        w_in = sem(ctx, "norm_w_in")
        x_in = [[sem(ctx, f"x_in{half}_{c}") for c in range(U // CH)] for half in range(2)]
        xn_out = [sem(ctx, f"xn_out{c}") for c in range(U // CH)]
        nstep = sem(ctx, "nstep")
        stats_taken = sem(ctx, "nstep_stats_taken")
        xn_ready = sem(ctx, "xn_ready")
        high_ready = sem(ctx, "high_ready")
        low_ready = sem(ctx, "low_part_ready")
        xn_stored = sem(ctx, "xn_stored")
        t_ready = sem(ctx, "t_ready")
        xT_saved = sem(ctx, "xT_saved")
        block = ctx.enter_context(nc.Block())
        ITERS = NSUB // U

        def sub_rows(i, j):
            return bass.ds(i * (U * SUB) + j * SUB, SUB)

        def chunk(dram, i, c):
            return dram[bass.ds(i * (U * SUB) + c * (CH * SUB), CH * SUB), :].rearrange("(j p) d -> p j d", p=SUB)

        @block.sync
        def _(sp):
            def load(i, c):
                sp.dma_start(xin[:, i % 2, c * CH:(c + 1) * CH, :], chunk(io["x"], i, c)).then_inc(x_in[i % 2][c], 16)

            def body(i):
                for c in range(U // CH):
                    sp.wait_ge(xn_ready, PRE + i * U + (c + 1) * CH)
                    sp.dma_start(chunk(xn_dram, i, c), xnb[:, c * CH:(c + 1) * CH, :]).then_inc(xn_out[c], 16)
                    sp.wait_ge(low_ready, PRE + i * U + (c + 1) * CH)
                    sp.dma_start(chunk(io["table_dram"], i, c), xhl[:, c * CH:(c + 1) * CH, :, :].rearrange("p j t d -> p j (t d)")
                                 ).then_inc(xn_out[c], 16)
                if i + 2 < ITERS:
                    for c in range(U // CH):
                        load(i + 2, c)
                for c in range(U // CH):
                    sp.wait_ge(xn_out[c], i * 32 + 32)
                    sp.sem_inc(xn_stored, 1)

            for c in range(U // CH):
                load(0, c)
            for c in range(U // CH):
                load(1, c)
            sp.dma_start(wkv[:], io["mix_wkv"]).then_inc(w_in, 16)
            sp.dma_start(bkv[:], io["mix_bkv"]).then_inc(w_in, 16)
            sp.dma_start(wo[:], io["mix_wo"]).then_inc(w_in, 16)
            sp.dma_start(w_root[:], io["w_root"]).then_inc(w_in, 16)
            sp.dma_start(headm[:], io["headm"]).then_inc(w_in, 16)
            for i in range(ITERS):
                body(i)
            sp.wait_ge(w_in, 80)

        @block.gpsimd
        def _(pool):
            pool.sem_inc(low_ready, PRE)
            pool.memset(accT[:, 1, :], 0.0)
            with pool.Fori(0, ITERS) as i:
                for j in range(U):
                    pool.wait_ge(high_ready, PRE + i * U + j + 1)
                    pool.tensor_tensor(xhl[:, j, 1, :], xnb[:, j, :], xhl[:, j, 0, :], ALU.subtract).then_inc(low_ready, 1)

        @block.vector
        def _(dve):
            dve.sem_inc(xn_ready, PRE)
            dve.sem_inc(xn_stored, PRE)
            nc.vector.memset(xnT[:, :, N:NPAD], 0.0)

            def body(i, half, turn):
                step = Chain(dve, nstep, i * (2 * U + 1 + RSQRT_STEPS), 2 * U + 1 + RSQRT_STEPS)
                for j in range(U):
                    if j % CH == 0:
                        dve.wait_ge(x_in[half][j // CH], turn * 16 + 16)
                    step.start(nc.vector.bn_stats(st[:, j, :], xin[:, half, j, :]))
                step.wait()
                dve.sem_inc(stats_taken, 1)
                for j in range(U):
                    step.start(nc.vector.bn_aggr(mv[:, j, :], st[:, j, :]))
                step.wait()
                step(nc.vector.tensor_scalar(var[:], mv[:, :, 1], EPS, None, ALU.add))
                rsqrt_steps(nc, step, var[:], rstd[:], tmp[:])
                step.end()
                dve.wait_ge(t_ready, PRE + i * U)
                for j in range(U):
                    if j % CH == 0:
                        dve.wait_ge(xn_stored, PRE + (i - 1) * (U // CH) + j // CH + 1)
                    nc.vector.tensor_scalar(xnb[:, j, :], xin[:, half, j, :], mv[:, j, 0:1], rstd[:, j:j + 1],
                                            ALU.subtract, ALU.mult).then_inc(xn_ready, 1)

            with dve.Fori(0, ITERS // 2) as turn:
                for half in range(2):
                    body(turn * 2 + half, half, turn)
            body(ITERS - 1, 0, ITERS // 2)

        @block.scalar
        def _(act):
            act.sem_inc(high_ready, PRE)
            act.sem_inc(xT_saved, PRE)
            with act.Fori(0, ITERS) as i:
                for j in range(U + 1):
                    if j < U:
                        act.wait_ge(xn_ready, PRE + i * U + j + 1)
                        nc.scalar.copy(xhl[:, j, 0, :], xnb[:, j, :]).then_inc(high_ready, 1)
                    if j:
                        act.wait_ge(t_ready, PRE + i * U + j)
                        nc.scalar.copy(xnT[:, :, sub_rows(i, j - 1)],
                                       psT[:, (j - 1) % T, 0:K2 * SUB].rearrange("p (k n) -> p k n", k=K2)).then_inc(xT_saved, 1)

        @block.tensor
        def _(pe):
            pe.sem_inc(t_ready, PRE)
            with pe.Fori(0, ITERS) as i:
                for j in range(U):
                    pe.wait_ge(xn_ready, PRE + i * U + j + 1)
                    pe.wait_ge(xT_saved, PRE + i * U + j + 1 - T)
                    for k in range(K2):
                        last = nc.tensor.transpose(psT[:, j % T, k * SUB:(k + 1) * SUB],
                                                   xnb[:, j, k * P:(k + 1) * P], ident[0:SUB, 0:SUB])
                    last.then_inc(t_ready, 1)


def kv_phase(nc, io, sb, psum, sem, xnT, accT, ident, src_t, dst_rel, base_i, iota_w, wkv, bkv, wo, w_root, headm, qdiv, kvwo,
             wq, w1, w2, colb, rows):
    U = NORM_U
    VE = P + 1
    RING = HALF = OH = U // 2
    with ExitStack() as ctx:
        ring = sb(ctx, "kv_ring", [P, RING, CPS, 2 * D], F16)
        stage = sb(ctx, "kv_stage", [P, 2, HALF * CPS], I32)
        oh = sb(ctx, "kv_oh", [P, OH, CPS, W], F16)
        xT = sb(ctx, "xT", [P, 2, K2, SUB])
        kb = sb(ctx, "kb", [SUB, 2, D])
        vx = sb(ctx, "vx", [SUB, 2, K2, VE])
        ek = sb(ctx, "ek", [SUB, 2, D])
        rk = sb(ctx, "rk", [SUB, 2, D])
        kphi = sb(ctx, "kphi", [SUB, 2, D])
        zero = sb(ctx, "zero", [SUB, VE])
        kvm = sb(ctx, "kvm", [P, K2, P])
        kvmT = sb(ctx, "kvmT", [P, K2, P])
        ksum = sb(ctx, "ksum", [P, K2])
        psG = psum(ctx, "kv_psG", [P, 2, 512])
        root = sb(ctx, "root", [P, 2, 2, 2 * SUB])
        psR = psum(ctx, "kv_psR", [P, 2, 512])
        psT = psR[:, 0, :]
        psKV = psum(ctx, "psKV", [P, 2, 2 * D])
        psA = psum(ctx, "psA", [P, K2, 512])
        zeroed = sem(ctx, "zeroed")
        mix_w_in = sem(ctx, "mix_w_in")
        root_ready = sem(ctx, "root_ready")
        root_saved = sem(ctx, "root_saved")
        root_out = sem(ctx, "root_out")
        root_stored = sem(ctx, "root_stored")
        staged = sem(ctx, "kv_staged")
        slot_taken = sem(ctx, "kv_slot_taken")
        gathered = [sem(ctx, f"kv_gathered{r}") for r in range(RING)]
        oh_ready = sem(ctx, "kv_oh_ready")
        ag_ready = sem(ctx, "kv_ag_ready")
        ag_added = sem(ctx, "kv_ag_added")
        xT_ready = sem(ctx, "xT_ready")
        kv_ready = sem(ctx, "kv_ready")
        kb_ready = sem(ctx, "kb_ready")
        vx_ready = sem(ctx, "vx_ready")
        ek_ready = sem(ctx, "ek_ready")
        rk_ready = sem(ctx, "rk_ready")
        kphi_ready = sem(ctx, "kphi_ready")
        acc_done = sem(ctx, "acc_done")
        sums_done = sem(ctx, "sums_done")
        kvm_ready = sem(ctx, "kvm_ready")
        kvmT_ps = sem(ctx, "kvmT_ps")
        kvmT_sb = sem(ctx, "kvmT_sb")
        kvwo_ps = sem(ctx, "kvwo_ps")
        fin = sem(ctx, "norm_fin")
        block = ctx.enter_context(nc.Block())
        ITERS = NSUB // U

        @block.sync
        def _(sp):
            for dst, src in ((wq, "mix_wq"), (w1, "mix_w1"), (w2, "mix_w2"), (colb, "mix_cols"), (rows, "mix_rows")):
                sp.dma_start(dst[:], io[src]).then_inc(mix_w_in, 16)
            with sp.Fori(0, ITERS) as i:
                for j in range(U):
                    sp.wait_ge(root_saved, PRE + i * U + j + 1)
                    tiles = slice(j % 2 * 2, j % 2 * 2 + 2)
                    sp.dma_start(io["root_dram"][:, tiles, bass.ds(i * (U * SUB) + j // 2 * (2 * SUB), 2 * SUB)],
                                 root[:, j % 2, :, :]).then_inc(root_out, 16)
                    sp.wait_ge(root_out, i * (U * 16) + (j + 1) * 16)
                    sp.sem_inc(root_stored, 1)
            sp.wait_ge(mix_w_in, 80)

        @block.gpsimd
        def _(pool):
            def stage_half(first, a, half):
                pool.wait_ge(ag_ready, PRE + first - HALF)
                pool.tensor_copy(stage[:, a, :], src_t[:, bass.ds(first * CPS, HALF * CPS)]).then_inc(staged, 1)
                pool.wait_ge(staged, half + 1)

            def gather(sg, a, h):
                pool.wait_ge(ag_ready, PRE + sg + 1 - RING)
                pool.sem_inc(slot_taken, 1)
                for c in range(CPS):
                    col = h * CPS + c
                    pool.indirect_dma_start(
                        out=ring[:, h, c, :], out_offset=None, in_=io["table_dram"][:, :],
                        in_offset=bass.IndirectOffsetOnAxis(ap=stage[:, a, col:col + 1], axis=0),
                    ).then_inc(gathered[h], 16)

            with pool.Fori(0, ITERS) as i:
                for a in range(2):
                    stage_half(i * U + a * HALF, a, i * 2 + a)
                    for h in range(HALF):
                        gather(i * U + a * HALF + h, a, h)
            stage_half(NSUB, 0, ITERS * 2)
            for h in range(KV_SG - NSUB):
                gather(NSUB + h, 0, h)

        @block.vector
        def _(dve):
            dve.sem_inc(root_stored, PRE)
            dve.sem_inc(kb_ready, PRE)
            dve.sem_inc(vx_ready, PRE)
            dve.sem_inc(kphi_ready, PRE)
            dve.sem_inc(ag_added, PRE)
            dve.sem_inc(oh_ready, PRE)
            nc.vector.memset(zero[:], 0.0).then_inc(zeroed, 1)
            nc.vector.memset(vx[:], 1.0).then_inc(zeroed, 1)
            nc.vector.memset(psG[:, LAG, :], 0.0).then_inc(zeroed, 1)
            dve.wait_ge(zeroed, 3)

            def one_hot(sg, slot):
                dve.wait_ge(ag_ready, PRE + sg + 1 - OH)
                nc.vector.tensor_tensor(
                    oh[:, slot, :, :],
                    dst_rel[:, bass.ds(sg * CPS, CPS)].rearrange("p (c o) -> p c o", o=1).to_broadcast([P, CPS, W]),
                    iota_w[:].rearrange("p (o w) -> p o w", o=1).to_broadcast([P, CPS, W]),
                    ALU.is_equal).then_inc(oh_ready, 1)

            def add_window(turn, bank):
                base = dve.value_load(base_i[0:1, bass.ds(turn, 1)], min_val=0, max_val=N - 1)
                dve.wait_ge(ag_ready, PRE + turn + 1 - LAG)
                dve.wait_ge(ag_added, PRE + turn)
                win = accT[:, :, bass.ds(base, W)]
                nc.vector.tensor_tensor(win, win, psG[:, bank, 0:K2 * W].rearrange("p (k w) -> p k w", k=K2),
                                        ALU.add).then_inc(ag_added, 1)

            for s in range(LEAD):
                one_hot(s, s)
            with dve.Fori(0, ITERS) as i:
                for j in range(U + 2):
                    if j < U:
                        one_hot(i * U + j + LEAD, (j + LEAD) % OH)
                        add_window(i * U + j, (j - LAG) % 2)
                    if 1 <= j <= U:
                        a = j - 1
                        dve.wait_ge(kv_ready, PRE + i * U + a + 1)
                        dve.wait_ge(ek_ready, PRE + i * U + a + 1 - 2)
                        dve.wait_ge(rk_ready, PRE + i * U + a + 1 - 2)
                        nc.vector.tensor_tensor(kb[:, a % 2, :], psKV[0:SUB, a % 2, 0:D], bkv[0:SUB, 0:D],
                                                ALU.add).then_inc(kb_ready, 1)
                        dve.wait_ge(acc_done, PRE + i * U + a + 1 - 2)
                        nc.vector.tensor_tensor(vx[:, a % 2, :, 0:P],
                                                psKV[0:SUB, a % 2, D:2 * D].rearrange("p (h e) -> p h e", h=K2),
                                                bkv[0:SUB, D:2 * D].rearrange("p (h e) -> p h e", h=K2),
                                                ALU.add).then_inc(vx_ready, 1)
                    if j >= 2:
                        a = j - 2
                        dve.wait_ge(rk_ready, PRE + i * U + a + 1)
                        dve.wait_ge(acc_done, PRE + i * U + a + 1 - 2)
                        nc.vector.scalar_tensor_tensor(out=kphi[:, a % 2, :], in0=ek[:, a % 2, :], scalar=1.0,
                                                       in1=rk[:, a % 2, :], op0=ALU.min, op1=ALU.add
                                                       ).then_inc(kphi_ready, 1)
            for turn in range(NSUB, KV_SG + LAG):
                add_window(turn, (turn - LAG) % 2)
            dve.wait_ge(sums_done, 1)
            for h in range(K2):
                nc.vector.tensor_tensor(kvm[:, h, :], psA[:, h, 0:P], headm[:], ALU.mult).then_inc(kvm_ready, 1)
                nc.vector.tensor_copy(ksum[:, h:h + 1], psA[:, h, P:P + 1]).then_inc(kvm_ready, 1)
            dve.wait_ge(kvm_ready, 4)
            for h in range(K2):
                nc.vector.tensor_scalar(qdiv[:, h, :], headm[:], ksum[:, h:h + 1], None, ALU.mult).then_inc(fin, 1)
            dve.wait_ge(kvmT_ps, 1)
            nc.vector.tensor_copy(kvmT[:], psT[:, 0:K2 * P].rearrange("p (h e) -> p h e", h=K2)).then_inc(kvmT_sb, 1)
            dve.wait_ge(kvwo_ps, 1)
            nc.vector.tensor_copy(kvwo[:], psKV[:, 0, :].rearrange("p (h e) -> p h e", h=K2)).then_inc(fin, 1)

        @block.scalar
        def _(act):
            act.sem_inc(xT_ready, PRE)
            act.sem_inc(ek_ready, PRE)
            act.sem_inc(rk_ready, PRE)
            act.sem_inc(root_saved, PRE)
            with act.Fori(0, ITERS) as i:
                for j in range(U + 1):
                    if j < U:
                        act.wait_ge(kv_ready, PRE + i * U + j + 1 - 2)
                        nc.scalar.copy(xT[:, j % 2, :, :], xnT[:, :, bass.ds(i * (U * SUB) + j * SUB, SUB)]).then_inc(xT_ready, 1)
                    if j >= 1:
                        a = j - 1
                        act.wait_ge(kb_ready, PRE + i * U + a + 1)
                        act.wait_ge(kphi_ready, PRE + i * U + a + 1 - 2)
                        nc.scalar.activation(ek[:, a % 2, :], kb[:, a % 2, :], ACT.Exp).then_inc(ek_ready, 1)
                        nc.scalar.activation(rk[:, a % 2, :], kb[:, a % 2, :], ACT.Relu).then_inc(rk_ready, 1)
                        act.wait_ge(root_ready, PRE + i * U + a + 1)
                        act.wait_ge(root_stored, PRE + i * U + a + 1 - 2)
                        nc.scalar.copy(root[:, a % 2, :, :], psR[:, a % 2, 0:4 * SUB].rearrange("p (t n) -> p t n", t=2)
                                       ).then_inc(root_saved, 1)

        @block.tensor
        def _(pe):
            pe.sem_inc(kv_ready, PRE)
            pe.sem_inc(root_ready, PRE)
            pe.sem_inc(acc_done, PRE)
            pe.sem_inc(ag_ready, PRE)
            pe.wait_ge(zeroed, 3)

            def sum_edges(sg, slot, count, bank):
                pe.wait_ge(oh_ready, PRE + sg + 1)
                pe.wait_ge(ag_added, PRE + sg + LAG - 1)
                pe.wait_ge(gathered[slot], count * (16 * CPS))
                for k in range(K2):
                    for c in range(CPS):
                        for part in range(2):
                            cut = part * D + k * P
                            last = nc.tensor.matmul(psG[:, bank, k * W:(k + 1) * W], ring[:, slot, c, cut:cut + P],
                                                    oh[:, slot, c, :], start=(c + part == 0), stop=(c + part == CPS))
                last.then_inc(ag_ready, 1)

            for h in range(K2):
                nc.tensor.matmul(psA[:, h, 0:VE], zero[:, 0:P], zero[:], start=True, stop=False)
            with pe.Fori(0, ITERS) as i:
                for j in range(U + 3):
                    if j < U:
                        pe.wait_ge(xT_ready, PRE + i * U + j + 1)
                        pe.wait_ge(kb_ready, PRE + i * U + j + 1 - 2)
                        pe.wait_ge(vx_ready, PRE + i * U + j + 1 - 2)
                        for k in range(K2):
                            last = nc.tensor.matmul(psKV[0:SUB, j % 2, :], xT[:, j % 2, k, :], wkv[:, k, :],
                                                    start=(k == 0), stop=(k == K2 - 1))
                        last.then_inc(kv_ready, 1)
                        sum_edges(i * U + j, j % RING, i * 2 + j // RING + 1, j % 2)
                        pe.wait_ge(root_saved, PRE + i * U + j + 1 - 2)
                        for t in range(2):
                            tile = j % 2 * 2 + t
                            for k in range(K2):
                                last = nc.tensor.matmul(psR[:, j % 2, t * 2 * SUB:(t + 1) * 2 * SUB],
                                                        w_root[:, k, tile * P:(tile + 1) * P],
                                                        xnT[:, k, bass.ds(i * (U * SUB) + j // 2 * (2 * SUB), 2 * SUB)],
                                                        start=(k == 0), stop=(k == K2 - 1))
                        last.then_inc(root_ready, 1)
                    if j >= 3:
                        a = j - 3
                        pe.wait_ge(vx_ready, PRE + i * U + a + 1)
                        pe.wait_ge(kphi_ready, PRE + i * U + a + 1)
                        for h in range(K2):
                            last = nc.tensor.matmul(psA[:, h, 0:VE], kphi[:, a % 2, h * P:(h + 1) * P],
                                                    vx[:, a % 2, h, :], start=False, stop=False)
                        last.then_inc(acc_done, 1)
            for h in range(K2):
                last = nc.tensor.matmul(psA[:, h, 0:VE], zero[:, 0:P], zero[:], start=False, stop=True)
            last.then_inc(sums_done, 1)
            for sg in range(NSUB, KV_SG):
                sum_edges(sg, sg - NSUB, ITERS * 2 + 1, sg % 2)
            pe.wait_ge(root_saved, PRE + NSUB)
            pe.wait_ge(kvm_ready, 4)
            for h in range(K2):
                last = nc.tensor.transpose(psT[:, h * P:(h + 1) * P], kvm[:, h, :], ident[:])
            last.then_inc(kvmT_ps, 1)
            pe.wait_ge(kvmT_sb, 1)
            for h in range(K2):
                last = nc.tensor.matmul(psKV[:, 0, h * D:(h + 1) * D], kvmT[:, h, :], wo[:, h, :], start=True, stop=True)
            last.then_inc(kvwo_ps, 1)


BQ, G1, B1LN, B1 = 0, 2, 4, 6
R_BO, R_G1, R_G2, R_LN1B, R_B2, R_LN2B, R_BFC = range(7)

def mix_order(ns, first=False, last=False):
    plan = """t0 E ln20 t1 E ln21 w10 q0 w11 E norm20 norm21 qphi0 q1 w12 E qphi1 den0 w13 out0 E
              w14 den1 divide0 w15 E divide1 w16 w17 E residual0 residual1 out1 wo0 wo1 wo_sum0 E wo_sum1 ln10
              w20 E ln11 norm10 norm11 w21 E w2_sum0 w22 E w23 E w2_sum1"""
    of_last = ("ln2", "norm2", "out")
    of_next = ("q", "qphi", "den", "divide", "wo", "wo_sum", "ln1", "norm1")
    beyond = (("t", 1), ("residual", 1), ("w2", 2), ("w2", 3), ("w2_sum", 1)) if ns < GS else ()
    order = []
    s = 0
    for word in plan.split():
        what, part = word[:-1], int(word[-1]) if word != "E" else 0
        if word == "E":
            order.extend([("ag", s), ("hot", s), ("add", s)])
            s += 1
        elif not (first and what in of_last or last and what in of_next or (what, part) in beyond):
            order.append((what, part))
    assert s == SGI
    return order


def product_positions(order):
    return {step: n for n, step in enumerate(step for step in order if step[0] in ("w1", "q", "den"))}


def mix_phase(nc, io, sb, psum, sem, xnT, accT, ident, src_t, dst_rel, base_i, iota_w,
              qdiv, kvwo, wq, w1, w2, colb, rows, xn_dram, s1_dram):
    F = 3
    NP = GS // 2
    FPG = 2 * K2 + FF // P
    FIRST = 2 * K2
    assert FPG % F == 0
    with ExitStack() as ctx:
        ring = sb(ctx, "ring", [P, RING, CPS, 2 * D], F16)
        stage = sb(ctx, "stage", [P, 2, HALF * CPS], I32)
        oh = sb(ctx, "oh", [P, OH, CPS, W], F16)
        ea = sb(ctx, "ea", [P, K2, GN])
        eb = sb(ctx, "eb", [P, K2, GN])
        qphi = sb(ctx, "qphi", [P, K2, GN])
        xng = sb(ctx, "xng", [SUB, GS, D])
        ya = sb(ctx, "ya", [SUB, GS, D])
        yr = sb(ctx, "yr", [SUB, GS, D])
        yb = sb(ctx, "yb", [SUB, GS, D])
        x1T = sb(ctx, "x1T", [P, K2, GN])
        ffh = sb(ctx, "ffh", [P, FF // P, GN])
        st = sb(ctx, "st2", [SUB, 2, GS, 6])
        mv = sb(ctx, "mv2", [SUB, 2, GS, 2])
        var = sb(ctx, "var2", [SUB, 2, GS])
        rstd = sb(ctx, "rstd2", [SUB, 2, GS])
        shift = sb(ctx, "shift2", [SUB, 2, GS])
        tmp = sb(ctx, "tmp2", [SUB, 2, GS])
        psF = psum(ctx, "psF", [P, F, 512])
        psN = psum(ctx, "psN", [P, 2, 2, D])
        psX = psum(ctx, "psX", [P, K2, 2 * P])
        psG = psum(ctx, "psG", [P, 2, 512])
        mstep = sem(ctx, "mstep")
        late_step = sem(ctx, "late_step")
        stats_taken = sem(ctx, "mstep_stats_taken")
        rows_ready = sem(ctx, "rows_ready")
        bank_zeroed = sem(ctx, "bank_zeroed")
        staged = sem(ctx, "staged")
        slot_taken = sem(ctx, "slot_taken")
        gathered = [sem(ctx, f"gathered{r}") for r in range(RING)]
        oh_ready = sem(ctx, "oh_ready")
        ag_ready = sem(ctx, "ag_ready")
        ag_added = sem(ctx, "ag_added")
        xn_in = sem(ctx, "xn_in")
        s1_out = sem(ctx, "s1_out")
        s1_stored = sem(ctx, "s1_stored")
        f_ready = sem(ctx, "f_ready")
        f_saved = sem(ctx, "f_saved")
        qphi_ready = sem(ctx, "qphi_ready")
        divided = sem(ctx, "divided")
        qscaled = sem(ctx, "qscaled")
        wo_ready = sem(ctx, "wo_ready")
        wo_saved = sem(ctx, "wo_saved")
        ln1_ready = sem(ctx, "ln1_ready")
        x1_ready = sem(ctx, "x1_ready")
        residual_ready = sem(ctx, "residual_ready")
        x_t = sem(ctx, "x_t")
        x1T_ready = sem(ctx, "x1T_ready")
        w2_ready = sem(ctx, "w2_ready")
        w2_saved = sem(ctx, "w2_saved")
        ln2_ready = sem(ctx, "ln2_ready")
        norm2_ready = sem(ctx, "norm2_ready")
        s1_ready = sem(ctx, "s1_ready")
        block = ctx.enter_context(nc.Block())

        @block.sync
        def _(sp):
            def load(g, ns):
                sp.wait_ge(wo_saved, PRE + g * NP)
                sp.dma_start(xng[:, 0:ns, :], xn_dram[bass.ds(g * GN, ns * SUB), :].rearrange("(j p) d -> p j d", p=SUB)
                             ).then_inc(xn_in, 16)

            def store(g, ns):
                sp.wait_ge(s1_ready, PRE + g * NP + ns // 2)
                sp.dma_start(s1_dram[bass.ds(g * GN, ns * SUB), :].rearrange("(j p) d -> p j d", p=SUB),
                             yb[:, 0:ns, :]).then_inc(s1_out, 16)
                sp.wait_ge(s1_out, g * 16 + 16)
                sp.sem_inc(s1_stored, 1)

            load(0, GS)
            load(1, GS)
            with sp.Fori(1, GROUPS - 1) as g:
                load(g + 1, GS)
                store(g - 1, GS)
            load(GROUPS, TAIL)
            store(GROUPS - 2, GS)
            store(GROUPS - 1, GS)
            store(GROUPS, TAIL)

        @block.gpsimd
        def _(pool):
            def body(g):
                for a in range(2):
                    pool.wait_ge(ag_ready, PRE + g * SGI + (a + 1) * HALF - SGI)
                    pool.tensor_copy(stage[:, a, :], src_t[:, bass.ds(g * (SGI * CPS) + (KV_SG + a * HALF) * CPS, HALF * CPS)]
                                     ).then_inc(staged, 1)
                    pool.wait_ge(staged, g * 2 + a + 1)
                    for h in range(HALF):
                        s = a * HALF + h
                        r = s % RING
                        pool.wait_ge(ag_ready, PRE + g * SGI + s + 1 - RING)
                        pool.sem_inc(slot_taken, 1)
                        for c in range(CPS):
                            col = h * CPS + c
                            pool.indirect_dma_start(
                                out=ring[:, r, c, :], out_offset=None, in_=io["table_dram"][:, :],
                                in_offset=bass.IndirectOffsetOnAxis(ap=stage[:, a, col:col + 1], axis=0),
                            ).then_inc(gathered[r], 16)

            with pool.Fori(0, GROUPS + 1) as g:
                body(g)

        @block.scalar
        def _(act):
            act.sem_inc(f_saved, PRE)
            act.sem_inc(x1T_ready, PRE)
            act.sem_inc(x1_ready, PRE)
            act.sem_inc(norm2_ready, PRE)

            def queries(g, s, pos, bank):
                act.wait_ge(f_ready, PRE + pos + 1)
                act.wait_ge(qscaled, PRE + g * K2 + s + 1 - K2)
                nc.scalar.activation(ea[:, s, :], psF[:, bank, 0:GN], ACT.Exp, bias=colb[:, BQ + s:BQ + s + 1])
                nc.scalar.activation(eb[:, s, :], psF[:, bank, 0:GN], ACT.Relu, bias=colb[:, BQ + s:BQ + s + 1]
                                     ).then_inc(f_saved, 1)

            def divisors(g, s, pos, bank):
                act.wait_ge(f_ready, PRE + pos + 1)
                act.wait_ge(qphi_ready, PRE + g * K2 + s + 1)
                nc.scalar.activation(eb[:, s, :], psF[:, bank, 0:GN], ACT.Copy, bias=1e-6).then_inc(f_saved, 1)

            def normalize(y, which, p):
                for j in (2 * p, 2 * p + 1):
                    last = nc.scalar.activation(y[:, j, :], y[:, j, :], ACT.Identity, scale=rstd[:, which, j:j + 1],
                                                bias=shift[:, which, j:j + 1])
                return last

            def first_norm(g, p):
                act.wait_ge(ln1_ready, PRE + g + 1)
                normalize(ya, 0, p).then_inc(x1_ready, 1)

            def second_norm(g, p):
                act.wait_ge(ln2_ready, PRE + g + 1)
                normalize(yb, 1, p).then_inc(norm2_ready, 1)

            for s in range(K2):
                queries(0, s, s, s % F)
            for s in range(K2):
                divisors(0, s, K2 + s, (K2 + s) % F)
            for p in range(NP):
                first_norm(0, p)

            def body(g, ns, **place):
                n = ns * SUB
                order = mix_order(ns, **place)
                at = product_positions(order)
                for what, s in order:
                    pos, bank = (g * FPG + FIRST + at[what, s], (FIRST + at[what, s]) % F) if (what, s) in at else (None, None)
                    if what == "q":
                        queries(g + 1, s, pos, bank)
                    elif what == "den":
                        divisors(g + 1, s, pos, bank)
                    elif what == "t":
                        act.wait_ge(x_t, PRE + g * NP + s + 1)
                        act.wait_ge(f_ready, PRE + g * FPG + FIRST)
                        for k in range(K2):
                            last = nc.scalar.activation(
                                x1T[:, k, s * (2 * SUB):(s + 1) * (2 * SUB)].rearrange("p (j n) -> p j n", j=2),
                                psX[:, k, :].rearrange("p (j n) -> p j n", j=2)[:, :, 0:SUB], ACT.Identity,
                                scale=colb[:, G1 + k:G1 + k + 1], bias=colb[:, B1LN + k:B1LN + k + 1])
                        last.then_inc(x1T_ready, 1)
                    elif what == "w1":
                        act.wait_ge(f_ready, PRE + pos + 1)
                        if s == 0:
                            act.wait_ge(w2_ready, PRE + g * NP)
                        nc.scalar.activation(ffh[:, s, 0:n], psF[:, bank, 0:n], ACT.Relu,
                                             bias=colb[:, B1 + s:B1 + s + 1]).then_inc(f_saved, 1)
                    elif what == "norm1":
                        first_norm(g + 1, s)
                    elif what == "norm2":
                        second_norm(g - 1, s)

            body(0, GS, first=True)
            with act.Fori(1, GROUPS) as g:
                body(g, GS)
            body(GROUPS, TAIL, last=True)
            for p in range(TAIL // 2):
                second_norm(GROUPS, p)

        @block.vector
        def _(dve):
            dve.sem_inc(ag_added, PRE)
            dve.sem_inc(oh_ready, PRE)
            dve.sem_inc(qphi_ready, PRE)
            dve.sem_inc(qscaled, PRE)
            dve.sem_inc(wo_saved, PRE)
            dve.sem_inc(ln1_ready, PRE)
            dve.sem_inc(w2_saved, PRE)
            dve.sem_inc(ln2_ready, PRE)
            dve.sem_inc(residual_ready, PRE)
            dve.sem_inc(s1_stored, PRE)
            dve.sem_inc(s1_ready, PRE)
            nc.vector.tensor_tensor(rows[:, R_LN1B, :], rows[:, R_LN1B, :], rows[:, R_B2, :], ALU.add).then_inc(rows_ready, 1)
            nc.vector.tensor_tensor(rows[:, R_LN2B, :], rows[:, R_LN2B, :], rows[:, R_BFC, :], ALU.add).then_inc(rows_ready, 1)
            nc.vector.memset(psG[:, LAG, :], 0.0).then_inc(bank_zeroed, 1)
            dve.wait_ge(rows_ready, 2)
            dve.wait_ge(bank_zeroed, 1)

            def pair(t, p):
                return t[:, 2 * p:2 * p + 2, :]

            def row(r):
                return rows[0:SUB, r:r + 1, :].to_broadcast([SUB, 2, D])

            def norm(step, which, ns, part, ready=None):
                m, v, y, t = mv[:, which, 0:ns, 0], var[:, which, 0:ns], rstd[:, which, 0:ns], tmp[:, which, 0:ns]
                if part == 0:
                    dve.sem_inc(stats_taken, 1)
                    for j in range(ns):
                        step.start(nc.vector.bn_aggr(mv[:, which, j, :], st[:, which, j, :]))
                    step.wait()
                    step(nc.vector.tensor_scalar(v, mv[:, which, 0:ns, 1], EPS, None, ALU.add))
                    rsqrt_guess(nc, step, v, y, t)
                    rsqrt_newton(nc, step, v, y, t, 1)
                else:
                    rsqrt_newton(nc, step, v, y, t, 2)
                    nc.vector.scalar_tensor_tensor(out=shift[:, which, 0:ns], in0=m, scalar=-1.0, in1=y,
                                                   op0=ALU.mult, op1=ALU.mult).then_inc(ready, 1)

            def out(step, g, s):
                dve.wait_ge(norm2_ready, PRE + g * NP + s + 1)
                step(nc.vector.tensor_tensor(pair(yb, s), pair(yb, s), row(R_G2), ALU.mult))
                nc.vector.tensor_tensor(pair(yb, s), pair(yb, s), row(R_LN2B), ALU.add).then_inc(s1_ready, 1)

            def one_hot(sg, slot):
                dve.wait_ge(ag_ready, PRE + sg + 1 - OH)
                nc.vector.tensor_tensor(
                    oh[:, slot, :, :],
                    dst_rel[:, bass.ds(sg * CPS + KV_SG * CPS, CPS)].rearrange("p (c o) -> p c o", o=1).to_broadcast([P, CPS, W]),
                    iota_w[:].rearrange("p (o w) -> p o w", o=1).to_broadcast([P, CPS, W]),
                    ALU.is_equal).then_inc(oh_ready, 1)

            def load_bases(turn, count):
                _, bases = nc.values_load_multi_w_load_instructions(
                    base_i[0:1, bass.ds(turn + KV_SG, count)], engines=[mybir.EngineType.DVE], min_val=0, max_val=N - 1)
                return bases

            def add_window(turn, bank, base):
                dve.wait_ge(ag_ready, PRE + turn + 1 - LAG)
                dve.wait_ge(ag_added, PRE + turn)
                win = accT[:, :, bass.ds(base, W)]
                nc.vector.tensor_tensor(win, win, psG[:, bank, 0:K2 * W].rearrange("p (k w) -> p k w", k=K2),
                                        ALU.add).then_inc(ag_added, 1)

            def queries(g, s, pos):
                dve.wait_ge(f_saved, PRE + pos + 1)
                dve.wait_ge(wo_ready, PRE + g * NP)
                nc.vector.scalar_tensor_tensor(out=qphi[:, s, :], in0=ea[:, s, :], scalar=1.0, in1=eb[:, s, :],
                                               op0=ALU.min, op1=ALU.add).then_inc(qphi_ready, 1)

            def divide(g, s, pos):
                dve.wait_ge(f_saved, PRE + pos + 1)
                nc.vector.reciprocal(ea[:, s, :], eb[:, s, :]).then_inc(divided, 1)
                dve.wait_ge(divided, g * K2 + s + 1)
                nc.vector.tensor_tensor(qphi[:, s, :], qphi[:, s, :], ea[:, s, :], ALU.mult).then_inc(qscaled, 1)

            def attention_sum(step, g, s):
                dve.wait_ge(wo_ready, PRE + g * NP + s + 1)
                dve.wait_ge(x_t, PRE + g * NP)
                nc.vector.tensor_tensor(pair(ya, s), psN[0:SUB, s, :, :], pair(xng, s), ALU.add).then_inc(wo_saved, 1)
                dve.wait_ge(wo_saved, PRE + g * NP + s + 1)
                step(nc.vector.tensor_tensor(pair(ya, s), pair(ya, s), row(R_BO), ALU.add))
                for j in (2 * s, 2 * s + 1):
                    step.start(nc.vector.bn_stats(st[:, 0, j, :], ya[:, j, :]))
                step.wait()

            ATTENTION = (NP + GS) + (GS + 1 + RSQRT_STEPS)
            PER = ATTENTION + (NP + GS)
            PER_LATE = (GS + 1 + RSQRT_STEPS) + NP
            for s in range(LEAD):
                one_hot(s, s)
            for s in range(K2):
                queries(0, s, s)
            for s in range(K2):
                divide(0, s, K2 + s)
            step = Chain(dve, mstep, 0, ATTENTION)
            dve.wait_ge(xn_in, 16)
            for p in range(NP):
                attention_sum(step, 0, p)
            norm(step, 0, GS, 0)
            norm(step, 0, GS, 1, ln1_ready)
            step.end()

            def body(g, ns, **place):
                step = Chain(dve, mstep, ATTENTION + g * PER, None if "last" in place else PER)
                late = Chain(dve, late_step, (g - 1) * PER_LATE, PER_LATE)
                order = mix_order(ns, **place)
                at = product_positions(order)
                for what, s in order:
                    if what == "hot":
                        one_hot(g * SGI + s + LEAD, (s + LEAD) % OH)
                    elif what == "add":
                        if s % 4 == 0:
                            bases = load_bases(g * SGI + s, 4)
                        add_window(g * SGI + s, (s - LAG) % 2, bases[s % 4])
                    elif what == "qphi":
                        queries(g + 1, s, g * FPG + FIRST + at["q", s])
                    elif what == "divide":
                        divide(g + 1, s, g * FPG + FIRST + at["den", s])
                    elif what == "wo_sum":
                        dve.wait_ge(xn_in, g * 16 + 32)
                        attention_sum(step, g + 1, s)
                    elif what == "ln1":
                        norm(step, 0, GS, s, ln1_ready)
                    elif what == "residual":
                        dve.wait_ge(x1_ready, PRE + g * NP + s + 1)
                        step(nc.vector.tensor_tensor(pair(yr, s), pair(ya, s), row(R_G1), ALU.mult))
                        nc.vector.tensor_tensor(pair(yr, s), pair(yr, s), row(R_LN1B), ALU.add).then_inc(residual_ready, 1)
                    elif what == "w2_sum":
                        dve.wait_ge(residual_ready, PRE + g * NP + s + 1)
                        dve.wait_ge(s1_stored, PRE + g)
                        dve.wait_ge(w2_ready, PRE + g * NP + s + 1)
                        nc.vector.tensor_tensor(pair(yb, s), pair(yr, s), psN[0:SUB, s, :, :], ALU.add
                                                ).then_inc(w2_saved, 1)
                        dve.wait_ge(w2_saved, PRE + g * NP + s + 1)
                        for j in (2 * s, 2 * s + 1):
                            step.start(nc.vector.bn_stats(st[:, 1, j, :], yb[:, j, :]))
                        step.wait()
                    elif what == "ln2":
                        norm(late, 1, GS, s, ln2_ready)
                    elif what == "out":
                        out(late, g - 1, s)
                step.end()
                if "first" not in place:
                    late.end()

            body(0, GS, first=True)
            with dve.Fori(1, GROUPS) as g:
                body(g, GS)
            body(GROUPS, TAIL, last=True)
            for turn in range(NSG - KV_SG, NSG - KV_SG + LAG):
                add_window(turn, (turn - LAG) % 2, load_bases(turn, 1)[0])
            late = Chain(dve, late_step, GROUPS * PER_LATE, None)
            norm(late, 1, TAIL, 0)
            norm(late, 1, TAIL, 1, ln2_ready)
            for s in range(TAIL // 2):
                out(late, GROUPS, s)

        @block.tensor
        def _(pe):
            pe.sem_inc(f_ready, PRE)
            pe.sem_inc(wo_ready, PRE)
            pe.sem_inc(w2_ready, PRE)
            pe.sem_inc(x_t, PRE)
            pe.sem_inc(ag_ready, PRE)

            def queries(g, s, pos, bank):
                pe.wait_ge(f_saved, PRE + pos + 1 - F)
                for k in range(K2):
                    last = nc.tensor.matmul(psF[:, bank, 0:GN], wq[:, k, s * P:(s + 1) * P],
                                            xnT[:, k, bass.ds(g * GN, GN)], start=(k == 0), stop=(k == K2 - 1))
                last.then_inc(f_ready, 1)

            def divisors(g, s, pos, bank):
                pe.wait_ge(f_saved, PRE + pos + 1 - F)
                pe.wait_ge(qphi_ready, PRE + g * K2 + s + 1)
                nc.tensor.matmul(psF[:, bank, 0:GN], qdiv[:, s, :], qphi[:, s, :],
                                 start=True, stop=True).then_inc(f_ready, 1)

            def attention_out(g, s):
                pe.wait_ge(qscaled, PRE + g * K2 + K2)
                pe.wait_ge(w2_saved, PRE + g * NP + s + 1 - 2 * NP)
                for j in range(2):
                    for k in range(K2):
                        cut = (2 * s + j) * SUB
                        last = nc.tensor.matmul(psN[0:SUB, s, j, :], qphi[:, k, cut:cut + SUB], kvwo[:, k, :],
                                                start=(k == 0), stop=(k == K2 - 1))
                last.then_inc(wo_ready, 1)

            for s in range(K2):
                queries(0, s, s, s % F)
            for s in range(K2):
                divisors(0, s, K2 + s, (K2 + s) % F)
            for p in range(NP):
                attention_out(0, p)

            def body(g, ns, **place):
                n = ns * SUB
                order = mix_order(ns, **place)
                at = product_positions(order)
                for what, s in order:
                    pos, bank = (g * FPG + FIRST + at[what, s], (FIRST + at[what, s]) % F) if (what, s) in at else (None, None)
                    if what == "q":
                        queries(g + 1, s, pos, bank)
                    elif what == "den":
                        divisors(g + 1, s, pos, bank)
                    elif what == "wo":
                        attention_out(g + 1, s)
                    elif what == "t":
                        pe.wait_ge(x1_ready, PRE + g * NP + s + 1)
                        pe.wait_ge(x1T_ready, PRE + g * NP + s)
                        for j in range(2):
                            for k in range(K2):
                                last = nc.tensor.transpose(psX[:, k, j * P:j * P + SUB], ya[:, 2 * s + j, k * P:(k + 1) * P],
                                                           ident[0:SUB, 0:SUB])
                        last.then_inc(x_t, 1)
                    elif what == "w1":
                        pe.wait_ge(x1T_ready, PRE + g * NP + ns // 2)
                        pe.wait_ge(f_saved, PRE + pos + 1 - F)
                        for k in range(K2):
                            last = nc.tensor.matmul(psF[:, bank, 0:n], w1[:, k, s * P:(s + 1) * P], x1T[:, k, 0:n],
                                                    start=(k == 0), stop=(k == K2 - 1))
                        last.then_inc(f_ready, 1)
                    elif what == "w2":
                        p = s // 2
                        if s % 2 == 0:
                            pe.wait_ge(f_saved, PRE + g * FPG + FIRST + at["w1", FF // P - 1] + 1)
                            pe.wait_ge(w2_saved, PRE + g * NP + p + 1 - NP)
                            if "last" not in place:
                                pe.wait_ge(wo_saved, PRE + (g + 1) * NP + p + 1)
                        for k in range(FF // P):
                            last = nc.tensor.matmul(psN[0:SUB, p, s % 2, :], ffh[:, k, s * SUB:(s + 1) * SUB],
                                                    w2[:, k, :], start=(k == 0), stop=(k == FF // P - 1))
                        if s % 2:
                            last.then_inc(w2_ready, 1)
                    elif what == "ag":
                        pe.wait_ge(oh_ready, PRE + g * SGI + s + 1)
                        pe.wait_ge(ag_added, PRE + g * SGI + s + LAG - 1)
                        pe.wait_ge(gathered[s % RING], (g * (SGI // RING) + s // RING + 1) * (16 * CPS))
                        for k in range(K2):
                            for c in range(CPS):
                                for part in range(2):
                                    cut = part * D + k * P
                                    last = nc.tensor.matmul(psG[:, s % 2, k * W:(k + 1) * W], ring[:, s % RING, c, cut:cut + P],
                                                            oh[:, s % OH, c, :], start=(c + part == 0), stop=(c + part == CPS))
                        last.then_inc(ag_ready, 1)

            body(0, GS, first=True)
            with pe.Fori(1, GROUPS) as g:
                body(g, GS)
            body(GROUPS, TAIL, last=True)


def rest_phase(nc, io, sb, psum, sem, accT, src_t, iota_w, flag_i, w_rel, w_ih, w_fc, cols):
    WINS = -(-N // W)
    with ExitStack() as ctx:
        dst_rest = sb(ctx, "rest_dst", [P, NCH])
        rows4 = sb(ctx, "rest_rows", [P, CPS, 2 * D], F16)
        dst_in = sem(ctx, "rest_dst_in")
        pieces = [(f"raw_rel{k}", io["w_rel"][:, k, :], w_rel, k) for k in range(K2)]
        pieces += [(f"raw_ih{k}", io["w_ih"][:, k, :], w_ih, k) for k in range(DH // P)]
        raw = [sb(ctx, name, [P, src.shape[-1]]) for name, src, _, _ in pieces]
        raw_in = [sem(ctx, f"{name}_in") for name, _, _, _ in pieces]
        small_in = sem(ctx, "gnn_small_in")
        w_high = sem(ctx, "w_high_ready")
        idx = sb(ctx, "rest_idx", [P, CPS], I32)
        rel = sb(ctx, "rest_rel", [P, CPS])
        hot = sb(ctx, "rest_hot", [P, CPS, W], F16)
        psR = psum(ctx, "psR", [P, K2, W])
        idx_ready = sem(ctx, "r_idx_ready")
        rest_in = sem(ctx, "rest_in")
        rest_begun = sem(ctx, "rest_begun")
        rel_ready = sem(ctx, "rel_ready")
        hot_ready = sem(ctx, "hot_ready")
        r_summed = sem(ctx, "r_summed")
        r_added = sem(ctx, "r_added")
        block = ctx.enter_context(nc.Block())

        def some(eng):
            return eng.If(eng.value_load(flag_i[0:1, 0:1], min_val=0, max_val=1))

        @block.gpsimd
        def _(pool):
            with some(pool):
                with pool.Fori(0, NSG) as s:
                    pool.wait_ge(r_added, PRE + s * WINS)
                    pool.tensor_copy(idx[:], src_t[:, bass.ds(s * CPS, CPS)]).then_inc(idx_ready, 1)
                    pool.wait_ge(idx_ready, s + 1)
                    pool.sem_inc(rest_begun, 1)
                    for c in range(CPS):
                        pool.indirect_dma_start(out=rows4[:, c, :], out_offset=None, in_=io["table_dram"][:, :],
                                                in_offset=bass.IndirectOffsetOnAxis(ap=idx[:, c:c + 1], axis=0),
                                                ).then_inc(rest_in, 16)
                    pool.wait_ge(rest_in, (s + 1) * (16 * CPS))

        @block.sync
        def _(sp):
            sp.dma_start(dst_rest[:], io["rest_dram"]).then_inc(dst_in, 16)
            for n, (_, src, _, _) in enumerate(pieces):
                sp.dma_start(raw[n][:], src).then_inc(raw_in[n], 16)
            sp.dma_start(cols[:], io["gnn_cols"]).then_inc(small_in, 16)
            sp.dma_start(w_fc[:], io["w_fc"]).then_inc(small_in, 16)
            sp.wait_ge(small_in, 32)
            sp.wait_ge(dst_in, 16)

        @block.scalar
        def _(act):
            for n, (_, _, dst, k) in enumerate(pieces):
                act.wait_ge(raw_in[n], 16)
                nc.scalar.copy(dst[:, 0, k, :], raw[n][:]).then_inc(w_high, 1)

        @block.vector
        def _(dve):
            for n, (_, _, dst, k) in enumerate(pieces):
                dve.wait_ge(raw_in[n], 16)
                dve.wait_ge(w_high, n + 1)
                nc.vector.tensor_tensor(dst[:, 1, k, :], raw[n][:], dst[:, 0, k, :].bitcast(F32), ALU.subtract)
            dve.wait_ge(small_in, 32)
            BIASES = 3 * DH // P
            nc.vector.tensor_tensor(cols[:, DH // P:DH // P + BIASES], cols[:, DH // P:DH // P + BIASES],
                                    cols[:, DH // P + BIASES:DH // P + 2 * BIASES], ALU.add)
            dve.wait_ge(dst_in, 16)
            dve.sem_inc(r_added, PRE)
            with some(dve):
                with dve.Fori(0, NSG) as s:
                    nc.vector.tensor_copy(rel[:], dst_rest[:, bass.ds(s * CPS, CPS)]).then_inc(rel_ready, 1)
                    with dve.Fori(0, WINS) as w:
                        dve.wait_ge(rel_ready, s * (WINS + 1) + w + 1)
                        nc.vector.tensor_tensor(hot[:], rel[:].rearrange("p (c o) -> p c o", o=1).to_broadcast([P, CPS, W]),
                                                iota_w[:].rearrange("p (o w) -> p o w", o=1).to_broadcast([P, CPS, W]),
                                                ALU.is_equal).then_inc(hot_ready, 1)
                        dve.wait_ge(hot_ready, s * WINS + w + 1)
                        nc.vector.tensor_scalar(rel[:], rel[:], -float(W), None, ALU.add).then_inc(rel_ready, 1)
                        dve.wait_ge(r_summed, s * WINS + w + 1)
                        win = accT[:, :, bass.ds(w * W, W)]
                        nc.vector.tensor_tensor(win, win, psR[:], ALU.add).then_inc(r_added, 1)
                        dve.wait_ge(r_added, PRE + s * WINS + w + 1)

        @block.tensor
        def _(pe):
            with some(pe):
                with pe.Fori(0, NSG) as s:
                    with pe.Fori(0, WINS) as w:
                        pe.wait_ge(rest_in, (s + 1) * (16 * CPS))
                        pe.wait_ge(hot_ready, s * WINS + w + 1)
                        pe.wait_ge(r_added, PRE + s * WINS + w)
                        for k in range(K2):
                            for c in range(CPS):
                                for part in range(2):
                                    cut = part * D + k * P
                                    last = nc.tensor.matmul(psR[:, k, :], rows4[:, c, cut:cut + P], hot[:, c, :],
                                                            start=(c + part == 0), stop=(c + part == CPS))
                        last.then_inc(r_summed, 1)


PARTS = ((0, 0), (0, 1), (1, 0))


def gnn_phase(nc, io, sb, psum, sem, accT, ident, zsum, z_mv, w_rel, w_ih, w_fc, cols, s1_dram, x2_dram):
    F = 4
    NP = GS // 2
    HM = DH // P
    GATES = 3
    FPG = HM + GATES * HM
    with ExitStack() as ctx:
        root = sb(ctx, "root_tile", [P, HM, GN])
        acc_s = sb(ctx, "acc_split", [P, 2, K2, GN], F32R)
        hx = sb(ctx, "hx", [P, 2, GN])
        h_s = sb(ctx, "h_split", [P, 2, HM, GN], F32R)
        gi = sb(ctx, "gi", [P, 2, GN])
        gg = sb(ctx, "gg", [P, 2, GN])
        go = sb(ctx, "go", [P, 2, GN])
        hl = sb(ctx, "hl", [P, HM, GN])
        s1g = sb(ctx, "s1g", [SUB, GS, D])
        xg = sb(ctx, "xg", [SUB, GS, D])
        x2 = sb(ctx, "x2", [SUB, GS, D])
        zz = sb(ctx, "zz", [SUB, GS, D])
        st = sb(ctx, "st3", [SUB, GS, 6])
        mv = sb(ctx, "mv3", [SUB, GS, 2])
        var = sb(ctx, "var3", [SUB, GS])
        rstd = sb(ctx, "rstd3", [SUB, GS])
        tmp = sb(ctx, "tmp3", [SUB, GS])
        psF = psum(ctx, "psF3", [P, F, 512])
        psN = psum(ctx, "psN3", [P, 2, 2, D])
        psX = psum(ctx, "psX3", [P, 2, K2, 2 * P])
        gstep = sem(ctx, "gstep")
        late_step = sem(ctx, "gnn_late_step")
        stats_taken = sem(ctx, "gstep_stats_taken")
        root_in = sem(ctx, "root_tile_in")
        s1_in = sem(ctx, "s1_in")
        x_in = sem(ctx, "gnn_x_in")
        base_ready = sem(ctx, "residual_sum_ready")
        x2_out = sem(ctx, "x2_out")
        x2_stored = sem(ctx, "x2_stored")
        high_ready = sem(ctx, "in_high_ready")
        split_ready = sem(ctx, "split_ready")
        f_ready = sem(ctx, "gf_ready")
        gate_saved = sem(ctx, "gate_saved")
        h_saved = sem(ctx, "h_saved")
        h_high = sem(ctx, "h_high")
        h_ready = sem(ctx, "h_ready")
        c_ready = sem(ctx, "c_ready")
        tc_ready = sem(ctx, "tc_ready")
        hl_ready = sem(ctx, "hl_ready")
        fc_ready = sem(ctx, "fc_ready")
        x2_ready = sem(ctx, "x2_ready")
        z_ready = sem(ctx, "z_ready")
        z_t = sem(ctx, "z_t")
        zT_saved = sem(ctx, "zT_saved")
        block = ctx.enter_context(nc.Block())

        def order(ns, first=False, last=False):
            late = {} if first else {-1: [("ln", 0), ("ln", 1), ("z", 0), ("z", 1)], 0: [("t", 0)], 1: [("t", 1), ("zsum", 0)],
                                     2: [("zsum", 1)]}
            out = late.get(-1, [])
            for m in range(HM + 1):
                if m < HM:
                    out = out + [("gate", (m, x)) for x in range(GATES)] + [("cell", m)]
                if m:
                    out = out + [("tanh", m - 1)]
                out = out + late.get(m, [])
                if m == 1 and not last:
                    out = out + [("split", 0)]
            if not last:
                for m in range(HM):
                    out = out + [("h", m), ("h_split", m)]
            return out + [(what, p) for p in range(ns // 2) for what in ("fc", "x2")]

        @block.sync
        def _(sp):
            def load_root(g, n):
                sp.wait_ge(h_saved, PRE + g * HM)
                sp.dma_start(root[:, :, 0:n], io["root_dram"][:, :, bass.ds(g * GN, n)]).then_inc(root_in, 16)

            def body(g, ns, next_n):
                if next_n:
                    load_root(g + 1, next_n)
                sp.wait_ge(x2_ready, PRE + g * NP)
                sp.dma_start(s1g[:, 0:ns, :], s1_dram[bass.ds(g * GN, ns * SUB), :].rearrange("(j p) d -> p j d", p=SUB)
                             ).then_inc(s1_in, 16)
                sp.dma_start(xg[:, 0:ns, :], io["x"][bass.ds(g * GN, ns * SUB), :].rearrange("(j p) d -> p j d", p=SUB)
                             ).then_inc(x_in, 16)
                sp.wait_ge(x2_ready, PRE + g * NP + ns // 2)
                sp.dma_start(x2_dram[bass.ds(g * GN, ns * SUB), :].rearrange("(j p) d -> p j d", p=SUB), x2[:, 0:ns, :]
                             ).then_inc(x2_out, 16)
                sp.wait_ge(x2_out, g * 16 + 16)
                sp.sem_inc(x2_stored, 1)

            load_root(0, GN)
            with sp.Fori(0, GROUPS - 1) as g:
                body(g, GS, GN)
            body(GROUPS - 1, GS, TAIL * SUB)
            body(GROUPS, TAIL, 0)

        @block.scalar
        def _(act):
            act.sem_inc(gate_saved, PRE)
            act.sem_inc(tc_ready, PRE)
            act.sem_inc(zT_saved, PRE)

            def save_z(g, s):
                act.wait_ge(z_t, PRE + g * NP + s + 1)
                for k in range(K2):
                    last = nc.scalar.copy(
                        accT[:, k, bass.ds(g * GN + s * (2 * SUB), 2 * SUB)].rearrange("p (j n) -> p j n", j=2),
                        psX[:, s % 2, k, :].rearrange("p (j n) -> p j n", j=2)[:, :, 0:SUB])
                last.then_inc(zT_saved, 1)

            def body(g, ns, **place):
                n = ns * SUB
                for what, s in order(ns, **place):
                    if what == "gate":
                        m, x = s
                        pos = HM + GATES * m + x
                        act.wait_ge(f_ready, PRE + g * FPG + pos + 1)
                        act.wait_ge(hl_ready, PRE + g * HM + m + 1 - 2)
                        dst = (gi, gg, go)[x]
                        nc.scalar.activation(dst[:, m % 2, 0:n], psF[:, pos % F, 0:n], (ACT.Sigmoid, ACT.Tanh, ACT.Sigmoid)[x],
                                             bias=cols[:, HM + x * HM + m:HM + x * HM + m + 1]).then_inc(gate_saved, 1)
                    elif what == "tanh":
                        act.wait_ge(c_ready, PRE + g * HM + s + 1)
                        nc.scalar.activation(gi[:, s % 2, 0:n], gi[:, s % 2, 0:n], ACT.Tanh).then_inc(tc_ready, 1)
                    elif what == "t":
                        save_z(g - 1, s)

            body(0, GS, first=True)
            with act.Fori(1, GROUPS) as g:
                body(g, GS)
            body(GROUPS, TAIL, last=True)
            for s in range(TAIL // 2):
                save_z(GROUPS, s)

        @block.vector
        def _(dve):
            dve.sem_inc(c_ready, PRE)
            dve.sem_inc(hl_ready, PRE)
            dve.sem_inc(x2_ready, PRE)
            dve.sem_inc(x2_stored, PRE)
            dve.sem_inc(z_ready, PRE)
            dve.sem_inc(split_ready, PRE)
            dve.sem_inc(h_ready, PRE)
            dve.sem_inc(h_saved, PRE)
            PER = GS
            PER_LATE = GS + 1 + RSQRT_STEPS

            def split_inputs(g):
                sums = accT[:, :, bass.ds(g * GN, GN)]
                dve.wait_ge(f_ready, PRE + (g - 1) * FPG + HM)
                nc.vector.tensor_copy(acc_s[:, 0, :, :], sums).then_inc(high_ready, 1)
                dve.wait_ge(high_ready, g + 1)
                nc.vector.tensor_tensor(acc_s[:, 1, :, :], sums, acc_s[:, 0, :, :].bitcast(F32), ALU.subtract
                                        ).then_inc(split_ready, 1)

            def split_hidden(g, m):
                x = hx[:, m % 2, :]
                dve.wait_ge(root_in, g * 16 + 16)
                dve.wait_ge(f_ready, PRE + g * FPG + m + 1)
                nc.vector.scalar_tensor_tensor(out=x, in0=psF[:, m % F, 0:GN], scalar=cols[:, m:m + 1], in1=root[:, m, :],
                                               op0=ALU.add, op1=ALU.add).then_inc(h_saved, 1)
                dve.wait_ge(h_saved, PRE + g * HM + m + 1)
                nc.vector.tensor_scalar(h_s[:, 0, m, :], x, 0.0, None, ALU.max).then_inc(h_high, 1)
                dve.wait_ge(h_high, g * HM + m + 1)
                nc.vector.scalar_tensor_tensor(out=h_s[:, 1, m, :], in0=x, scalar=0.0, in1=h_s[:, 0, m, :].bitcast(F32),
                                               op0=ALU.max, op1=ALU.subtract).then_inc(h_ready, 1)

            def norm(step, g, ns, part):
                v, y, t = var[:, 0:ns], rstd[:, 0:ns], tmp[:, 0:ns]
                if part == 0:
                    for j in range(ns):
                        step.start(nc.vector.bn_aggr(mv[:, j, :], st[:, j, :]))
                    step.wait()
                    step(nc.vector.tensor_scalar(v, mv[:, 0:ns, 1], EPS, None, ALU.add))
                    rsqrt_guess(nc, step, v, y, t)
                    rsqrt_newton(nc, step, v, y, t, 1)
                else:
                    rsqrt_newton(nc, step, v, y, t, 2)
                    nc.vector.tensor_copy(z_mv[:, bass.ds(g * GS, ns), 0], mv[:, 0:ns, 0])
                    nc.vector.tensor_copy(z_mv[:, bass.ds(g * GS, ns), 1], y)

            def make_z(g, s):
                dve.wait_ge(z_t, PRE + g * NP)
                for j in (2 * s, 2 * s + 1):
                    last = nc.vector.tensor_scalar(zz[:, j, :], x2[:, j, :], mv[:, j, 0:1], rstd[:, j:j + 1],
                                                   ALU.subtract, ALU.mult)
                last.then_inc(z_ready, 1)

            def sum_z(g, s):
                dve.wait_ge(zT_saved, PRE + g * NP + s + 1)
                nc.vector.tensor_reduce(zsum[:, :, bass.ds(g * NP + s, 1)].rearrange("p k o -> p (k o)"),
                                        accT[:, :, bass.ds(g * GN + s * (2 * SUB), 2 * SUB)], AX.X, ALU.add)

            def body(g, ns, **place):
                n = ns * SUB
                step = Chain(dve, gstep, g * PER, None if "last" in place else PER)
                late = Chain(dve, late_step, (g - 1) * PER_LATE, None if "first" in place else PER_LATE)
                for what, s in order(ns, **place):
                    if what == "split":
                        split_inputs(g + 1)
                    elif what == "h_split":
                        split_hidden(g + 1, s)
                    elif what == "cell":
                        dve.wait_ge(gate_saved, PRE + g * (GATES * HM) + GATES * s + 2)
                        nc.vector.tensor_tensor(gi[:, s % 2, 0:n], gi[:, s % 2, 0:n], gg[:, s % 2, 0:n],
                                                ALU.mult).then_inc(c_ready, 1)
                    elif what == "tanh":
                        dve.wait_ge(gate_saved, PRE + g * (GATES * HM) + GATES * s + 3)
                        dve.wait_ge(tc_ready, PRE + g * HM + s + 1)
                        dve.wait_ge(fc_ready, PRE + g * NP)
                        nc.vector.tensor_tensor(hl[:, s, 0:n], go[:, s % 2, 0:n], gi[:, s % 2, 0:n],
                                                ALU.mult).then_inc(hl_ready, 1)
                    elif what == "x2":
                        if s == 0:
                            dve.wait_ge(s1_in, g * 16 + 16)
                            dve.wait_ge(x_in, g * 16 + 16)
                            nc.vector.tensor_tensor(s1g[:, 0:ns, :], s1g[:, 0:ns, :], xg[:, 0:ns, :], ALU.add
                                                    ).then_inc(base_ready, 1)
                            dve.wait_ge(base_ready, g + 1)
                            dve.wait_ge(x2_stored, PRE + g)
                        dve.wait_ge(fc_ready, PRE + g * NP + s + 1)
                        nc.vector.tensor_tensor(x2[:, 2 * s:2 * s + 2, :], psN[0:SUB, s % 2, :, :], s1g[:, 2 * s:2 * s + 2, :],
                                                ALU.add).then_inc(x2_ready, 1)
                        dve.wait_ge(x2_ready, PRE + g * NP + s + 1)
                        for j in (2 * s, 2 * s + 1):
                            step.start(nc.vector.bn_stats(st[:, j, :], x2[:, j, :]))
                    elif what == "ln":
                        norm(late, g - 1, GS, s)
                    elif what == "z":
                        make_z(g - 1, s)
                    elif what == "zsum":
                        sum_z(g - 1, s)
                step.wait()
                dve.sem_inc(stats_taken, 1)
                step.end()
                if "first" not in place:
                    late.end()

            split_inputs(0)
            for m in range(HM):
                split_hidden(0, m)
            body(0, GS, first=True)
            with dve.Fori(1, GROUPS) as g:
                body(g, GS)
            body(GROUPS, TAIL, last=True)
            late = Chain(dve, late_step, GROUPS * PER_LATE, None)
            for part in range(2):
                norm(late, GROUPS, TAIL, part)
            for s in range(TAIL // 2):
                make_z(GROUPS, s)
                sum_z(GROUPS, s)

        @block.tensor
        def _(pe):
            pe.sem_inc(f_ready, PRE)
            pe.sem_inc(fc_ready, PRE)
            pe.sem_inc(z_t, PRE)

            def hidden(g, m):
                pe.wait_ge(split_ready, PRE + g + 1)
                pe.wait_ge(gate_saved, PRE + g * (GATES * HM) - F + m + 1)
                for k in range(K2):
                    for wp, xp in PARTS:
                        last = nc.tensor.matmul(psF[:, m % F, 0:GN], w_rel[:, wp, k, m * P:(m + 1) * P], acc_s[:, xp, k, :],
                                                start=(k == 0 and (wp, xp) == PARTS[0]),
                                                stop=(k == K2 - 1 and (wp, xp) == PARTS[-1]))
                last.then_inc(f_ready, 1)

            def transposes(g, s):
                pe.wait_ge(z_ready, PRE + g * NP + s + 1)
                pe.wait_ge(zT_saved, PRE + g * NP + s + 1 - 2)
                for j in range(2):
                    for k in range(K2):
                        last = nc.tensor.transpose(psX[:, s % 2, k, j * P:j * P + SUB],
                                                   zz[:, 2 * s + j, k * P:(k + 1) * P], ident[0:SUB, 0:SUB])
                last.then_inc(z_t, 1)

            def body(g, ns, **place):
                n = ns * SUB
                for what, s in order(ns, **place):
                    if what == "h":
                        hidden(g + 1, s)
                    elif what == "gate":
                        m, x = s
                        pos = HM + GATES * m + x
                        pe.wait_ge(h_ready, PRE + g * HM + HM)
                        pe.wait_ge(gate_saved, PRE + g * (GATES * HM) + max(0, pos + 1 - HM - F))
                        for k in range(HM):
                            for wp, xp in PARTS:
                                last = nc.tensor.matmul(psF[:, pos % F, 0:n], w_ih[:, wp, k, x * DH + m * P:x * DH + (m + 1) * P],
                                                        h_s[:, xp, k, 0:n], start=(k == 0 and (wp, xp) == PARTS[0]),
                                                        stop=(k == HM - 1 and (wp, xp) == PARTS[-1]))
                        last.then_inc(f_ready, 1)
                    elif what == "fc":
                        pe.wait_ge(hl_ready, PRE + g * HM + HM)
                        pe.wait_ge(x2_ready, PRE + g * NP + s + 1 - 2)
                        for j in range(2):
                            for k in range(HM):
                                cut = (2 * s + j) * SUB
                                last = nc.tensor.matmul(psN[0:SUB, s % 2, j, :], hl[:, k, cut:cut + SUB], w_fc[:, k, :],
                                                        start=(k == 0), stop=(k == HM - 1))
                        last.then_inc(fc_ready, 1)
                    elif what == "t":
                        transposes(g - 1, s)

            for m in range(HM):
                hidden(0, m)
            body(0, GS, first=True)
            with pe.Fori(1, GROUPS) as g:
                body(g, GS)
            body(GROUPS, TAIL, last=True)
            for s in range(TAIL // 2):
                transposes(GROUPS, s)


def route_phase(nc, io, sb, psum, sem, zsum, e1, e2, e1b, zb2):
    CAP = float(-(-N * 5 // (4 * NE)))
    HM = DH // P
    with ExitStack() as ctx:
        wr = sb(ctx, "wr", [P, K2, NE])
        br = sb(ctx, "br", [1, NE])
        ones = sb(ctx, "ones", [1, P])
        zm = sb(ctx, "zm", [P, K2])
        a = sb(ctx, "a", [1, NE])
        ex = sb(ctx, "ex", [1, NE])
        rw = sb(ctx, "rw", [1, NE])
        ld = sb(ctx, "ld", [1, NE])
        mx = sb(ctx, "mx", [1, 1])
        sm = sb(ctx, "sm", [1, 1])
        rs = sb(ctx, "rs", [1, 1])
        tv = sb(ctx, "tv", [1, NE])
        ti = sb(ctx, "ti", [1, NE], U32)
        wt = sb(ctx, "wt", [1, 2])
        wb = sb(ctx, "wb", [P, 2])
        b2 = sb(ctx, "b2", [P, 2, D])
        raw1 = sb(ctx, "raw1", [P, 2, K2, DH])
        psL = psum(ctx, "psL", [P, NE])
        psW = psum(ctx, "psW", [P, 2])
        r_in = sem(ctx, "route_in")
        rstep = sem(ctx, "rstep")
        zm_ready = sem(ctx, "zm_ready")
        lg_ready = sem(ctx, "lg_ready")
        arg_ready = sem(ctx, "arg_ready")
        exp_ready = sem(ctx, "exp_ready")
        top_ready = sem(ctx, "top_ready")
        wt_ready = sem(ctx, "wt_ready")
        wb_ready = sem(ctx, "wb_ready")
        wb_saved = sem(ctx, "wb_saved")
        e1_in = [sem(ctx, f"e1_in{n}") for n in range(2)]
        e1_high = sem(ctx, "e1_high")
        e_in = sem(ctx, "e_in")
        block = ctx.enter_context(nc.Block())

        @block.sync
        def _(sp):
            sp.dma_start(wr[:], io["ffn_wr"]).then_inc(r_in, 16)
            sp.dma_start(br[:], io["ffn_br"]).then_inc(r_in, 16)
            sp.wait_ge(top_ready, 1)
            for s in range(2):
                e = sp.value_load(ti[0:1, s:s + 1], min_val=0, max_val=NE - 1)
                rows = bass.ds(e * P, P)
                sp.dma_start(raw1[:, s, :, :], io["ffn_w1"][rows, :].rearrange("p (k f) -> p k f", k=K2)).then_inc(e1_in[s], 16)
                sp.dma_start(e2[:, s * HM:(s + 1) * HM, :], io["ffn_w2"][rows, :].rearrange("p (k f) -> p k f", k=HM)
                             ).then_inc(e_in, 16)
                sp.dma_start(e1b[:, s, :], io["ffn_b1"][rows, :]).then_inc(e_in, 16)
                sp.dma_start(b2[:, s, :], io["ffn_b2"][rows, :]).then_inc(e_in, 16)
            sp.wait_ge(e_in, 96)

        @block.scalar
        def _(act):
            for n in range(3):
                act.wait_ge(arg_ready, n + 1)
                width = 2 if n == 2 else NE
                nc.scalar.activation(ex[0:1, 0:width], a[0:1, 0:width], ACT.Exp, accum_out=sm[:]).then_inc(exp_ready, 1)
            for s in range(2):
                act.wait_ge(e1_in[s], 16)
                nc.scalar.copy(e1[:, 0, s, :, :], raw1[:, s, :, :]).then_inc(e1_high, 1)
            act.wait_ge(wb_saved, 1)
            act.wait_ge(e_in, 96)
            for s in range(2):
                nc.scalar.activation(e2[:, s * HM:(s + 1) * HM, :], e2[:, s * HM:(s + 1) * HM, :], ACT.Copy, scale=wb[:, s:s + 1])

        @block.vector
        def _(dve):
            step = Chain(dve, rstep, 0, None)
            step(nc.vector.memset(ones[:], 1.0))
            step(nc.vector.tensor_reduce(zm[:], zsum[:], AX.X, ALU.add))
            nc.vector.tensor_scalar(zm[:], zm[:], 1.0 / N, None, ALU.mult).then_inc(zm_ready, 1)
            dve.wait_ge(r_in, 32)
            dve.wait_ge(lg_ready, 1)
            step(nc.vector.tensor_tensor(rw[:], psL[0:1, :], br[:], ALU.add))

            def softmax(src, n, dst, width):
                step(nc.vector.tensor_reduce(mx[:], src, AX.X, ALU.max))
                nc.vector.tensor_scalar(a[0:1, 0:width], src, mx[:], None, ALU.subtract).then_inc(arg_ready, 1)
                dve.wait_ge(exp_ready, n)
                step(nc.vector.reciprocal(rs[:], sm[:]))
                return nc.vector.tensor_scalar(dst, ex[0:1, 0:width], rs[:], None, ALU.mult)

            step(softmax(rw[:], 1, rw[:], NE))
            step(nc.vector.tensor_scalar(ld[:], rw[:], float(N), None, ALU.mult))
            step(nc.vector.reciprocal(ld[:], ld[:]))
            step(nc.vector.tensor_scalar(ld[:], ld[:], CAP, 1.0, ALU.mult, ALU.min))
            step(nc.vector.tensor_tensor(rw[:], rw[:], ld[:], ALU.mult))
            step(softmax(rw[:], 2, rw[:], NE))
            step(nc.vector.max(tv[:], rw[:]))
            nc.vector.max_index(ti[:], tv[:], rw[:]).then_inc(top_ready, 1)
            softmax(tv[0:1, 0:2], 3, wt[:], 2).then_inc(wt_ready, 1)
            dve.wait_ge(wb_ready, 1)
            nc.vector.tensor_copy(wb[:], psW[:]).then_inc(wb_saved, 1)
            dve.wait_ge(wb_saved, 1)
            for s in range(2):
                dve.wait_ge(e1_in[s], 16)
                dve.wait_ge(e1_high, s + 1)
                nc.vector.tensor_tensor(e1[:, 1, s, :, :], raw1[:, s, :, :], e1[:, 0, s, :, :].bitcast(F32), ALU.subtract)
            dve.wait_ge(e_in, 96)
            step(nc.vector.tensor_scalar(zb2[:], b2[:, 0, :], wb[:, 0:1], None, ALU.mult))
            step(nc.vector.scalar_tensor_tensor(out=zb2[:], in0=b2[:, 1, :], scalar=wb[:, 1:2], in1=zb2[:],
                                                op0=ALU.mult, op1=ALU.add))

        @block.tensor
        def _(pe):
            pe.wait_ge(r_in, 32)
            pe.wait_ge(zm_ready, 1)
            for k in range(K2):
                last = nc.tensor.matmul(psL[0:1, :], zm[:, k:k + 1], wr[:, k, :], start=(k == 0), stop=(k == K2 - 1))
            last.then_inc(lg_ready, 1)
            pe.wait_ge(wt_ready, 1)
            nc.tensor.matmul(psW[:], ones[:], wt[:], start=True, stop=True).then_inc(wb_ready, 1)


def moe_phase(nc, io, sb, psum, sem, zT, z_mv, e1, e2, e1b, zb2, x2_dram):
    F = 4
    HM = DH // P
    TILES = 2 * HM
    NP = GS // 2
    BEHIND = 2
    with ExitStack() as ctx:
        gb = sb(ctx, "gb", [P, 2, D])
        z_s = sb(ctx, "z_split", [P, 2, K2, GN], F32R)
        hg = sb(ctx, "hg", [P, TILES, GN])
        x2 = sb(ctx, "x2m", [SUB, GS, D])
        y = sb(ctx, "ym", [SUB, GS, D])
        st = sb(ctx, "st4", [SUB, GS, 6])
        mv = sb(ctx, "mv4", [SUB, GS, 2])
        var = sb(ctx, "var4", [SUB, GS])
        rstd = sb(ctx, "rstd4", [SUB, GS])
        tmp = sb(ctx, "tmp4", [SUB, GS])
        psF = psum(ctx, "psF4", [P, F, 512])
        psN = psum(ctx, "psN4", [P, GS, 512])
        gb_in = sem(ctx, "gb_in")
        x2_in = sem(ctx, "x2_in")
        y_out = sem(ctx, "y_out")
        y_stored = sem(ctx, "y_stored")
        z_high = sem(ctx, "z_high")
        z_low = sem(ctx, "z_low")
        f_ready = sem(ctx, "mf_ready")
        f_saved = sem(ctx, "mf_saved")
        n_ready = sem(ctx, "mn_ready")
        n_saved = sem(ctx, "mn_saved")
        y_ready = sem(ctx, "y_ready")
        ystep = sem(ctx, "ystep")
        stats_taken = sem(ctx, "ystep_stats_taken")
        block = ctx.enter_context(nc.Block())

        @block.sync
        def _(sp):
            sp.dma_start(gb[:], io["ffn_gb"]).then_inc(gb_in, 16)

            def body(g, ns):
                sp.wait_ge(y_ready, PRE + g * NP)
                sp.dma_start(x2[:, 0:ns, :], x2_dram[bass.ds(g * GN, ns * SUB), :].rearrange("(j p) d -> p j d", p=SUB)
                             ).then_inc(x2_in, 16)
                sp.wait_ge(y_ready, PRE + g * NP + ns // 2)
                sp.dma_start(io["out"][bass.ds(g * GN, ns * SUB), :].rearrange("(j p) d -> p j d", p=SUB), y[:, 0:ns, :]
                             ).then_inc(y_out, 16)
                sp.wait_ge(y_out, g * 16 + 16)
                sp.sem_inc(y_stored, 1)

            with sp.Fori(0, GROUPS) as g:
                body(g, GS)
            body(GROUPS, TAIL)

        @block.scalar
        def _(act):
            act.sem_inc(f_saved, PRE)

            def z_highs(g, n):
                act.wait_ge(f_ready, PRE + g * TILES)
                nc.scalar.copy(z_s[:, 0, :, 0:n], zT[:, :, bass.ds(g * GN, n)]).then_inc(z_high, 1)

            def body(g, ns, next_ns):
                n = ns * SUB
                for m in range(TILES):
                    act.wait_ge(f_ready, PRE + g * TILES + m + 1)
                    if m == 0:
                        act.wait_ge(n_ready, PRE + g * GS)
                    nc.scalar.activation(hg[:, m, 0:n], psF[:, m % F, 0:n], ACT.Gelu, bias=e1b[:, m // HM, m % HM:m % HM + 1]
                                         ).then_inc(f_saved, 1)
                if next_ns:
                    z_highs(g + 1, next_ns * SUB)

            z_highs(0, GN)
            with act.Fori(0, GROUPS - 1) as g:
                body(g, GS, GS)
            body(GROUPS - 1, GS, TAIL)
            body(GROUPS, TAIL, 0)

        @block.vector
        def _(dve):
            dve.sem_inc(n_saved, PRE)
            dve.sem_inc(y_ready, PRE)
            dve.sem_inc(y_stored, PRE)
            PER = 2 * GS + GS + GS + 1 + RSQRT_STEPS + GS + 2 * NP
            dve.wait_ge(gb_in, 16)

            def z_lows(g, n):
                dve.wait_ge(z_high, g + 1)
                nc.vector.tensor_tensor(z_s[:, 1, :, 0:n], zT[:, :, bass.ds(g * GN, n)], z_s[:, 0, :, 0:n].bitcast(F32),
                                        ALU.subtract).then_inc(z_low, 1)

            def body(g, ns, next_ns, per):
                step = Chain(dve, ystep, g * PER, per)

                def pair(t, p):
                    return t[:, 2 * p:2 * p + 2, :]

                def row(t, r):
                    return t[0:SUB, r:r + 1, :].to_broadcast([SUB, 2, D])

                dve.wait_ge(x2_in, g * 16 + 16)
                dve.wait_ge(y_stored, PRE + g)
                for j in range(ns):
                    step.start(nc.vector.tensor_scalar(y[:, j, :], x2[:, j, :], z_mv[:, bass.ds(g * GS + j, 1), 0],
                                                       z_mv[:, bass.ds(g * GS + j, 1), 1], ALU.subtract, ALU.mult))
                step.wait()
                for j in range(ns):
                    step.start(nc.vector.tensor_tensor(y[:, j, :], y[:, j, :], zb2[0:SUB, :], ALU.add))
                step.wait()
                if next_ns:
                    z_lows(g + 1, next_ns * SUB)
                for j in range(ns):
                    dve.wait_ge(n_ready, PRE + g * GS + j + 1)
                    nc.vector.tensor_tensor(y[:, j, :], y[:, j, :], psN[0:SUB, j, 0:D], ALU.add).then_inc(n_saved, 1)
                for j in range(ns):
                    dve.wait_ge(n_saved, PRE + g * GS + j + 1)
                    step.start(nc.vector.bn_stats(st[:, j, :], y[:, j, :]))
                step.wait()
                dve.sem_inc(stats_taken, 1)
                for j in range(ns):
                    step.start(nc.vector.bn_aggr(mv[:, j, :], st[:, j, :]))
                step.wait()
                step(nc.vector.tensor_scalar(var[:, 0:ns], mv[:, 0:ns, 1], EPS, None, ALU.add))
                rsqrt_steps(nc, step, var[:, 0:ns], rstd[:, 0:ns], tmp[:, 0:ns])
                for j in range(ns):
                    step.start(nc.vector.tensor_scalar(y[:, j, :], y[:, j, :], mv[:, j, 0:1], rstd[:, j:j + 1],
                                                       ALU.subtract, ALU.mult))
                step.wait()
                for p in range(ns // 2):
                    step(nc.vector.tensor_tensor(pair(y, p), pair(y, p), row(gb, 0), ALU.mult))
                    step(nc.vector.tensor_tensor(pair(y, p), pair(y, p), row(gb, 1), ALU.add))
                    nc.vector.tensor_tensor(pair(y, p), pair(y, p), pair(x2, p), ALU.add).then_inc(y_ready, 1)
                step.end()

            z_lows(0, GN)
            with dve.Fori(0, GROUPS - 1) as g:
                body(g, GS, GS, PER)
            body(GROUPS - 1, GS, TAIL, PER)
            body(GROUPS, TAIL, 0, None)

        @block.tensor
        def _(pe):
            pe.sem_inc(f_ready, PRE)
            pe.sem_inc(n_ready, PRE)

            def body(g, ns):
                n = ns * SUB
                for turn in range(TILES + BEHIND):
                    if turn < TILES:
                        m = turn
                        pe.wait_ge(z_low, g + 1)
                        pe.wait_ge(f_saved, PRE + g * TILES + m + 1 - F)
                        for k in range(K2):
                            for wp, xp in PARTS:
                                last = nc.tensor.matmul(psF[:, m % F, 0:n], e1[:, wp, m // HM, k, (m % HM) * P:(m % HM + 1) * P],
                                                        z_s[:, xp, k, 0:n], start=(k == 0 and (wp, xp) == PARTS[0]),
                                                        stop=(k == K2 - 1 and (wp, xp) == PARTS[-1]))
                        last.then_inc(f_ready, 1)
                    if turn >= BEHIND:
                        m = turn - BEHIND
                        pe.wait_ge(f_saved, PRE + g * TILES + m + 1)
                        for j in range(ns):
                            if m == 0:
                                pe.wait_ge(n_saved, PRE + g * GS + j + 1 - GS)
                            last = nc.tensor.matmul(psN[0:SUB, j, 0:D], hg[:, m, j * SUB:(j + 1) * SUB], e2[:, m, :],
                                                    start=(m == 0), stop=(m == TILES - 1))
                            if m == TILES - 1:
                                last.then_inc(n_ready, 1)

            with pe.Fori(0, GROUPS) as g:
                body(g, GS)
            body(GROUPS, TAIL)


def kernel(**inputs):
    import numpy as _np
    import concourse.bacc as _bacc
    from concourse.bass_utils import run_bass_kernel_spmd as _run

    a = {name: _np.ascontiguousarray(value) for name, value in inputs.items()}

    def kxn(w):
        return _np.ascontiguousarray(w.reshape(-1, P, w.shape[-1]).transpose(1, 0, 2))

    def columns(*vectors):
        return _np.concatenate([v.reshape(-1, P).T for v in vectors], axis=1)

    def broadcast_rows(*vectors):
        return _np.ascontiguousarray(_np.broadcast_to(_np.stack(vectors)[None], (P, len(vectors), vectors[0].shape[0])))

    def edges(v, pad):
        full = _np.full(NCH * P, pad, v.dtype)
        full[:EDGES] = v
        return _np.ascontiguousarray(full.reshape(NCH, P).T)

    head = _np.arange(P) // 32
    w_ih = a["L0_gnn_W_ih"].reshape(4, DH, DH)
    gates = [0, 2, 3]
    arrays = {
        "x": a["x"],
        "src": edges(a["src"], 0), "dst": edges(a["dst"], PAD_DST),
        "mix_wkv": kxn(_np.concatenate([a["L0_mix_Wk"], a["L0_mix_Wv"]], axis=1)),
        "mix_bkv": broadcast_rows(_np.concatenate([a["L0_mix_bk"], a["L0_mix_bv"]])).reshape(P, 2 * D),
        "mix_wq": kxn(a["L0_mix_Wq"]), "mix_wo": kxn(a["L0_mix_Wo"]),
        "mix_w1": kxn(a["L0_mix_W1"]), "mix_w2": kxn(a["L0_mix_W2"]),
        "mix_cols": columns(a["L0_mix_bq"], a["L0_mix_ln1_g"], a["L0_mix_ln1_b"], a["L0_mix_b1"]),
        "mix_rows": broadcast_rows(a["L0_mix_bo"], a["L0_mix_ln1_g"], a["L0_mix_ln2_g"], a["L0_mix_ln1_b"],
                                   a["L0_mix_b2"], a["L0_mix_ln2_b"], a["L0_gnn_b_fc"]),
        "headm": (head[:, None] == head[None, :]).astype(_np.float32),
        "w_rel": kxn(a["L0_gnn_W_rel"]), "w_root": kxn(a["L0_gnn_W_root"]),
        "w_ih": kxn(_np.ascontiguousarray(_np.concatenate([w_ih[g] for g in gates]).T)),
        "w_fc": kxn(a["L0_gnn_W_fc"]),
        "gnn_cols": columns(a["L0_gnn_b_rel"], *[a[b].reshape(4, DH)[g] for b in ("L0_gnn_b_ih", "L0_gnn_b_hh") for g in gates]),
        "ffn_wr": kxn(a["L0_ffn_Wr"]), "ffn_br": a["L0_ffn_br"].reshape(1, NE),
        "ffn_w1": _np.ascontiguousarray(a["L0_ffn_W1"].reshape(NE, K2, P, DH).transpose(0, 2, 1, 3)).reshape(NE * P, K2 * DH),
        "ffn_w2": _np.ascontiguousarray(a["L0_ffn_W2"].reshape(NE, DH // P, P, D).transpose(0, 2, 1, 3)).reshape(NE * P, -1),
        "ffn_b1": _np.ascontiguousarray(a["L0_ffn_b1"].reshape(NE, DH // P, P).transpose(0, 2, 1)).reshape(NE * P, -1),
        "ffn_b2": _np.ascontiguousarray(_np.broadcast_to(a["L0_ffn_b2"][:, None, :], (NE, P, D))).reshape(NE * P, D),
        "ffn_gb": broadcast_rows(a["L0_ffn_gamma"], a["L0_ffn_beta"]),
    }
    nc = _bacc.Bacc("TRN2", target_bir_lowering=False, num_devices=1)
    arrays = {f"in_{name}": _np.ascontiguousarray(v) for name, v in arrays.items()}
    io = {name[3:]: nc.dram_tensor(name, v.shape, mybir.dt.from_np(v.dtype), kind="ExternalInput").ap()
          for name, v in arrays.items()}
    for name in ("xn_dram", "s1_dram", "x2_dram"):
        io[name] = nc.dram_tensor(name, (N, D), F32, kind="Internal").ap()
    io["table_dram"] = nc.dram_tensor("table_dram", (N, 2 * D), F16, kind="Internal").ap()
    io["root_dram"] = nc.dram_tensor("root_dram", (P, DH // P, N), F32, kind="Internal").ap()
    io["rest_dram"] = nc.dram_tensor("rest_dram", (P, NCH), F32, kind="Internal").ap()
    io["out"] = nc.dram_tensor("out", (N, D), F32, kind="ExternalOutput").ap()
    gps_layer(nc, io)
    r = _run(nc, [arrays], core_ids=[0])
    return r.results[0]["out"]
```
